# Optimizing a Trainium2 kernel written in Bass

```python
import numpy as np
import jax
import jax.numpy as jnp

def _softmax(x, axis=-1):
    return jax.nn.softmax(x, axis=axis)

def _gelu(x):
    return jax.nn.gelu(x, approximate=True)

def _silu(x):
    return jax.nn.silu(x)

def _sigmoid(x):
    return jax.nn.sigmoid(x)

def _layernorm(x, axis=-1, eps=1e-05):
    m = jnp.mean(x, axis=axis, keepdims=True)
    v = jnp.var(x, axis=axis, keepdims=True)
    return (x - m) / jnp.sqrt(v + eps)

def _scatter_add(tgt, idx, src, axis=0):
    return tgt.at[idx].add(src)

def _segment_sum(src, seg, n):
    return jax.ops.segment_sum(src, seg, n)
kernel_name = 'mk_prb_d1_jaxref_r8_5e9536'

def setup_inputs(seed: int=0):
    np.random.seed(seed)
    _w = jnp.asarray

    def _L0_attn_setup():
        import jax, jax.numpy as jnp
        import numpy as np
        H = 256
        NH = 16
        NOPE = 128
        ROPE = 64
        VD = 128
        QR = 128
        KVR = 64
        ROPE_BASE = 10000.0
        EPS = 1e-06

        def rmsnorm(x, scale):
            var = jnp.mean(jnp.square(x), axis=-1, keepdims=True)
            return x * jax.lax.rsqrt(var + EPS) * scale

        def rope_cos_sin(seq_len, dim, offset=0):
            half = dim // 2
            inv_freq = 1.0 / ROPE_BASE ** (jnp.arange(half, dtype=jnp.float32) * 2.0 / dim)
            pos = jnp.arange(offset, offset + seq_len, dtype=jnp.float32)
            ang = pos[:, None] * inv_freq[None, :]
            return (jnp.cos(ang), jnp.sin(ang))

        def apply_rope_single(x, cos, sin):
            x1 = x[..., ::2]
            x2 = x[..., 1::2]
            c = cos[None, None, :, :]
            s = sin[None, None, :, :]
            rotated = jnp.stack([x1 * c - x2 * s, x1 * s + x2 * c], axis=-1)
            return rotated.reshape(x.shape)
        key = jax.random.key(seed)
        ks = jax.random.split(key, 12)
        B, S = (2, 256)
        w = lambda k, shp: jax.random.normal(k, shp, dtype=jnp.float32) * 0.02
        return {'x': jax.random.normal(ks[0], (B, S, H), dtype=jnp.float32), 'W_cq': w(ks[1], (H, QR)), 'q_scale': jnp.ones((QR,), dtype=jnp.float32), 'W_dq_nope': w(ks[2], (QR, NH * NOPE)), 'W_dq_rope': w(ks[3], (QR, NH * ROPE)), 'W_ckv': w(ks[4], (H, KVR)), 'kv_scale': jnp.ones((KVR,), dtype=jnp.float32), 'W_dk_nope': w(ks[5], (KVR, NH * NOPE)), 'W_dv': w(ks[6], (KVR, NH * VD)), 'W_krope': w(ks[7], (H, ROPE)), 'W_o': w(ks[8], (NH * VD, H))}
    _L0_attn_in = _L0_attn_setup()

    def _L0_ffn_setup():
        import jax, jax.numpy as jnp
        import numpy as np
        HID = 256
        N_EXP = 32
        F_EXP = 96
        TOP_K = 6
        F_SH = 192
        B, S = (1, 128)
        key = jax.random.key(seed)
        ks = jax.random.split(key, 8)
        s = 0.02
        return {'hidden_states': jax.random.normal(ks[0], (B, S, HID), dtype=jnp.float32), 'gate_w': jax.random.normal(ks[1], (HID, N_EXP), dtype=jnp.float32) * s, 'wg': jax.random.normal(ks[2], (N_EXP, HID, F_EXP), dtype=jnp.float32) * s, 'wu': jax.random.normal(ks[3], (N_EXP, HID, F_EXP), dtype=jnp.float32) * s, 'wd': jax.random.normal(ks[4], (N_EXP, F_EXP, HID), dtype=jnp.float32) * s, 'sg': jax.random.normal(ks[5], (HID, F_SH), dtype=jnp.float32) * s, 'su': jax.random.normal(ks[6], (HID, F_SH), dtype=jnp.float32) * s, 'sd': jax.random.normal(ks[7], (F_SH, HID), dtype=jnp.float32) * s}
    _L0_ffn_in = _L0_ffn_setup()
    _d = {'L0_attn_x': _L0_attn_in['x'], 'L0_attn_W_cq': _L0_attn_in['W_cq'], 'L0_attn_q_scale': _L0_attn_in['q_scale'], 'L0_attn_W_dq_nope': _L0_attn_in['W_dq_nope'], 'L0_attn_W_dq_rope': _L0_attn_in['W_dq_rope'], 'L0_attn_W_ckv': _L0_attn_in['W_ckv'], 'L0_attn_kv_scale': _L0_attn_in['kv_scale'], 'L0_attn_W_dk_nope': _L0_attn_in['W_dk_nope'], 'L0_attn_W_dv': _L0_attn_in['W_dv'], 'L0_attn_W_krope': _L0_attn_in['W_krope'], 'L0_attn_W_o': _L0_attn_in['W_o'], 'L0_ffn_gate_w': _L0_ffn_in['gate_w'], 'L0_ffn_wg': _L0_ffn_in['wg'], 'L0_ffn_wu': _L0_ffn_in['wu'], 'L0_ffn_wd': _L0_ffn_in['wd'], 'L0_ffn_sg': _L0_ffn_in['sg'], 'L0_ffn_su': _L0_ffn_in['su'], 'L0_ffn_sd': _L0_ffn_in['sd']}
    _x0 = _d['L0_attn_x']
    _d['L0_attn_x'] = jax.random.normal(jax.random.fold_in(jax.random.key(seed), 1), (8, 512, 256), dtype=_x0.dtype)
    del _x0
    return _d

def reference(L0_attn_x, L0_attn_W_cq, L0_attn_q_scale, L0_attn_W_dq_nope, L0_attn_W_dq_rope, L0_attn_W_ckv, L0_attn_kv_scale, L0_attn_W_dk_nope, L0_attn_W_dv, L0_attn_W_krope, L0_attn_W_o, L0_ffn_gate_w, L0_ffn_wg, L0_ffn_wu, L0_ffn_wd, L0_ffn_sg, L0_ffn_su, L0_ffn_sd):

    def _L0_attn_ref(x, W_cq, q_scale, W_dq_nope, W_dq_rope, W_ckv, kv_scale, W_dk_nope, W_dv, W_krope, W_o):
        import jax, jax.numpy as jnp
        import numpy as np
        H = 256
        NH = 16
        NOPE = 128
        ROPE = 64
        VD = 128
        QR = 128
        KVR = 64
        ROPE_BASE = 10000.0
        EPS = 1e-06

        def rmsnorm(x, scale):
            var = jnp.mean(jnp.square(x), axis=-1, keepdims=True)
            return x * jax.lax.rsqrt(var + EPS) * scale

        def rope_cos_sin(seq_len, dim, offset=0):
            half = dim // 2
            inv_freq = 1.0 / ROPE_BASE ** (jnp.arange(half, dtype=jnp.float32) * 2.0 / dim)
            pos = jnp.arange(offset, offset + seq_len, dtype=jnp.float32)
            ang = pos[:, None] * inv_freq[None, :]
            return (jnp.cos(ang), jnp.sin(ang))

        def apply_rope_single(x, cos, sin):
            x1 = x[..., ::2]
            x2 = x[..., 1::2]
            c = cos[None, None, :, :]
            s = sin[None, None, :, :]
            rotated = jnp.stack([x1 * c - x2 * s, x1 * s + x2 * c], axis=-1)
            return rotated.reshape(x.shape)
        B, S, _ = x.shape
        norm_q = rmsnorm(x @ W_cq, q_scale)
        q_nope = (norm_q @ W_dq_nope).reshape(B, S, NH, NOPE)
        q_rope = (norm_q @ W_dq_rope).reshape(B, S, NH, ROPE)
        norm_kv = rmsnorm(x @ W_ckv, kv_scale)
        k_nope = (norm_kv @ W_dk_nope).reshape(B, S, NH, NOPE)
        value = (norm_kv @ W_dv).reshape(B, S, NH, VD)
        k_rope = (x @ W_krope).reshape(B, S, 1, ROPE)
        q_nope = q_nope.transpose(0, 2, 1, 3)
        q_rope = q_rope.transpose(0, 2, 1, 3)
        k_nope = k_nope.transpose(0, 2, 1, 3)
        k_rope = k_rope.transpose(0, 2, 1, 3)
        value = value.transpose(0, 2, 1, 3)
        cos, sin = rope_cos_sin(S, ROPE, offset=0)
        q_rope = apply_rope_single(q_rope, cos, sin)
        k_rope = apply_rope_single(k_rope, cos, sin) / NH
        full_head_dim = NOPE + ROPE
        query = jnp.concatenate([q_nope, q_rope], axis=-1)
        key = jnp.concatenate([k_nope, jnp.broadcast_to(k_rope, k_nope.shape[:-1] + (ROPE,))], axis=-1)
        scale = 1.0 / jnp.sqrt(jnp.asarray(full_head_dim, dtype=x.dtype))
        scores = jnp.einsum('bhqd,bhkd->bhqk', query, key) * scale
        causal = jnp.tril(jnp.ones((S, S), dtype=jnp.bool_))
        scores = jnp.where(causal[None, None, :, :], scores, -1000000000.0)
        attn = jax.nn.softmax(scores, axis=-1)
        out = jnp.einsum('bhqk,bhkd->bhqd', attn, value)
        out = out.transpose(0, 2, 1, 3).reshape(B, S, NH * VD)
        return out @ W_o

    def _L0_ffn_ref(hidden_states, gate_w, wg, wu, wd, sg, su, sd):
        import jax, jax.numpy as jnp
        import numpy as np
        HID = 256
        N_EXP = 32
        F_EXP = 96
        TOP_K = 6
        F_SH = 192
        B, S = (1, 128)
        orig_shape = hidden_states.shape
        x = hidden_states.reshape(-1, HID)
        scores = jax.nn.sigmoid(x @ gate_w)
        topk_w, topk_i = jax.lax.top_k(scores, TOP_K)
        topk_w = topk_w / (jnp.sum(topk_w, axis=-1, keepdims=True) + 1e-20)
        combine = jnp.sum(jax.nn.one_hot(topk_i, N_EXP, dtype=topk_w.dtype) * topk_w[..., None], axis=1)
        g = jnp.einsum('td,edf->tef', x, wg)
        u = jnp.einsum('td,edf->tef', x, wu)
        act = jax.nn.silu(g) * u
        routed = jnp.einsum('tef,efd,te->td', act, wd, combine)
        routed = routed.reshape(orig_shape)
        shared = jax.nn.silu(hidden_states @ sg) * (hidden_states @ su) @ sd
        return routed + shared
    x = L0_attn_x
    xn = _layernorm(x, axis=-1)
    x = x + _L0_attn_ref(xn, L0_attn_W_cq, L0_attn_q_scale, L0_attn_W_dq_nope, L0_attn_W_dq_rope, L0_attn_W_ckv, L0_attn_kv_scale, L0_attn_W_dk_nope, L0_attn_W_dv, L0_attn_W_krope, L0_attn_W_o) + _L0_ffn_ref(xn, L0_ffn_gate_w, L0_ffn_wg, L0_ffn_wu, L0_ffn_wd, L0_ffn_sg, L0_ffn_su, L0_ffn_sd)
    return x

_drawn_inputs = setup_inputs


def setup_inputs(seed=0):
    import zlib

    import numpy as np

    out = dict(_drawn_inputs(seed))
    spreads = {'L0_attn_q_scale': (1.0, 0.6), 'L0_attn_kv_scale': (1.0, 0.6)}
    factors = {'L0_attn_W_cq': 8.0,
     'L0_attn_W_dq_nope': 8.0,
     'L0_attn_W_dq_rope': 8.0,
     'L0_attn_W_ckv': 3.257,
     'L0_attn_W_dk_nope': 8.0,
     'L0_attn_W_dv': 3.246,
     'L0_attn_W_krope': 8.0,
     'L0_attn_W_o': 3.366,
     'L0_ffn_gate_w': 8.0,
     'L0_ffn_wg': 8.0,
     'L0_ffn_wu': 8.0,
     'L0_ffn_wd': 8.0,
     'L0_ffn_sg': 3.926,
     'L0_ffn_su': 3.863,
     'L0_ffn_sd': 3.862}
    for name, (base, spread) in spreads.items():
        noise = np.random.default_rng([zlib.crc32(name.encode()), seed]).standard_normal(out[name].shape)
        drawn = base * np.exp(spread * noise) if base else spread * noise
        out[name] = jnp.asarray(drawn.astype(out[name].dtype))
    for name, factor in factors.items():
        out[name] = (out[name] * factor).astype(out[name].dtype)
    return out
```

```python
from contextlib import ExitStack

import concourse.bass as bass
from concourse import mybir

F32 = mybir.dt.float32
F32R = mybir.dt.float32r
BF16 = mybir.dt.bfloat16
ALU = mybir.AluOpType
ACT = mybir.ActivationFunctionType
AX = mybir.AxisListType

P = 128
B, S, H = 8, 512, 256
TT = S // P
KC = H // P
NH, NOPE, ROPE, VD = 16, 128, 64, 128
HALF = ROPE // 2
QR, KVR = 128, 64
NP_ = NH // 2
NE, FE, FSH, TOPK = 32, 96, 192, 6
EG = 4
NG = NE // EG
FG = EG * FE
FC = FG // P
FALL = NE * FE + FSH
NCOMB = NE + FSH // FE
CW = QR + KVR + ROPE + NE
CKV, CKR, CG = QR, QR + KVR, QR + KVR + ROPE
SCALE = float((NOPE + ROPE) ** -0.5)
LN_EPS, RMS_EPS = 1e-5, 1e-6
MASKED = -1e30
PT_AT = [0, 512, 1024, 896]
PT_W = 1280


def split(dve, act, hi, lo, src, hi_sem, hi_value, lo_sem, hi_inc=1):
    if act is not None:
        act.activation(hi, src, ACT.Copy).then_inc(hi_sem, hi_inc)
    if dve is not None:
        dve.wait_ge(hi_sem, hi_value)
        dve.tensor_tensor(lo, src, hi.bitcast(F32), ALU.subtract).then_inc(lo_sem, 1)


def product3(pe, out, lhs, rhs, first, last, **kw):
    (lh, ll), (rh, rl) = lhs, rhs
    pe.matmul(out, lh, rh, start=first, stop=False, **kw)
    pe.matmul(out, lh, rl, start=False, stop=False, **kw)
    return pe.matmul(out, ll, rh, start=False, stop=last, **kw)


def build(nc, x, wc, wqr, nopeT, dkT, dvT, wo, qscale, kvscale, rope, wg, wu, wd, out):
    with ExitStack() as top:
        def sem(name):
            return top.enter_context(nc.semaphore(name))

        xnt_dram = nc.dram_tensor("xnt_dram", (B, P, 2, KC, S), F32, kind="Internal").ap()
        res_dram = nc.dram_tensor("res_dram", (B, P, TT, H), F32, kind="Internal").ap()
        comb = top.enter_context(nc.sbuf_tensor("comb", [P, B, TT, NCOMB], F32))
        ident = top.enter_context(nc.sbuf_tensor("ident", [P, P], F32))
        ps = top.enter_context(nc.psum_tensor("ps", [P, 8, 512], F32))
        with ExitStack() as ctx:
            attention(nc, ctx, sem, x, wc, wqr, nopeT, dkT, dvT, wo, qscale, kvscale, rope,
                      xnt_dram, res_dram, comb, ident, ps)
        with ExitStack() as ctx:
            experts(nc, ctx, sem, wg, wu, wd, xnt_dram, res_dram, comb, ident, ps, out)


def attention(nc, ctx, sem, x, wc, wqr, nopeT, dkT, dvT, wo, qscale, kvscale, rope,
              xnt_dram, res_dram, comb, ident, ps):
    def sb(name, shape, dt=F32):
        return ctx.enter_context(nc.sbuf_tensor(name, shape, dt))

    wc_s = [sb("wc_hi", [P, KC, CW], F32R), sb("wc_lo", [P, KC, CW], F32R)]
    wq_s = [sb("wq_hi", [P, NH, P], F32R), sb("wq_lo", [P, NH, P], F32R)]
    wvo_s = [sb("wvo_hi", [P, NP_, H], F32R), sb("wvo_lo", [P, NP_, H], F32R)]
    kvs_bc = sb("kvs_bc", [P, KVR])
    rope_sb = sb("rope_sb", [P, 2, TT, 2, ROPE])
    minus_half = sb("minus_half", [P, 2 * TT])
    ident_bf = sb("ident_bf", [P, P], BF16)
    mask_bf = sb("mask_bf", [P, P], BF16)

    consts_ready = sem("consts_ready")
    loaded = sem("weights_loaded")
    absorbed = sem("absorbed")
    prep_dve = sem("prep_dve")
    prep_hi = sem("prep_hi")
    prep_lo = sem("prep_lo")

    with ExitStack() as pctx:
        def tb(name, shape, dt=F32):
            return pctx.enter_context(nc.sbuf_tensor(name, shape, dt))

        wc_raw = tb("wc_raw", [P, KC, CW])
        wqr_raw = tb("wqr_raw", [P, NH, ROPE])
        nope_raw = tb("nope_raw", [P, NH, QR])
        dk_raw = tb("dk_raw", [P, NH, KVR])
        dv_raw = tb("dv_raw", [P, NH, KVR])
        wo_raw = tb("wo_raw", [P, NH, H])
        qs = tb("qs", [P, 1])
        wq_f = tb("wq_f", [P, NH, P])
        absorbed_ps = ps[:, 0:2, :].rearrange("p b (h r) -> p (b h) r", r=KVR)
        wvo_ps = ps[:, 2:6, :].rearrange("p b (h n) -> p (b h) n", n=H)

        with nc.Block() as block:
            @block.sync
            def _(sp):
                for dst, src in ((nope_raw, nopeT), (dk_raw, dkT), (wqr_raw, wqr), (dv_raw, dvT),
                                 (wo_raw, wo), (wc_raw, wc), (rope_sb, rope)):
                    sp.dma_start(dst[:], src).then_inc(loaded, 16)
                sp.dma_start(qs[:], qscale.rearrange("(p a) -> p a", a=1)).then_inc(loaded, 16)
                sp.dma_start(kvs_bc[:], kvscale.rearrange("(a r) -> a r", a=1).to_broadcast([P, KVR]))\
                  .then_inc(loaded, 16)
                sp.wait_ge(loaded, 9 * 16)

            @block.gpsimd
            def _(pool):
                pool.memset(ident[:], 0.0).then_inc(consts_ready, 1)
                pool.memset(ident_bf[:], 0.0).then_inc(consts_ready, 1)
                pool.memset(mask_bf[:], 0.0).then_inc(consts_ready, 1)
                pool.memset(minus_half[:], -0.5).then_inc(consts_ready, 1)
                pool.wait_ge(consts_ready, 4)
                for m in (ident, ident_bf):
                    pool.affine_select(out=m[:], in_=m[:], compare_op=ALU.not_equal, fill=1.0, base=0,
                                       pattern=[[-1, P]], channel_multiplier=1).then_inc(consts_ready, 1)
                pool.affine_select(out=mask_bf[:], in_=mask_bf[:], compare_op=ALU.is_ge, fill=MASKED, base=0,
                                   pattern=[[-1, P]], channel_multiplier=1).then_inc(consts_ready, 1)

            @block.tensor
            def _(pe):
                pe.wait_ge(loaded, 9 * 16)
                for h in range(NH):
                    mm = pe.matmul(absorbed_ps[:, h, :], nope_raw[:, h, :], dk_raw[:, h, :], start=True, stop=True)
                mm.then_inc(absorbed, 1)
                for h in range(NH):
                    at = (h % 2) * KVR
                    mm = pe.matmul(wvo_ps[at:at + KVR, h // 2, :], dv_raw[:, h, :], wo_raw[:, h, :],
                                   start=True, stop=True)
                mm.then_inc(absorbed, 1)

            @block.scalar
            def _(act):
                act.wait_ge(loaded, 9 * 16)
                split(None, act, wc_s[0][:], None, wc_raw[:], prep_hi, 0, None)
                act.wait_ge(prep_dve, 2)
                split(None, act, wq_s[0][:], None, wq_f[:], prep_hi, 0, None)
                act.wait_ge(absorbed, 2)
                split(None, act, wvo_s[0][:], None, wvo_ps, prep_hi, 0, None)

            @block.vector
            def _(dve):
                dve.wait_ge(loaded, 9 * 16)
                dve.tensor_scalar(wq_f[:, :, KVR:P], wqr_raw[:], qs[:, 0:1], SCALE, ALU.mult, ALU.mult)\
                   .then_inc(prep_dve, 1)
                dve.memset(comb[:, :, :, NE:NCOMB], 1.0)
                dve.wait_ge(absorbed, 1)
                dve.tensor_scalar(wq_f[:, :, 0:KVR], absorbed_ps, qs[:, 0:1], SCALE, ALU.mult, ALU.mult)\
                   .then_inc(prep_dve, 1)
                dve.wait_ge(prep_dve, 2)
                split(dve, None, wc_s[0][:], wc_s[1][:], wc_raw[:], prep_hi, 1, prep_lo)
                split(dve, None, wq_s[0][:], wq_s[1][:], wq_f[:], prep_hi, 2, prep_lo)
                dve.wait_ge(absorbed, 2)
                split(dve, None, wvo_s[0][:], wvo_s[1][:], wvo_ps, prep_hi, 3, prep_lo)

    x_in = sb("x_in", [P, TT, H])
    x_res = sb("x_res", [P, TT, H])
    res = sb("res", [P, TT, H])
    spare = sb("spare", [P, 3])
    stats = sb("stats", [P, TT, 6])
    mv = sb("mv", [P, TT, 2])
    var = sb("var", [P, TT])
    rstd = sb("rstd", [P, TT])
    xn = sb("xn", [P, TT, H])
    xnt = [sb("xnt_hi", [P, KC, S], F32R), sb("xnt_lo", [P, KC, S], F32R)]
    junk = sb("junk", [P, TT, QR + KVR])
    sumsq = sb("sumsq", [P, 2, TT])
    meansq = sb("meansq", [P, 2, TT])
    rms = sb("rms", [P, 2, TT])
    nq = sb("nq", [P, TT, QR])
    tkv = sb("tkv", [P, TT, KVR])
    kp = sb("kp", [P, TT, P])
    ka = sb("ka", [P, TT, ROPE])
    kb = sb("kb", [P, TT, ROPE])
    nkv = sb("nkv", [P, TT, 2 * KVR], F32R)
    nqt = [sb("nqt_hi", [P, S], F32R), sb("nqt_lo", [P, S], F32R)]
    kt_s = [sb("kt_hi", [P, S], F32R), sb("kt_lo", [P, S], F32R)]
    expg = sb("expg", [P, TT, NE])
    gate = sb("gate", [P, TT, NE])
    score = sb("score", [P, TT, NE + 2])
    top8 = sb("top8", [P, TT, 8])
    picked = sb("picked", [P, TT, NE + 2])
    chosen = sb("chosen", [P, TT, NE])
    wsum = sb("wsum", [P, TT])
    winv = sb("winv", [P, TT])
    qp = sb("qp", [P, TT, 2, P])
    qa = sb("qa", [P, TT, 2, ROPE])
    qb = sb("qb", [P, TT, 2, ROPE])
    qt_s = [[sb(f"qt_hi{i}", [P, S], F32R), sb(f"qt_lo{i}", [P, S], F32R)] for i in range(2)]
    negmax = sb("negmax", [P, 2, TT])
    rowsum = sb("rowsum", [P, 2, TT])
    rinv = sb("rinv", [P, 2, TT])
    prob = sb("prob", [P, 2, TT, S])
    pt_s = [[sb(f"pt_hi{i}", [P, PT_W], F32R), sb(f"pt_lo{i}", [P, PT_W], F32R)] for i in range(2)]
    o_low = sb("o_low", [KVR, S])
    lat = sb("lat", [P, NP_, S])
    lat_s = [sb("lat_hi", [P, NP_, S], F32R), sb("lat_lo", [P, NP_, S], F32R)]

    xt_ps = ps[:, 0:2, :]
    c_ps = ps[:, 2:6, 0:CW]
    nqt_ps, kt_ps = ps[:, 6, :], ps[:, 7, :]
    q_ps = ps[:, 0:2, :].rearrange("p b (t h c) -> p (b t) h c", t=2, h=2)
    qt_ps = [ps[:, 0, :], ps[:, 1, :]]
    s_ps = [ps[:, 2, :], ps[:, 3, :]]
    pt_ps = ps[:, 4:7, :].rearrange("p b n -> p (b n)")
    o_ps = ps[:, 7, :]
    acc_ps = ps[:, 0:2, :].rearrange("p b (t n) -> p (b t) n", t=2)

    x_loaded, xres_loaded = sem("x_loaded"), sem("xres_loaded")
    var_ready, rstd_ready = sem("var_ready"), sem("rstd_ready")
    dve_chain = sem("dve_chain")
    xn_ready = sem("xn_ready")
    xt_ready, xt_hi, xt_lo, xt_stored = sem("xt_ready"), sem("xt_hi"), sem("xt_lo"), sem("xt_stored")
    c_ready, squared, logits_exp = sem("c_ready"), sem("squared"), sem("logits_exp")
    meansq_ready, rms_ready = sem("meansq_ready"), sem("rms_ready")
    nq_ready, kp_ready, nkv_ready = sem("nq_ready"), sem("kp_ready"), sem("nkv_ready")
    nk_ready, nk_hi, nk_lo = sem("nk_ready"), sem("nk_hi"), sem("nk_lo")
    q_ready, q_abs, q_rope, q_done = sem("q_ready"), sem("q_abs"), sem("q_rope"), sem("q_done")
    qt_ready, qt_hi, qt_lo = sem("qt_ready"), sem("qt_hi"), sem("qt_lo")
    s_ready, max_ready, exp_done, rinv_ready = sem("s_ready"), sem("max_ready"), sem("exp_done"), sem("rinv_ready")
    norm_dve, norm_pool = sem("norm_dve"), sem("norm_pool")
    pt_ready, pt_hi, pt_lo = sem("pt_ready"), sem("pt_hi"), sem("pt_lo")
    pv_ready, o_copied, lat_added = sem("pv_ready"), sem("o_copied"), sem("lat_added")
    lat_hi, lat_lo = sem("lat_hi"), sem("lat_lo")
    acc_ready, res_added, res_stored = sem("acc_ready"), sem("res_added"), sem("res_stored")

    x_t = x.rearrange("b (t p) h -> b p t h", p=P)
    DVE_CHAIN = 12

    def pairs(eng, step, tail):
        for g in range(4):
            step(g // 2, g % 2)
        with eng.Fori(2, NP_ - 1) as p:
            for par in range(2):
                step(p, par)
        for g in range(2 * (NP_ - 1), tail):
            step(g // 2, g % 2)

    def has(p, par, lag):
        if not isinstance(p, int):
            return True
        return 0 <= 2 * p + par - lag < NH

    with nc.Block() as block:
        @block.sync
        def _(sp):
            with sp.Fori(0, B) as b:
                sp.wait_ge(xn_ready, TT * b + TT)
                sp.dma_start(x_in[:], x_t[b]).then_inc(x_loaded, 16)
                sp.wait_ge(res_added, 2 * b + 2)
                sp.dma_start(x_res[:], x_t[b]).then_inc(xres_loaded, 16)
                for i, done in ((0, xt_hi), (1, xt_lo)):
                    sp.wait_ge(done, KC * b + KC)
                    sp.dma_start(xnt_dram[b][:, i], xnt[i][:].bitcast(F32)).then_inc(xt_stored, 16)
                sp.wait_ge(res_added, 2 * b + 4)
                sp.dma_start(res_dram[b], res[:]).then_inc(res_stored, 16)
            sp.wait_ge(xt_stored, 32 * B + 32)
            sp.wait_ge(res_stored, 16 * B + 16)

        @block.gpsimd
        def _(pool):
            with pool.Fori(0, B) as b:
                pool.wait_ge(var_ready, b + 1)
                pool.tensor_tensor(rstd[:], var[:], minus_half[:, 0:TT], ALU.pow).then_inc(rstd_ready, 1)
                pool.wait_ge(meansq_ready, 2 * b + 2)
                pool.tensor_tensor(rms[:].rearrange("p k t -> p (k t)"), meansq[:].rearrange("p k t -> p (k t)"),
                                   minus_half[:], ALU.pow).then_inc(rms_ready, 1)

                def rope_add(p):
                    pool.wait_ge(q_rope, NP_ * b + p + 1)
                    pool.tensor_tensor(qp[:, :, :, KVR:P], qa[:], qb[:], ALU.add).then_inc(q_done, 1)

                def norm(p, par, qt):
                    g = 2 * p + par
                    w = (qt + 1) * P
                    i = par % 2
                    pool.wait_ge(rinv_ready, 64 * b + 4 * g + qt + 1)
                    pool.tensor_tensor(prob[:, i, qt, 0:w], prob[:, i, qt, 0:w],
                                       rinv[:, i, qt:qt + 1].to_broadcast([P, w]), ALU.mult).then_inc(norm_pool, 1)

                def step(p, par):
                    if has(p, par, 1):
                        pp, pr = (p, 0) if par else (p - 1, 1)
                        norm(pp, pr, 3)
                    if par == 0 and not (isinstance(p, int) and p + 1 >= NP_):
                        rope_add(p + 1)
                    if has(p, par, 0):
                        norm(p, par, 2)
                    if par == 1 and has(p, 0, 4):
                        q = p - 2
                        pool.wait_ge(lat_hi, NP_ * b + q + 1)
                        pool.tensor_tensor(lat_s[1][:, q, :], lat[:, q, :], lat_s[0][:, q, :].bitcast(F32),
                                           ALU.subtract).then_inc(lat_lo, 1)

                rope_add(0)
                pairs(pool, step, NH + 4)

        @block.tensor
        def _(pe):
            pe.wait_ge(consts_ready, 7)
            with pe.Fori(0, B) as b:
                pe.wait_ge(res_added, 2 * b + 2)
                pe.wait_ge(xn_ready, TT * b + 2 * TT)
                for kc in range(KC):
                    for t in range(TT):
                        mm = pe.transpose(xt_ps[:, kc, t * P:(t + 1) * P], xn[:, t, kc * P:(kc + 1) * P], ident[:])
                    mm.then_inc(xt_ready, 1)
                pe.wait_ge(xt_lo, KC * b + KC)
                for t in range(TT):
                    for kc in range(KC):
                        mm = product3(pe, c_ps[:, t, :], [a[:, kc, t * P:(t + 1) * P] for a in xnt],
                                      [w[:, kc, :] for w in wc_s], kc == 0, kc == KC - 1)
                    mm.then_inc(c_ready, 1)
                pe.wait_ge(nq_ready, b + 1)
                for t in range(TT):
                    mm = pe.transpose(nqt_ps[:, t * P:(t + 1) * P], nq[:, t, :], ident[:])
                mm.then_inc(nk_ready, 1)
                pe.wait_ge(kp_ready, b + 1)
                for t in range(TT):
                    mm = pe.transpose(kt_ps[:, t * P:(t + 1) * P], kp[:, t, :], ident[:])
                mm.then_inc(nk_ready, 1)

                def queries(p):
                    if isinstance(p, int) and p == 0:
                        pe.wait_ge(nk_lo, 2 * b + 1)
                    else:
                        pe.wait_ge(qt_lo, 2 * NP_ * b + 2 * p)
                    for t in range(TT):
                        mm = product3(pe, q_ps[:, t], [a[:, t * P:(t + 1) * P] for a in nqt],
                                      [w[:, bass.ds(2 * p, 2), :] for w in wq_s], t % 2 == 0, t % 2 == 1,
                                      skip_group_check=True)
                    mm.then_inc(q_ready, 1)

                def queries_turn(p):
                    pe.wait_ge(q_abs, NP_ * b + p + 1)
                    pe.wait_ge(q_done, NP_ * b + p + 1)
                    for i in range(2):
                        for t in range(TT):
                            mm = pe.transpose(qt_ps[i][:, t * P:(t + 1) * P], qp[:, t, i, :], ident[:])
                    mm.then_inc(qt_ready, 1)

                def scores(p, par, qt):
                    u = 8 * p + 4 * par + qt
                    if qt == 0:
                        pe.wait_ge(qt_lo, 2 * NP_ * b + 2 * p + par + 1)
                    if not (isinstance(p, int) and u < 2):
                        pe.wait_ge(exp_done, 64 * b + u - 1)
                    w = (qt + 1) * P
                    s = s_ps[qt % 2]
                    product3(pe, s[:, 0:w], [a[:, qt * P:w] for a in qt_s[par]], [a[:, 0:w] for a in kt_s], True, False)
                    pe.matmul(s[:, qt * P:w], ident_bf[:], mask_bf[:], start=False, stop=True).then_inc(s_ready, 1)

                def turn(p, par):
                    g = 2 * p + par
                    if not (isinstance(p, int) and g == 0):
                        pe.wait_ge(pt_lo, 2 * NH * b + 2 * g)
                    for qt in range(TT):
                        if qt < 2:
                            pe.wait_ge(norm_dve, 2 * NH * b + 2 * g + qt + 1)
                        else:
                            pe.wait_ge(norm_pool, 2 * NH * b + 2 * g + qt - 1)
                        for kt in range(qt + 1):
                            at = PT_AT[kt] + (qt - kt) * P
                            mm = pe.transpose(pt_ps[:, at:at + P], prob[:, par, qt, kt * P:(kt + 1) * P], ident[:])
                    mm.then_inc(pt_ready, 1)

                def values(p, par):
                    g = 2 * p + par
                    pe.wait_ge(pt_lo, 2 * NH * b + 2 * g + 2)
                    if not (isinstance(p, int) and g == 0):
                        pe.wait_ge(lat_added, NH * b + g)
                    for kt in range(TT):
                        w = S - kt * P
                        for i in range(2):
                            mm = pe.matmul(o_ps[:, kt * P:S], nkv[:, kt, :], pt_s[par][i][:, PT_AT[kt]:PT_AT[kt] + w],
                                           start=(kt == 0 and i == 0), stop=(kt == TT - 1 and i == 1))
                    mm.then_inc(pv_ready, 1)

                def step(p, par):
                    if has(p, par, 0):
                        scores(p, par, 0)
                        scores(p, par, 1)
                        if par == 0 and not (isinstance(p, int) and p + 1 >= NP_):
                            queries(p + 1)
                        scores(p, par, 2)
                        scores(p, par, 3)
                        if par == 1 and not (isinstance(p, int) and p + 1 >= NP_):
                            queries_turn(p + 1)
                    if has(p, par, 1):
                        turn(*((p, 0) if par else (p - 1, 1)))
                    if has(p, par, 2):
                        values(p - 1, par)

                queries(0)
                queries_turn(0)
                pe.wait_ge(nk_lo, 2 * b + 2)
                pe.wait_ge(logits_exp, b + 1)
                pe.wait_ge(nkv_ready, b + 1)
                pairs(pe, step, NH + 2)

                for q in range(NP_):
                    pe.wait_ge(lat_lo, NP_ * b + q + 1)
                    for t in range(TT):
                        mm = product3(pe, acc_ps[:, t, :], [a[:, q, t * P:(t + 1) * P] for a in lat_s],
                                      [w[:, q, :] for w in wvo_s], q == 0 and t % 2 == 0, q == NP_ - 1 and t % 2 == 1,
                                      skip_group_check=True)
                        if q == NP_ - 1 and t % 2 == 1:
                            mm.then_inc(acc_ready, 1)

        @block.scalar
        def _(act):
            with act.Fori(0, B) as b:
                act.wait_ge(xt_stored, 32 * b + 32)
                for kc in range(KC):
                    act.wait_ge(xt_ready, KC * b + kc + 1)
                    act.activation(xnt[0][:, kc, :], xt_ps[:, kc, :], ACT.Copy).then_inc(xt_hi, 1)
                for t in range(TT):
                    act.wait_ge(c_ready, TT * b + t + 1)
                    for k, (at, w) in enumerate(((0, QR), (CKV, KVR))):
                        act.activation(junk[:, t, at:at + w], c_ps[:, t, at:at + w], ACT.Square,
                                       accum_out=sumsq[:, k, t:t + 1]).then_inc(squared, 1)
                act.activation(expg[:], c_ps[:, :, CG:CW], ACT.Exp, scale=-1.0).then_inc(logits_exp, 1)
                for i, (dst, src) in enumerate(((nqt[0], nqt_ps), (kt_s[0], kt_ps))):
                    act.wait_ge(nk_ready, 2 * b + i + 1)
                    act.activation(dst[:], src, ACT.Copy).then_inc(nk_hi, 1)

                def queries_latent(p):
                    act.wait_ge(q_ready, NP_ * b + p + 1)
                    act.activation(qp[:, :, :, 0:KVR], q_ps[:, :, :, 0:KVR], ACT.Copy).then_inc(q_abs, 1)

                def queries_hi(p):
                    act.wait_ge(qt_ready, NP_ * b + p + 1)
                    for i in range(2):
                        act.activation(qt_s[i][0][:], qt_ps[i], ACT.Copy).then_inc(qt_hi, 1)

                def exps(p, par, qt):
                    w = (qt + 1) * P
                    act.wait_ge(max_ready, 64 * b + 8 * p + 4 * par + qt + 1)
                    act.activation(prob[:, par, qt, 0:w], s_ps[qt % 2][:, 0:w], ACT.Exp,
                                   bias=negmax[:, par, qt:qt + 1],
                                   accum_out=rowsum[:, par, qt:qt + 1]).then_inc(exp_done, 1)

                def turned_hi(p, par, i):
                    lo, hi = ((0, 512), (512, PT_W))[i]
                    act.wait_ge(pt_ready, NH * b + 2 * p + par + 1)
                    act.activation(pt_s[par][0][:, lo:hi], pt_ps[:, lo:hi], ACT.Copy).then_inc(pt_hi, 1)

                def step(p, par):
                    if has(p, par, 2):
                        turned_hi(p - 1, par, 0)
                    if has(p, par, 0):
                        exps(p, par, 0)
                    if has(p, par, 2):
                        turned_hi(p - 1, par, 1)
                    if has(p, par, 0):
                        exps(p, par, 1)
                    if has(p, par, 3):
                        pp, pr = (p - 1, 0) if par else (p - 2, 1)
                        act.wait_ge(pv_ready, NH * b + 2 * pp + pr + 1)
                        act.activation(o_low[:], o_ps[KVR:P, :], ACT.Copy).then_inc(o_copied, 1)
                    if par == 0 and not (isinstance(p, int) and p + 1 >= NP_):
                        queries_latent(p + 1)
                    if has(p, par, 0):
                        exps(p, par, 2)
                        exps(p, par, 3)
                    if par == 1 and not (isinstance(p, int) and p + 1 >= NP_):
                        queries_hi(p + 1)
                    if par == 0 and has(p, 0, 4):
                        q = p - 2
                        act.wait_ge(lat_added, NH * b + 2 * q + 2)
                        act.activation(lat_s[0][:, q, :], lat[:, q, :], ACT.Copy).then_inc(lat_hi, 1)

                queries_latent(0)
                queries_hi(0)
                pairs(act, step, NH + 4)

        @block.vector
        def _(dve):
            dve.memset(score[:, :, NE:NE + 2], -1.0).then_inc(dve_chain, 1)
            dve.memset(rinv[:], 0.0).then_inc(xn_ready, TT)
            dve.memset(rowsum[:], 0.0).then_inc(res_added, 2)
            dve.memset(negmax[:], 0.0).then_inc(xt_stored, 32)
            dve.memset(wsum[:], 0.0).then_inc(res_stored, 16)
            dve.wait_ge(dve_chain, 1)
            with dve.Fori(0, B) as b:
                steps = [0]

                def chain(ins):
                    steps[0] += 1
                    ins.then_inc(dve_chain, 1)

                def chained():
                    dve.wait_ge(dve_chain, 1 + DVE_CHAIN * b + steps[0])

                def carry_wait(i):
                    dve.memset(spare[:, i:i + 1], 0.0)

                dve.wait_ge(x_loaded, 16 * b + 16)
                for t in range(TT):
                    ins = dve.bn_stats(stats[:, t, :], x_in[:, t, :])
                chain(ins)
                chained()
                carry_wait(0)
                for t in range(TT):
                    ins = dve.bn_aggr(mv[:, t, :], stats[:, t, :])
                chain(ins)
                chained()
                dve.tensor_scalar(var[:], mv[:, :, 1], LN_EPS, None, ALU.add).then_inc(var_ready, 1)
                dve.wait_ge(rstd_ready, b + 1)
                for t in range(TT):
                    ins = dve.tensor_scalar(xn[:, t, :], x_in[:, t, :], mv[:, t, 0:1], rstd[:, t:t + 1],
                                            ALU.subtract, ALU.mult)
                    ins.then_inc(xn_ready, 1)
                for kc in range(KC):
                    dve.wait_ge(xt_hi, KC * b + kc + 1)
                    dve.tensor_tensor(xnt[1][:, kc, :], xt_ps[:, kc, :], xnt[0][:, kc, :].bitcast(F32), ALU.subtract)\
                       .then_inc(xt_lo, 1)
                dve.wait_ge(squared, 2 * TT * b + 2 * TT)
                for k, n in enumerate((QR, KVR)):
                    dve.tensor_scalar(meansq[:, k, :], sumsq[:, k, :], 1.0 / n, RMS_EPS, ALU.mult, ALU.add)\
                       .then_inc(meansq_ready, 1)
                dve.wait_ge(rms_ready, b + 1)
                dve.wait_ge(logits_exp, b + 1)
                dve.tensor_tensor(nq[:], c_ps[:, :, 0:QR], rms[:, 0, :].unsqueeze(2).to_broadcast([P, TT, QR]),
                                  ALU.mult).then_inc(nq_ready, 1)
                dve.tensor_tensor(tkv[:], c_ps[:, :, CKV:CKR], rms[:, 1, :].unsqueeze(2).to_broadcast([P, TT, KVR]),
                                  ALU.mult)
                dve.tensor_tensor(ka[:], c_ps[:, :, CKR:CG], rope_sb[:, 1, :, 0, :], ALU.mult)
                dve.tensor_tensor(kb[:, :, 0:HALF], c_ps[:, :, CKR + HALF:CG], rope_sb[:, 1, :, 1, 0:HALF], ALU.mult)
                chain(dve.tensor_tensor(kb[:, :, HALF:ROPE], c_ps[:, :, CKR:CKR + HALF],
                                        rope_sb[:, 1, :, 1, HALF:ROPE], ALU.mult))
                chained()
                dve.tensor_tensor(kp[:, :, 0:KVR], tkv[:], kvs_bc[:].unsqueeze(1).to_broadcast([P, TT, KVR]), ALU.mult)
                chain(dve.tensor_tensor(kp[:, :, KVR:P], ka[:], kb[:], ALU.add))
                chained()
                dve.tensor_copy(nkv[:, :, 0:KVR], kp[:, :, 0:KVR]).then_inc(kp_ready, 1)
                dve.wait_ge(kp_ready, b + 1)
                dve.tensor_tensor(nkv[:, :, KVR:2 * KVR], kp[:, :, 0:KVR], nkv[:, :, 0:KVR].bitcast(F32),
                                  ALU.subtract).then_inc(nkv_ready, 1)
                for i, (dst, src) in enumerate(((nqt, nqt_ps), (kt_s, kt_ps))):
                    dve.wait_ge(nk_hi, 2 * b + i + 1)
                    dve.tensor_tensor(dst[1][:], src, dst[0][:].bitcast(F32), ALU.subtract).then_inc(nk_lo, 1)

                def queries_rope(p):
                    dve.wait_ge(q_abs, NP_ * b + p + 1)
                    cos = rope_sb[:, 0, :, 0, :].unsqueeze(2).to_broadcast([P, TT, 2, ROPE])
                    sin = rope_sb[:, 0, :, 1, :].unsqueeze(2).to_broadcast([P, TT, 2, ROPE])
                    dve.tensor_tensor(qa[:], q_ps[:, :, :, KVR:P], cos, ALU.mult)
                    dve.tensor_tensor(qb[:, :, :, 0:HALF], q_ps[:, :, :, KVR + HALF:P], sin[:, :, :, 0:HALF], ALU.mult)
                    dve.tensor_tensor(qb[:, :, :, HALF:ROPE], q_ps[:, :, :, KVR:KVR + HALF], sin[:, :, :, HALF:ROPE],
                                      ALU.mult).then_inc(q_rope, 1)

                def queries_lo(p):
                    for i in range(2):
                        dve.wait_ge(qt_hi, 2 * NP_ * b + 2 * p + i + 1)
                        dve.tensor_tensor(qt_s[i][1][:], qt_ps[i], qt_s[i][0][:].bitcast(F32), ALU.subtract)\
                           .then_inc(qt_lo, 1)

                def maxima(p, par, qt):
                    dve.wait_ge(s_ready, 64 * b + 8 * p + 4 * par + qt + 1)
                    dve.tensor_reduce(negmax[:, par, qt:qt + 1], s_ps[qt % 2][:, 0:(qt + 1) * P], AX.X, ALU.max,
                                      negate=True).then_inc(max_ready, 1)

                def inverse(p, par, qt):
                    dve.wait_ge(exp_done, 64 * b + 8 * p + 4 * par + qt + 1)
                    dve.reciprocal(rinv[:, par, qt:qt + 1], rowsum[:, par, qt:qt + 1]).then_inc(rinv_ready, 1)

                def norm(p, par, qt):
                    w = (qt + 1) * P
                    dve.wait_ge(rinv_ready, 64 * b + 8 * p + 4 * par + qt + 1)
                    dve.tensor_scalar(prob[:, par, qt, 0:w], prob[:, par, qt, 0:w], rinv[:, par, qt:qt + 1], None,
                                      ALU.mult).then_inc(norm_dve, 1)

                def turned_lo(p, par, i):
                    lo, hi = ((0, 512), (512, PT_W))[i]
                    dve.wait_ge(pt_hi, 2 * NH * b + 4 * p + 2 * par + i + 1)
                    dve.tensor_tensor(pt_s[par][1][:, lo:hi], pt_ps[:, lo:hi], pt_s[par][0][:, lo:hi].bitcast(F32),
                                      ALU.subtract).then_inc(pt_lo, 1)

                def step(p, par):
                    now = has(p, par, 0)
                    if now:
                        maxima(p, par, 0)
                    if has(p, par, 1):
                        inverse(*((p, 0) if par else (p - 1, 1)), 3)
                    if has(p, par, 2):
                        turned_lo(p - 1, par, 0)
                    if now:
                        maxima(p, par, 1)
                        inverse(p, par, 0)
                        norm(p, par, 0)
                    if has(p, par, 2):
                        turned_lo(p - 1, par, 1)
                    if now:
                        inverse(p, par, 1)
                        norm(p, par, 1)
                        maxima(p, par, 2)
                    if has(p, par, 3):
                        pp, pr = (p - 1, 0) if par else (p - 2, 1)
                        dve.wait_ge(o_copied, NH * b + 2 * pp + pr + 1)
                        dve.tensor_tensor(lat[pr * KVR:pr * KVR + KVR, pp, :], o_ps[0:KVR, :], o_low[:], ALU.add)\
                           .then_inc(lat_added, 1)
                    if par == 0 and not (isinstance(p, int) and p + 1 >= NP_):
                        queries_rope(p + 1)
                    if now:
                        maxima(p, par, 3)
                        inverse(p, par, 2)
                    if par == 1 and not (isinstance(p, int) and p + 1 >= NP_):
                        queries_lo(p + 1)

                queries_rope(0)
                queries_lo(0)

                chain(dve.tensor_scalar(gate[:], expg[:], 1.0, None, ALU.add))
                chained()
                chain(dve.reciprocal(score[:, :, 0:NE], gate[:]))
                chained()
                carry_wait(1)
                for t in range(TT):
                    ins = dve.max(top8[:, t, :], score[:, t, :])
                chain(ins)
                chained()
                chain(dve.memset(top8[:, :, TOPK:8], -1.0))
                chained()
                carry_wait(2)
                for t in range(TT):
                    ins = dve.match_replace(picked[:, t, :], top8[:, t, :], score[:, t, :], -2.0)
                chain(ins)
                chained()
                for t in range(TT):
                    ins = dve.scalar_tensor_tensor(chosen[:, t, :], picked[:, t, 0:NE], -2.0, score[:, t, 0:NE],
                                                   ALU.is_equal, ALU.mult, accum_out=wsum[:, t:t + 1])
                chain(ins)
                chained()
                chain(dve.tensor_scalar(winv[:], wsum[:], 1e-20, None, ALU.add))
                chained()
                chain(dve.reciprocal(wsum[:], winv[:]))
                chained()
                dve.tensor_tensor(comb[:, b, :, 0:NE], chosen[:], wsum[:].unsqueeze(2).to_broadcast([P, TT, NE]),
                                  ALU.mult)

                pairs(dve, step, NH + 4)

                dve.wait_ge(xres_loaded, 16 * b + 16)
                dve.wait_ge(res_stored, 16 * b + 16)
                for i in range(2):
                    dve.wait_ge(acc_ready, 2 * b + i + 1)
                    dve.tensor_tensor(res[:, 2 * i:2 * i + 2, :], acc_ps[:, 2 * i:2 * i + 2, :],
                                      x_res[:, 2 * i:2 * i + 2, :], ALU.add).then_inc(res_added, 1)
                assert steps[0] == DVE_CHAIN, steps[0]


def experts(nc, ctx, sem, wg, wu, wd, xnt_dram, res_dram, comb, ident, ps, out):
    def sb(name, shape, dt=F32):
        return ctx.enter_context(nc.sbuf_tensor(name, shape, dt))

    wg_s = [sb("wg_hi", [P, KC, FALL], F32R), sb("wg_lo", [P, KC, FALL], F32R)]
    wu_s = [sb("wu_hi", [P, KC, FALL], F32R), sb("wu_lo", [P, KC, FALL], F32R)]
    wd_s = [sb("wd_hi", [P, NG * FC + 2, H], F32R), sb("wd_lo", [P, NG * FC + 2, H], F32R)]
    raw_g = sb("raw_g", [P, KC, FG])
    raw_u = sb("raw_u", [P, KC, FG])
    raw_d = sb("raw_d", [P, FC, H])
    xt = [sb("xt_hi_e", [P, KC, S], F32R), sb("xt_lo_e", [P, KC, S], F32R)]
    hidden = sb("hidden", [P, 2, FG])
    weighted = sb("weighted", [P, 2, FG])
    at_s = [[sb(f"at_hi{i}", [P, FC, P], F32R), sb(f"at_lo{i}", [P, FC, P], F32R)] for i in range(2)]
    res = sb("res_e", [P, TT, H])

    g_ps = [ps[:, 0, :], ps[:, 1, :]]
    u_ps = [ps[:, 2, :], ps[:, 3, :]]
    at_ps = [ps[:, 4 + i, 0:FG].rearrange("p (c t) -> p c t", c=FC) for i in range(2)]
    acc_ps = ps[:, 6:8, :].rearrange("p b (t n) -> p (b t) n", t=2)

    raw_loaded = [sem(f"raw_loaded{j}") for j in range(3)]
    w_hi, w_lo = sem("w_hi"), sem("w_lo")
    xt_loaded = [sem(f"xt_loaded{t}") for t in range(TT)]
    res_loaded, out_stored = sem("res_loaded"), sem("out_stored")
    gu_ready, silu_done, act_done = sem("gu_ready"), sem("silu_done"), sem("act_done")
    at_ready, at_hi, at_lo = sem("at_ready"), sem("at_hi"), sem("at_lo")
    out_ready, out_added = sem("out_ready"), sem("out_added")
    U = (NG + 1) * TT
    out_t = out.rearrange("b (t p) h -> b p t h", p=P)

    MAIN = (FG, EG, [P] * FC)
    SHARED = (FSH, FSH // FE, [P, FSH - P])

    def batch(eng, b, group, weights=None):
        if weights is not None:
            weights(0, MAIN)
        for e in range(2):
            if weights is not None:
                weights(e + 1, MAIN)
            group(b, e, MAIN)
        with eng.Fori(2, NG - 1) as e:
            if weights is not None:
                weights(e + 1, MAIN)
            group(b, e, MAIN)
        if weights is not None:
            weights(NG, SHARED)
        group(b, NG - 1, MAIN)
        group(b, NG, SHARED)

    def before(b, e, kind, t, lag):
        if t >= lag:
            return b, e, kind, t - lag
        t += TT - lag
        if isinstance(e, int) and e == 0:
            if isinstance(b, int) and b == 0:
                return None
            return b - 1, NG, SHARED, t
        return b, e - 1, MAIN, t

    def unit(b, e, t):
        return U * b + TT * e + t

    def all_batches(eng, group, weights=None):
        batch(eng, 0, group, weights)
        with eng.Fori(1, B) as b:
            batch(eng, b, group)

    def blocks(kind):
        return [(slice(0, FC), P)] if kind is MAIN else [(slice(0, 1), P), (slice(1, 2), FSH - P)]

    def w_parts(e, kind):
        f, _, rows = kind
        for raw, w, dram in ((raw_g, wg_s, wg), (raw_u, wu_s, wu)):
            yield raw[:, :, 0:f], [a[:, :, bass.ds(e * FG, f)] for a in w], dram[:, :, bass.ds(e * FG, f)]
        n = len(rows)
        yield raw_d[:, 0:n, :], [a[:, bass.ds(e * FC, n), :] for a in wd_s], wd[:, bass.ds(e * FC, n), :]

    with nc.Block() as block:
        @block.sync
        def _(sp):
            def load_tile(b, t):
                for i in range(2):
                    sp.dma_start(xt[i][:, :, t * P:(t + 1) * P].bitcast(F32),
                                 xnt_dram[b][:, i, :, t * P:(t + 1) * P]).then_inc(xt_loaded[t], 16)

            def load_weights(e, kind):
                for j, (raw, _, dram) in enumerate(w_parts(e, kind)):
                    if not (isinstance(e, int) and e == 0):
                        sp.wait_ge(w_lo, 3 * e + j - 2)
                    sp.dma_start(raw, dram).then_inc(raw_loaded[j], 16)

            for t in range(TT):
                load_tile(0, t)
            sp.dma_start(res[:], res_dram[0]).then_inc(res_loaded, 16)
            load_weights(0, MAIN)
            with sp.Fori(1, NG) as e:
                load_weights(e, MAIN)
            load_weights(NG, SHARED)

            def finish(b):
                sp.wait_ge(out_added, 2 * b + 2)
                sp.dma_start(out_t[b], res[:]).then_inc(out_stored, 16)

            with sp.Fori(1, B) as b:
                for t in range(TT):
                    sp.wait_ge(gu_ready, U * b - TT + t + 1)
                    load_tile(b, t)
                finish(b - 1)
                sp.wait_ge(out_stored, 16 * b)
                sp.dma_start(res[:], res_dram[b]).then_inc(res_loaded, 16)
            finish(B - 1)
            sp.wait_ge(out_stored, 16 * B)

        @block.tensor
        def _(pe):
            def turn(b, e, kind, t):
                f, _, rows = kind
                u = unit(b, e, t)
                pe.wait_ge(act_done, u + 1)
                if not (isinstance(b, int) and isinstance(e, int) and u < 2):
                    pe.wait_ge(at_lo, u - 1)
                for c, k in enumerate(rows):
                    mm = pe.transpose(at_ps[t % 2][0:k, c, :], weighted[:, t % 2, c * P:c * P + k], ident[:])
                mm.then_inc(at_ready, 1)

            def down(b, e, kind, t):
                _, _, rows = kind
                pe.wait_ge(at_lo, unit(b, e, t) + 1)
                first = isinstance(e, int) and e == 0
                last = kind is SHARED
                if first and t % 2 == 0 and not (isinstance(b, int) and b == 0):
                    pe.wait_ge(out_added, 2 * b - 1 + t // 2)
                for c, k in enumerate(rows):
                    mm = product3(pe, acc_ps[:, t, :], [a[0:k, c, :] for a in at_s[t % 2]],
                                  [w[0:k, e * FC + c, :] for w in wd_s], first and c == 0 and t % 2 == 0,
                                  last and c == len(rows) - 1, skip_group_check=True)
                if last and t % 2 == 1:
                    mm.then_inc(out_ready, 1)

            def group(b, e, kind):
                f = kind[0]
                for t in range(TT):
                    u = unit(b, e, t)
                    if isinstance(b, int) and t == 0:
                        pe.wait_ge(w_lo, 3 * e + 3)
                    if isinstance(e, int) and e == 0:
                        pe.wait_ge(xt_loaded[t], 32 * b + 32)
                    if not (isinstance(b, int) and isinstance(e, int) and u < 2):
                        pe.wait_ge(act_done, u - 1)
                    for dst, w in ((g_ps, wg_s), (u_ps, wu_s)):
                        for kc in range(KC):
                            mm = product3(pe, dst[t % 2][:, 0:f], [a[:, kc, t * P:(t + 1) * P] for a in xt],
                                          [a[:, kc, bass.ds(e * FG, f)] for a in w], kc == 0, kc == KC - 1)
                    mm.then_inc(gu_ready, 1)
                    if before(b, e, kind, t, 1):
                        turn(*before(b, e, kind, t, 1))
                    if before(b, e, kind, t, 2):
                        down(*before(b, e, kind, t, 2))

            all_batches(pe, group)
            turn(B - 1, NG, SHARED, TT - 1)
            down(B - 1, NG, SHARED, TT - 2)
            down(B - 1, NG, SHARED, TT - 1)

        @block.scalar
        def _(act):
            def weights(e, kind):
                for j, (raw, (hi, _), _) in enumerate(w_parts(e, kind)):
                    act.wait_ge(raw_loaded[j], 16 * e + 16)
                    act.activation(hi, raw, ACT.Copy).then_inc(w_hi, 1)

            def turned_hi(b, e, kind, t):
                act.wait_ge(at_ready, unit(b, e, t) + 1)
                for c, k in blocks(kind):
                    ins = act.activation(at_s[t % 2][0][0:k, c, :], at_ps[t % 2][0:k, c, :], ACT.Copy)
                ins.then_inc(at_hi, 1)

            def group(b, e, kind):
                f = kind[0]
                for t in range(TT):
                    act.wait_ge(gu_ready, unit(b, e, t) + 1)
                    act.activation(hidden[:, t % 2, 0:f], g_ps[t % 2][:, 0:f], ACT.Silu).then_inc(silu_done, 1)
                    if before(b, e, kind, t, 1):
                        turned_hi(*before(b, e, kind, t, 1))

            all_batches(act, group, weights)
            turned_hi(B - 1, NG, SHARED, TT - 1)

        @block.vector
        def _(dve):
            def weights(e, kind):
                for j, (raw, (hi, lo), _) in enumerate(w_parts(e, kind)):
                    dve.wait_ge(w_hi, 3 * e + j + 1)
                    dve.tensor_tensor(lo, raw, hi.bitcast(F32), ALU.subtract).then_inc(w_lo, 1)

            def turned_lo(b, e, kind, t):
                dve.wait_ge(at_hi, unit(b, e, t) + 1)
                for c, k in blocks(kind):
                    ins = dve.tensor_tensor(at_s[t % 2][1][0:k, c, :], at_ps[t % 2][0:k, c, :],
                                            at_s[t % 2][0][0:k, c, :].bitcast(F32), ALU.subtract)
                ins.then_inc(at_lo, 1)

            def add(b, i):
                dve.wait_ge(out_ready, 2 * b + i + 1)
                if i == 0:
                    dve.wait_ge(res_loaded, 16 * b + 16)
                half = res[:, 2 * i:2 * i + 2, :]
                dve.tensor_tensor(half, acc_ps[:, 2 * i:2 * i + 2, :], half, ALU.add).then_inc(out_added, 1)

            def group(b, e, kind):
                _, ne, _ = kind
                for t in range(TT):
                    if isinstance(e, int) and e == 0 and t % 2 == 0 and not (isinstance(b, int) and b == 0):
                        add(b - 1, t // 2)
                    dve.wait_ge(silu_done, unit(b, e, t) + 1)
                    for j in range(ne):
                        cols = slice(j * FE, (j + 1) * FE)
                        ins = dve.scalar_tensor_tensor(weighted[:, t % 2, cols], hidden[:, t % 2, cols],
                                                       comb[:, b, t, bass.ds(e * EG + j, 1)], u_ps[t % 2][:, cols],
                                                       ALU.mult, ALU.mult)
                    ins.then_inc(act_done, 1)
                    if before(b, e, kind, t, 1):
                        turned_lo(*before(b, e, kind, t, 1))

            all_batches(dve, group, weights)
            turned_lo(B - 1, NG, SHARED, TT - 1)
            for i in range(2):
                add(B - 1, i)


def kernel(**inputs):
    import numpy as np
    import concourse.bacc as bacc
    from concourse.bass_utils import run_bass_kernel_spmd

    def arr(name):
        return np.asarray(inputs["L0_" + name])

    def rows(a, n=P):
        return a.reshape(-1, n, a.shape[-1]).transpose(1, 0, 2)

    halves = np.concatenate([np.arange(0, ROPE, 2), np.arange(1, ROPE, 2)])
    wqr = arr("attn_W_dq_rope").reshape(QR, NH, ROPE)[:, :, halves]
    krope = arr("attn_W_krope")[:, halves]
    hid = arr("ffn_wg"), arr("ffn_wu")
    shared = arr("ffn_sg"), arr("ffn_su")
    up = [np.concatenate([w.transpose(1, 0, 2).reshape(H, NE * FE), s], axis=1) for w, s in zip(hid, shared)]
    down = np.concatenate([arr("ffn_wd").reshape(NE * FE, H), arr("ffn_sd"), np.zeros((P - FSH % P, H), np.float32)])

    inv_freq = (np.float32(1.0) / np.float32(10000.0) ** (np.arange(HALF, dtype=np.float32) * np.float32(2.0 / ROPE)))
    ang = np.arange(S, dtype=np.float32)[:, None] * inv_freq.astype(np.float32)[None, :]
    cos, sin = np.cos(ang), np.sin(ang)
    table = np.stack([np.concatenate([cos, cos], 1), np.concatenate([-sin, sin], 1)], 1).astype(np.float32)
    table = np.stack([table, table / np.float32(NH)]).reshape(2, TT, P, 2, ROPE).transpose(2, 0, 1, 3, 4)

    arrays = {
        "x": arr("attn_x"),
        "wc": rows(np.concatenate([arr("attn_W_cq"), arr("attn_W_ckv"), krope, arr("ffn_gate_w")], axis=1)),
        "wqr": wqr,
        "nopeT": arr("attn_W_dq_nope").reshape(QR, NH, NOPE).transpose(2, 1, 0),
        "dkT": arr("attn_W_dk_nope").reshape(KVR, NH, NOPE).transpose(2, 1, 0),
        "dvT": arr("attn_W_dv").reshape(KVR, NH, VD).transpose(2, 1, 0),
        "wo": arr("attn_W_o").reshape(NH, VD, H).transpose(1, 0, 2),
        "qscale": arr("attn_q_scale"),
        "kvscale": arr("attn_kv_scale"),
        "rope": table,
        "wg": rows(up[0]),
        "wu": rows(up[1]),
        "wd": rows(down),
    }
    nc = bacc.Bacc("TRN2", target_bir_lowering=False, num_devices=1)
    args, given = [], {}
    for name, a in arrays.items():
        a = np.ascontiguousarray(a)
        given[f"in_{name}"] = a
        args.append(nc.dram_tensor(f"in_{name}", a.shape, mybir.dt.from_np(a.dtype), kind="ExternalInput").ap())
    args.append(nc.dram_tensor("out", (B, S, H), F32, kind="ExternalOutput").ap())
    build(nc, *args)
    r = run_bass_kernel_spmd(nc, [given], core_ids=[0])
    return r.results[0]["out"]
```

```python
from contextlib import ExitStack

import concourse.bass as bass
from concourse import mybir

F32 = mybir.dt.float32
F32R = mybir.dt.float32r
BF16 = mybir.dt.bfloat16
ALU = mybir.AluOpType
ACT = mybir.ActivationFunctionType
AX = mybir.AxisListType

P = 128
B, S, H = 8, 512, 256
TT = S // P
KC = H // P
NH, NOPE, ROPE, VD = 16, 128, 64, 128
HALF = ROPE // 2
QR, KVR = 128, 64
NP_ = NH // 2
NE, FE, FSH, TOPK = 32, 96, 192, 6
EG = 4
NG = NE // EG
FG = EG * FE
FC = FG // P
FALL = NE * FE + FSH
NCOMB = NE + FSH // FE
CW = QR + KVR + ROPE + NE
CKV, CKR, CG = QR, QR + KVR, QR + KVR + ROPE
SCALE = float((NOPE + ROPE) ** -0.5)
LN_EPS, RMS_EPS = 1e-5, 1e-6
MASKED = -1e30
PT_AT = [0, 512, 1024, 896]
PT_W = 1280


def split(dve, act, hi, lo, src, hi_sem, hi_value, lo_sem, hi_inc=1):
    if act is not None:
        act.activation(hi, src, ACT.Copy).then_inc(hi_sem, hi_inc)
    if dve is not None:
        dve.wait_ge(hi_sem, hi_value)
        dve.tensor_tensor(lo, src, hi.bitcast(F32), ALU.subtract).then_inc(lo_sem, 1)


def product3(pe, out, lhs, rhs, first, last, **kw):
    (lh, ll), (rh, rl) = lhs, rhs
    pe.matmul(out, lh, rh, start=first, stop=False, **kw)
    pe.matmul(out, lh, rl, start=False, stop=False, **kw)
    return pe.matmul(out, ll, rh, start=False, stop=last, **kw)


def build(nc, x, wc, wqr, nopeT, dkT, dvT, wo, qscale, kvscale, rope, wg, wu, wd, out):
    with ExitStack() as top:
        def sem(name):
            return top.enter_context(nc.semaphore(name))

        xnt_dram = nc.dram_tensor("xnt_dram", (B, P, 2, KC, S), F32, kind="Internal").ap()
        res_dram = nc.dram_tensor("res_dram", (B, P, TT, H), F32, kind="Internal").ap()
        nqt_dram = nc.dram_tensor("nqt_dram", (B, P, 2, S), F32, kind="Internal").ap()
        nkv_dram = nc.dram_tensor("nkv_dram", (B, P, TT, 2 * KVR), F32, kind="Internal").ap()
        comb = top.enter_context(nc.sbuf_tensor("comb", [P, B, TT, NCOMB], F32))
        ident = top.enter_context(nc.sbuf_tensor("ident", [P, P], F32))
        ps = top.enter_context(nc.psum_tensor("ps", [P, 8, 512], F32))
        with ExitStack() as ctx:
            attention(nc, ctx, sem, x, wc, wqr, nopeT, dkT, dvT, wo, qscale, kvscale, rope,
                      xnt_dram, res_dram, nqt_dram, nkv_dram, comb, ident, ps)
        with ExitStack() as ctx:
            experts(nc, ctx, sem, wg, wu, wd, xnt_dram, res_dram, comb, ident, ps, out)


def attention(nc, ctx, sem, x, wc, wqr, nopeT, dkT, dvT, wo, qscale, kvscale, rope,
              xnt_dram, res_dram, nqt_dram, nkv_dram, comb, ident, ps):
    def sb(name, shape, dt=F32):
        return ctx.enter_context(nc.sbuf_tensor(name, shape, dt))

    wq_s = [sb("wq_hi", [P, NH, P], F32R), sb("wq_lo", [P, NH, P], F32R)]
    wvo_s = [sb("wvo_hi", [P, NP_, H], F32R), sb("wvo_lo", [P, NP_, H], F32R)]
    kt_s = [sb("kt_hi", [P, B, S], F32R), sb("kt_lo", [P, B, S], F32R)]
    rope_sb = sb("rope_sb", [P, 2, TT, 2, ROPE])
    minus_half = sb("minus_half", [P, 2 * TT])
    ident_bf = sb("ident_bf", [P, P], BF16)
    mask_bf = sb("mask_bf", [P, P], BF16)

    lctx = ExitStack()
    latents = lctx.enter_context
    wc_s = [latents(nc.sbuf_tensor(name, [P, KC, CW], F32R)) for name in ("wc_hi", "wc_lo")]
    kvs_bc = latents(nc.sbuf_tensor("kvs_bc", [P, KVR], F32))

    consts_ready = sem("consts_ready")
    loaded = sem("weights_loaded")
    absorbed = sem("absorbed")
    prep_dve = sem("prep_dve")
    prep_hi = sem("prep_hi")
    prep_lo = sem("prep_lo")

    with ExitStack() as pctx:
        def tb(name, shape, dt=F32):
            return pctx.enter_context(nc.sbuf_tensor(name, shape, dt))

        wc_raw = tb("wc_raw", [P, KC, CW])
        wqr_raw = tb("wqr_raw", [P, NH, ROPE])
        nope_raw = tb("nope_raw", [P, NH, QR])
        dk_raw = tb("dk_raw", [P, NH, KVR])
        dv_raw = tb("dv_raw", [P, NH, KVR])
        wo_raw = tb("wo_raw", [P, NH, H])
        qs = tb("qs", [P, 1])
        wq_f = tb("wq_f", [P, NH, P])
        absorbed_ps = ps[:, 0:2, :].rearrange("p b (h r) -> p (b h) r", r=KVR)
        wvo_ps = ps[:, 2:6, :].rearrange("p b (h n) -> p (b h) n", n=H)

        with nc.Block() as block:
            @block.sync
            def _(sp):
                for dst, src in ((nope_raw, nopeT), (dk_raw, dkT), (wqr_raw, wqr), (dv_raw, dvT),
                                 (wo_raw, wo), (wc_raw, wc), (rope_sb, rope)):
                    sp.dma_start(dst[:], src).then_inc(loaded, 16)
                sp.dma_start(qs[:], qscale.rearrange("(p a) -> p a", a=1)).then_inc(loaded, 16)
                sp.dma_start(kvs_bc[:], kvscale.rearrange("(a r) -> a r", a=1).to_broadcast([P, KVR]))\
                  .then_inc(loaded, 16)
                sp.wait_ge(loaded, 9 * 16)

            @block.gpsimd
            def _(pool):
                pool.memset(ident[:], 0.0).then_inc(consts_ready, 1)
                pool.memset(ident_bf[:], 0.0).then_inc(consts_ready, 1)
                pool.memset(mask_bf[:], 0.0).then_inc(consts_ready, 1)
                pool.memset(minus_half[:], -0.5).then_inc(consts_ready, 1)
                pool.wait_ge(consts_ready, 4)
                for m in (ident, ident_bf):
                    pool.affine_select(out=m[:], in_=m[:], compare_op=ALU.not_equal, fill=1.0, base=0,
                                       pattern=[[-1, P]], channel_multiplier=1).then_inc(consts_ready, 1)
                pool.affine_select(out=mask_bf[:], in_=mask_bf[:], compare_op=ALU.is_ge, fill=MASKED, base=0,
                                   pattern=[[-1, P]], channel_multiplier=1).then_inc(consts_ready, 1)

            @block.tensor
            def _(pe):
                pe.wait_ge(loaded, 9 * 16)
                for h in range(NH):
                    mm = pe.matmul(absorbed_ps[:, h, :], nope_raw[:, h, :], dk_raw[:, h, :], start=True, stop=True)
                mm.then_inc(absorbed, 1)
                for h in range(NH):
                    at = (h % 2) * KVR
                    mm = pe.matmul(wvo_ps[at:at + KVR, h // 2, :], dv_raw[:, h, :], wo_raw[:, h, :],
                                   start=True, stop=True)
                mm.then_inc(absorbed, 1)

            @block.scalar
            def _(act):
                act.wait_ge(loaded, 9 * 16)
                split(None, act, wc_s[0][:], None, wc_raw[:], prep_hi, 0, None)
                act.wait_ge(prep_dve, 2)
                split(None, act, wq_s[0][:], None, wq_f[:], prep_hi, 0, None)
                act.wait_ge(absorbed, 2)
                split(None, act, wvo_s[0][:], None, wvo_ps, prep_hi, 0, None)

            @block.vector
            def _(dve):
                dve.wait_ge(loaded, 9 * 16)
                dve.tensor_scalar(wq_f[:, :, KVR:P], wqr_raw[:], qs[:, 0:1], SCALE, ALU.mult, ALU.mult)\
                   .then_inc(prep_dve, 1)
                dve.memset(comb[:, :, :, NE:NCOMB], 1.0)
                dve.wait_ge(absorbed, 1)
                dve.tensor_scalar(wq_f[:, :, 0:KVR], absorbed_ps, qs[:, 0:1], SCALE, ALU.mult, ALU.mult)\
                   .then_inc(prep_dve, 1)
                dve.wait_ge(prep_dve, 2)
                split(dve, None, wc_s[0][:], wc_s[1][:], wc_raw[:], prep_hi, 1, prep_lo)
                split(dve, None, wq_s[0][:], wq_s[1][:], wq_f[:], prep_hi, 2, prep_lo)
                dve.wait_ge(absorbed, 2)
                split(dve, None, wvo_s[0][:], wvo_s[1][:], wvo_ps, prep_hi, 3, prep_lo)

    with lctx:
        project(nc, lctx, sem, x, wc_s, kvs_bc, kt_s, rope_sb, minus_half, ident, comb, ps,
                xnt_dram, nqt_dram, nkv_dram)
    heads(nc, ctx, sem, x, wq_s, wvo_s, kt_s, rope_sb, ident, ident_bf, mask_bf, ps,
          nqt_dram, nkv_dram, res_dram)


def project(nc, ctx, sem, x, wc_s, kvs_bc, kt_s, rope_sb, minus_half, ident, comb, ps,
            xnt_dram, nqt_dram, nkv_dram):
    def sb(name, shape, dt=F32):
        return ctx.enter_context(nc.sbuf_tensor(name, shape, dt))

    x_in = sb("x_in", [P, TT, H])
    spare = sb("spare", [P, 8])
    stats = sb("stats", [P, TT, 6])
    mv = sb("mv", [P, TT, 2])
    var = sb("var", [P, TT])
    rstd = sb("rstd", [P, TT])
    xn = sb("xn", [P, TT, H])
    xnt = [sb("xnt_hi", [P, KC, S], F32R), sb("xnt_lo", [P, KC, S], F32R)]
    junk = sb("junk", [P, TT, QR + KVR])
    sumsq = sb("sumsq", [P, 2, TT])
    meansq = sb("meansq", [P, 2, TT])
    rms = sb("rms", [P, 2, TT])
    nq = sb("nq", [P, TT, QR])
    tkv = sb("tkv", [P, TT, KVR])
    kp = sb("kp", [P, TT, P])
    ka = sb("ka", [P, TT, ROPE])
    kb = sb("kb", [P, TT, ROPE])
    nkv = sb("nkv_out", [P, TT, 2 * KVR], F32R)
    nqt = sb("nqt_out", [P, 2, S], F32R)
    expg = sb("expg", [P, TT, NE])
    gate = sb("gate", [P, TT, NE])
    score = sb("score", [P, TT, NE + 2])
    top8 = sb("top8", [P, TT, 8])
    picked = sb("picked", [P, TT, NE + 2])
    chosen = sb("chosen", [P, TT, NE])
    wsum = sb("wsum", [P, TT])
    winv = sb("winv", [P, TT])

    xt_ps = ps[:, 0:2, :]
    c_ps = ps[:, 2:6, 0:CW]
    nqt_ps, kt_ps = ps[:, 6, :], ps[:, 7, :]

    x_loaded = sem("x_loaded")
    var_ready, rstd_ready, xn_ready = sem("var_ready"), sem("rstd_ready"), sem("xn_ready")
    norm_chain, gate_chain = sem("norm_chain"), sem("gate_chain")
    xt_ready, xt_hi, xt_lo, xt_stored = sem("xt_ready"), sem("xt_hi"), sem("xt_lo"), sem("xt_stored")
    c_ready, squared, logits_exp = sem("c_ready"), sem("squared"), sem("logits_exp")
    meansq_ready, rms_ready = sem("meansq_ready"), sem("rms_ready")
    nq_ready, kp_parts, kp_ready, nkv_ready = sem("nq_ready"), sem("kp_parts"), sem("kp_ready"), sem("nkv_ready")
    nk_ready, nk_hi, nk_lo = sem("nk_ready"), sem("nk_hi"), sem("nk_lo")
    nq_stored, nkv_stored, expg_read = sem("nq_stored"), sem("nkv_stored"), sem("expg_read")

    x_t = x.rearrange("b (t p) h -> b p t h", p=P)
    GATE_CHAIN = 8

    def all_batches(eng, first, body):
        first()
        with eng.Fori(0, B - 1) as i:
            body(i, i + 1)
        body(B - 1, None)

    with nc.Block() as block:
        @block.sync
        def _(sp):
            def load():
                sp.dma_start(x_in[:], x_t[0]).then_inc(x_loaded, 16)

            def body(i, j):
                if j is not None:
                    sp.wait_ge(xn_ready, TT * i + TT)
                    sp.dma_start(x_in[:], x_t[j]).then_inc(x_loaded, 16)
                sp.wait_ge(xt_hi, KC * i + KC)
                sp.dma_start(xnt_dram[i][:, 0], xnt[0][:].bitcast(F32)).then_inc(xt_stored, 16)
                sp.wait_ge(xt_lo, KC * i + KC)
                sp.dma_start(xnt_dram[i][:, 1], xnt[1][:].bitcast(F32)).then_inc(xt_stored, 16)
                sp.wait_ge(nkv_ready, i + 1)
                sp.dma_start(nkv_dram[i], nkv[:].bitcast(F32)).then_inc(nkv_stored, 16)
                sp.wait_ge(nk_lo, 2 * i + 2)
                sp.dma_start(nqt_dram[i], nqt[:].bitcast(F32)).then_inc(nq_stored, 16)

            all_batches(sp, load, body)
            sp.wait_ge(xt_stored, 32 * B)
            sp.wait_ge(nkv_stored, 16 * B + 16)
            sp.wait_ge(nq_stored, 16 * B + 16)

        @block.gpsimd
        def _(pool):
            def token_rstd(i):
                pool.wait_ge(var_ready, i + 1)
                pool.tensor_tensor(rstd[:], var[:], minus_half[:, 0:TT], ALU.pow).then_inc(rstd_ready, 1)

            def body(i, j):
                if j is not None:
                    token_rstd(j)
                pool.wait_ge(meansq_ready, 2 * i + 2)
                pool.tensor_tensor(rms[:].rearrange("p k t -> p (k t)"), meansq[:].rearrange("p k t -> p (k t)"),
                                   minus_half[:], ALU.pow).then_inc(rms_ready, 1)

            all_batches(pool, lambda: token_rstd(0), body)

        @block.tensor
        def _(pe):
            def tokens_turn(i):
                pe.wait_ge(xn_ready, TT * i + TT)
                for kc in range(KC):
                    for t in range(TT):
                        mm = pe.transpose(xt_ps[:, kc, t * P:(t + 1) * P], xn[:, t, kc * P:(kc + 1) * P], ident[:])
                    mm.then_inc(xt_ready, 1)

            def body(i, j):
                pe.wait_ge(xt_lo, KC * i + KC)
                for t in range(TT):
                    for kc in range(KC):
                        mm = product3(pe, c_ps[:, t, :], [a[:, kc, t * P:(t + 1) * P] for a in xnt],
                                      [w[:, kc, :] for w in wc_s], kc == 0, kc == KC - 1)
                    mm.then_inc(c_ready, 1)
                if j is not None:
                    tokens_turn(j)
                pe.wait_ge(nq_ready, i + 1)
                for t in range(TT):
                    mm = pe.transpose(nqt_ps[:, t * P:(t + 1) * P], nq[:, t, :], ident[:])
                mm.then_inc(nk_ready, 1)
                pe.wait_ge(kp_ready, i + 1)
                for t in range(TT):
                    mm = pe.transpose(kt_ps[:, t * P:(t + 1) * P], kp[:, t, :], ident[:])
                mm.then_inc(nk_ready, 1)

            all_batches(pe, lambda: tokens_turn(0), body)

        @block.scalar
        def _(act):
            def tokens_hi(i, stored):
                for kc in range(KC):
                    act.wait_ge(xt_ready, KC * i + kc + 1)
                    if stored is not None and kc == 0:
                        act.wait_ge(xt_stored, stored)
                    act.activation(xnt[0][:, kc, :], xt_ps[:, kc, :], ACT.Copy).then_inc(xt_hi, 1)

            def body(i, j):
                for t in range(TT):
                    act.wait_ge(c_ready, TT * i + t + 1)
                    for k, (at, w) in enumerate(((0, QR), (CKV, KVR))):
                        act.activation(junk[:, t, at:at + w], c_ps[:, t, at:at + w], ACT.Square,
                                       accum_out=sumsq[:, k, t:t + 1]).then_inc(squared, 1)
                act.wait_ge(expg_read, i + 1)
                act.activation(expg[:], c_ps[:, :, CG:CW], ACT.Exp, scale=-1.0).then_inc(logits_exp, 1)
                if j is not None:
                    tokens_hi(j, 32 * i + 32)
                act.wait_ge(nk_ready, 2 * i + 1)
                act.wait_ge(nq_stored, 16 * i + 16)
                act.activation(nqt[:, 0, :], nqt_ps, ACT.Copy).then_inc(nk_hi, 1)
                act.wait_ge(nk_ready, 2 * i + 2)
                act.activation(kt_s[0][:, i, :], kt_ps, ACT.Copy).then_inc(nk_hi, 1)

            all_batches(act, lambda: tokens_hi(0, None), body)

        @block.vector
        def _(dve):
            def carry_wait(i):
                dve.memset(spare[:, i:i + 1], 0.0)

            def layer_norm(i):
                dve.wait_ge(x_loaded, 16 * i + 16)
                for t in range(TT):
                    ins = dve.bn_stats(stats[:, t, :], x_in[:, t, :])
                ins.then_inc(norm_chain, 1)
                dve.wait_ge(norm_chain, 2 * i + 1)
                carry_wait(0)
                for t in range(TT):
                    ins = dve.bn_aggr(mv[:, t, :], stats[:, t, :])
                ins.then_inc(norm_chain, 1)
                dve.wait_ge(norm_chain, 2 * i + 2)
                dve.tensor_scalar(var[:], mv[:, :, 1], LN_EPS, None, ALU.add).then_inc(var_ready, 1)
                dve.wait_ge(rstd_ready, i + 1)
                for t in range(TT):
                    dve.tensor_scalar(xn[:, t, :], x_in[:, t, :], mv[:, t, 0:1], rstd[:, t:t + 1],
                                      ALU.subtract, ALU.mult).then_inc(xn_ready, 1)

            def tokens_lo(i):
                for kc in range(KC):
                    dve.wait_ge(xt_hi, KC * i + kc + 1)
                    dve.tensor_tensor(xnt[1][:, kc, :], xt_ps[:, kc, :], xnt[0][:, kc, :].bitcast(F32), ALU.subtract)\
                       .then_inc(xt_lo, 1)

            def latents(i):
                dve.wait_ge(squared, 2 * TT * i + 2 * TT)
                for k, n in enumerate((QR, KVR)):
                    dve.tensor_scalar(meansq[:, k, :], sumsq[:, k, :], 1.0 / n, RMS_EPS, ALU.mult, ALU.add)\
                       .then_inc(meansq_ready, 1)
                dve.wait_ge(rms_ready, i + 1)
                dve.wait_ge(logits_exp, i + 1)
                dve.tensor_tensor(nq[:], c_ps[:, :, 0:QR], rms[:, 0, :].unsqueeze(2).to_broadcast([P, TT, QR]),
                                  ALU.mult).then_inc(nq_ready, 1)
                dve.tensor_tensor(tkv[:], c_ps[:, :, CKV:CKR], rms[:, 1, :].unsqueeze(2).to_broadcast([P, TT, KVR]),
                                  ALU.mult)
                dve.tensor_tensor(ka[:], c_ps[:, :, CKR:CG], rope_sb[:, 1, :, 0, :], ALU.mult)
                dve.tensor_tensor(kb[:, :, 0:HALF], c_ps[:, :, CKR + HALF:CG], rope_sb[:, 1, :, 1, 0:HALF], ALU.mult)
                dve.tensor_tensor(kb[:, :, HALF:ROPE], c_ps[:, :, CKR:CKR + HALF], rope_sb[:, 1, :, 1, HALF:ROPE],
                                  ALU.mult).then_inc(kp_parts, 1)
                dve.wait_ge(kp_parts, 2 * i + 1)
                dve.tensor_tensor(kp[:, :, KVR:P], ka[:], kb[:], ALU.add)
                dve.tensor_tensor(kp[:, :, 0:KVR], tkv[:], kvs_bc[:].unsqueeze(1).to_broadcast([P, TT, KVR]),
                                  ALU.mult).then_inc(kp_ready, 1)
                dve.wait_ge(kp_ready, i + 1)
                dve.wait_ge(nkv_stored, 16 * i + 16)
                dve.tensor_copy(nkv[:, :, 0:KVR], kp[:, :, 0:KVR]).then_inc(kp_parts, 1)
                dve.wait_ge(kp_parts, 2 * i + 2)
                dve.tensor_tensor(nkv[:, :, KVR:2 * KVR], kp[:, :, 0:KVR], nkv[:, :, 0:KVR].bitcast(F32),
                                  ALU.subtract).then_inc(nkv_ready, 1)

            def latents_lo(i):
                for k, (hi, lo, src) in enumerate(((nqt[:, 0, :], nqt[:, 1, :], nqt_ps),
                                                   (kt_s[0][:, i, :], kt_s[1][:, i, :], kt_ps))):
                    dve.wait_ge(nk_hi, 2 * i + k + 1)
                    dve.tensor_tensor(lo, src, hi.bitcast(F32), ALU.subtract).then_inc(nk_lo, 1)

            def gates(i):
                steps = [0]

                def chain(ins):
                    steps[0] += 1
                    ins.then_inc(gate_chain, 1)
                    dve.wait_ge(gate_chain, 1 + GATE_CHAIN * i + steps[0])

                dve.tensor_scalar(gate[:], expg[:], 1.0, None, ALU.add).then_inc(expg_read, 1)
                dve.wait_ge(expg_read, i + 2)
                chain(dve.reciprocal(score[:, :, 0:NE], gate[:]))
                carry_wait(1)
                for t in range(TT):
                    ins = dve.max(top8[:, t, :], score[:, t, :])
                chain(ins)
                chain(dve.memset(top8[:, :, TOPK:8], -1.0))
                carry_wait(2)
                for t in range(TT):
                    ins = dve.match_replace(picked[:, t, :], top8[:, t, :], score[:, t, :], -2.0)
                chain(ins)
                for t in range(TT):
                    ins = dve.scalar_tensor_tensor(chosen[:, t, :], picked[:, t, 0:NE], -2.0, score[:, t, 0:NE],
                                                   ALU.is_equal, ALU.mult, accum_out=wsum[:, t:t + 1])
                chain(ins)
                chain(dve.tensor_scalar(winv[:], wsum[:], 1e-20, None, ALU.add))
                chain(dve.reciprocal(wsum[:], winv[:]))
                chain(dve.tensor_tensor(comb[:, i, :, 0:NE], chosen[:],
                                        wsum[:].unsqueeze(2).to_broadcast([P, TT, NE]), ALU.mult))
                assert steps[0] == GATE_CHAIN, steps[0]

            def start():
                dve.memset(score[:, :, NE:NE + 2], -1.0).then_inc(gate_chain, 1)
                dve.memset(spare[:, 3:4], 0.0).then_inc(nq_stored, 16)
                dve.memset(spare[:, 4:5], 0.0).then_inc(nkv_stored, 16)
                dve.memset(spare[:, 5:6], 0.0).then_inc(expg_read, 1)
                dve.wait_ge(gate_chain, 1)
                layer_norm(0)
                tokens_lo(0)

            def body(i, j):
                if j is not None:
                    layer_norm(j)
                latents(i)
                if j is not None:
                    tokens_lo(j)
                latents_lo(i)
                gates(i)

            all_batches(dve, start, body)


def heads(nc, ctx, sem, x, wq_s, wvo_s, kt_s, rope_sb, ident, ident_bf, mask_bf, ps,
          nqt_dram, nkv_dram, res_dram):
    def sb(name, shape, dt=F32):
        return ctx.enter_context(nc.sbuf_tensor(name, shape, dt))

    QUART = NP_ // 2
    x_res = sb("x_res", [P, TT, H])
    res = sb("res", [P, TT, H])
    primer = sb("primer", [P, 1])
    nqt = [sb(f"nqt{i}", [P, 2, S], F32R) for i in range(2)]
    nkv = [sb(f"nkv{i}", [P, TT, 2 * KVR], F32R) for i in range(2)]
    qp = sb("qp", [P, TT, 2, P])
    qa = sb("qa", [P, TT, 2, ROPE])
    qb = sb("qb", [P, TT, 2, ROPE])
    qt_s = [[[sb(f"qt{i}{j}_{k}", [P, S], F32R) for k in ("hi", "lo")] for j in range(2)] for i in range(2)]
    negmax = sb("negmax", [P, 2, TT])
    rowsum = sb("rowsum", [P, 2, TT])
    rinv = sb("rinv", [P, 2, TT])
    minus_one = sb("minus_one", [P, 1])
    prob = sb("prob", [P, 2, TT, S])
    pt_s = [sb("pt_hi", [P, PT_W], F32R), sb("pt_lo", [P, PT_W], F32R)]
    o_low = sb("o_low", [KVR, S])
    lat = sb("lat", [P, 2, S])
    lat_s = [sb("lat_hi", [P, NP_, S], F32R), sb("lat_lo", [P, NP_, S], F32R)]

    q_ps = ps[:, 0:2, :].rearrange("p b (t h c) -> p (b t) h c", t=2, h=2)
    qt_ps = [ps[:, 0, :], ps[:, 1, :]]
    s_ps = [ps[:, 2, :], ps[:, 3, :]]
    pt_ps = ps[:, 4:7, :].rearrange("p b n -> p (b n)")
    o_ps = ps[:, 7, :]
    acc_ps = ps[:, 1, :].rearrange("p (t n) -> p t n", t=2)

    nqt_loaded = [sem(f"nqt_loaded{i}") for i in range(2)]
    nkv_loaded = [sem(f"nkv_loaded{i}") for i in range(2)]
    xres_loaded = sem("xres_loaded")
    q_ready, q_abs, q_rope, q_done = sem("q_ready"), sem("q_abs"), sem("q_rope"), sem("q_done")
    qt_ready, qt_hi, qt_lo = sem("qt_ready"), sem("qt_hi"), sem("qt_lo")
    s_ready, max_ready, exp_done, rinv_ready = sem("s_ready"), sem("max_ready"), sem("exp_done"), sem("rinv_ready")
    minus_one_ready, normed = sem("minus_one_ready"), sem("normed")
    pt_ready, pt_hi, pt_lo = sem("pt_ready"), sem("pt_hi"), sem("pt_lo")
    pv_ready, o_copied, lat_added = sem("pv_ready"), sem("o_copied"), sem("lat_added")
    lat_hi, lat_lo = sem("lat_hi"), sem("lat_lo")
    acc_ready, res_added = sem("acc_ready"), sem("res_added")
    res_stored = sem("res_stored")

    x_t = x.rearrange("b (t p) h -> b p t h", p=P)
    TAIL = 4

    class Batches:
        def __init__(self, now, last, following):
            self.now, self.last, self.following = now, last, following

        def back(self, g, lag):
            if 0 <= g - lag < NH:
                return self.now, g - lag
            return None if g >= NH + lag or self.last is None else (self.last, g - lag + NH)

        def next_pair(self, p):
            if p + 1 < NP_:
                return self.now, p + 1
            return None if self.following is None or p >= NP_ else (self.following, 0)

        def piece(self, g):
            p, par = divmod(g, 2)
            if par == 0 and p in (QUART - 2, QUART - 1) and self.last is not None:
                return self.last, 1, p - QUART + 2
            if par == 0 and p in (NP_ - 2, NP_ - 1):
                return self.now, 0, p - NP_ + 2
            return None

    def pipeline(step):
        def run(eng):
            for g in range(NH // 2):
                step(Batches(0, None, 1), g)
            with eng.Fori(0, B - 1) as b:
                for g in range(NH // 2, NH):
                    step(Batches(b, None, b + 1), g)
                for g in range(NH // 2):
                    step(Batches(b + 1, b, None), g)
            for g in range(NH // 2, NH + TAIL):
                step(Batches(B - 1, None, None), g)
        return run

    def unit(b, g, qt=0):
        return TT * (NH * b + g) + qt

    with nc.Block() as block:
        @block.sync
        def _(sp):
            for i in range(2):
                sp.dma_start(nqt[i][:].bitcast(F32), nqt_dram[0]).then_inc(nqt_loaded[i], 16)
            for i in range(2):
                sp.dma_start(nkv[i][:].bitcast(F32), nkv_dram[0]).then_inc(nkv_loaded[i], 16)
            sp.dma_start(x_res[:], x_t[0]).then_inc(xres_loaded, 16)
            with sp.Fori(0, B - 1) as b:
                sp.wait_ge(q_ready, NP_ * b + QUART)
                sp.dma_start(nqt[0][:].bitcast(F32), nqt_dram[b + 1]).then_inc(nqt_loaded[0], 16)
                sp.wait_ge(pv_ready, NH * b + NH // 2)
                sp.dma_start(nkv[0][:].bitcast(F32), nkv_dram[b + 1]).then_inc(nkv_loaded[0], 16)
                sp.wait_ge(q_ready, NP_ * b + NP_)
                sp.dma_start(nqt[1][:].bitcast(F32), nqt_dram[b + 1]).then_inc(nqt_loaded[1], 16)
                sp.wait_ge(res_added, 4 * b + 2)
                sp.dma_start(x_res[:], x_t[b + 1]).then_inc(xres_loaded, 16)
                sp.wait_ge(pv_ready, NH * b + NH)
                sp.dma_start(nkv[1][:].bitcast(F32), nkv_dram[b + 1]).then_inc(nkv_loaded[1], 16)
                sp.wait_ge(res_added, 4 * b + 4)
                sp.dma_start(res_dram[b], res[:]).then_inc(res_stored, 16)
            sp.wait_ge(res_added, 4 * B)
            sp.dma_start(res_dram[B - 1], res[:]).then_inc(res_stored, 16)
            sp.wait_ge(res_stored, 16 * B + 16)

        @block.gpsimd
        def _(pool):
            def rope_add(b, p):
                pool.wait_ge(q_rope, NP_ * b + p + 1)
                pool.tensor_tensor(qp[:, :, :, KVR:P], qa[:], qb[:], ALU.add).then_inc(q_done, 1)

            def norm(b, g, qt):
                w = (qt + 1) * P
                i = g % 2
                pool.wait_ge(exp_done, unit(b, g, qt) + 1)
                pool.tensor_tensor(rinv[:, i, qt:qt + 1], rowsum[:, i, qt:qt + 1], minus_one[:], ALU.pow)\
                    .then_inc(rinv_ready, 1)
                pool.wait_ge(rinv_ready, unit(b, g, qt) + 1)
                pool.tensor_tensor(prob[:, i, qt, 0:w], prob[:, i, qt, 0:w],
                                   rinv[:, i, qt:qt + 1].to_broadcast([P, w]), ALU.mult).then_inc(normed, 1)

            def latent_lo(b, q):
                pool.wait_ge(lat_hi, NP_ * b + q + 1)
                pool.tensor_tensor(lat_s[1][:, q, :], lat[:, q % 2, :], lat_s[0][:, q, :].bitcast(F32),
                                   ALU.subtract).then_inc(lat_lo, 1)

            def step(bt, g):
                p, par = divmod(g, 2)
                if bt.back(g, 1):
                    norm(*bt.back(g, 1), TT - 1)
                if par == 1 and bt.back(g, 4):
                    b, h = bt.back(g, 4)
                    latent_lo(b, h // 2)
                if g < NH:
                    norm(bt.now, g, 0)
                    norm(bt.now, g, 1)
                if par == 0 and bt.next_pair(p):
                    rope_add(*bt.next_pair(p))
                if g < NH:
                    norm(bt.now, g, 2)

            pool.memset(minus_one[:], -1.0).then_inc(minus_one_ready, 1)
            pool.wait_ge(minus_one_ready, 1)
            rope_add(0, 0)
            pipeline(step)(pool)

        @block.tensor
        def _(pe):
            def queries(b, p, after_piece=None):
                if not (isinstance(b, int) and b == 0 and p == 0):
                    pe.wait_ge(qt_lo, NH * b + 2 * p)
                if p % QUART == 0:
                    pe.wait_ge(nqt_loaded[p // QUART], 16 * b + 16)
                for t in range(TT):
                    if t == 2 and after_piece is not None:
                        pe.wait_ge(res_added, after_piece)
                    mm = product3(pe, q_ps[:, t], [nqt[p // QUART][:, i, t * P:(t + 1) * P] for i in range(2)],
                                  [w[:, 2 * p:2 * p + 2, :] for w in wq_s], t % 2 == 0, t % 2 == 1,
                                  skip_group_check=True)
                mm.then_inc(q_ready, 1)

            def queries_turn(b, p):
                pe.wait_ge(q_abs, NP_ * b + p + 1)
                pe.wait_ge(q_done, NP_ * b + p + 1)
                for i in range(2):
                    for t in range(TT):
                        mm = pe.transpose(qt_ps[i][:, t * P:(t + 1) * P], qp[:, t, i, :], ident[:])
                    mm.then_inc(qt_ready, 1)

            def scores(b, g, qt):
                if qt == 0:
                    pe.wait_ge(qt_lo, NH * b + g + 1)
                if not (isinstance(b, int) and unit(b, g, qt) < 2):
                    pe.wait_ge(exp_done, unit(b, g, qt) - 1)
                w = (qt + 1) * P
                s = s_ps[qt % 2]
                product3(pe, s[:, 0:w], [a[:, qt * P:w] for a in qt_s[g // 2 % 2][g % 2]],
                         [a[:, b, 0:w] for a in kt_s], True, False)
                pe.matmul(s[:, qt * P:w], ident_bf[:], mask_bf[:], start=False, stop=True).then_inc(s_ready, 1)

            def turn(b, g):
                if not (isinstance(b, int) and b == 0 and g == 0):
                    pe.wait_ge(pt_lo, 2 * (NH * b + g))
                for qt in range(TT):
                    pe.wait_ge(normed, unit(b, g, qt) + 1)
                    for kt in range(qt + 1):
                        at = PT_AT[kt] + (qt - kt) * P
                        mm = pe.transpose(pt_ps[:, at:at + P], prob[:, g % 2, qt, kt * P:(kt + 1) * P], ident[:])
                mm.then_inc(pt_ready, 1)

            def values(b, g):
                half = 2 * g // NH
                if g % (NH // 2) == 0:
                    pe.wait_ge(nkv_loaded[half], 16 * b + 16)
                pe.wait_ge(pt_lo, 2 * (NH * b + g) + 2)
                if not (isinstance(b, int) and b == 0 and g == 0):
                    pe.wait_ge(lat_added, NH * b + g)
                for kt in range(TT):
                    w = S - kt * P
                    for i in range(2):
                        mm = pe.matmul(o_ps[:, kt * P:S], nkv[half][:, kt, :], pt_s[i][:, PT_AT[kt]:PT_AT[kt] + w],
                                       start=(kt == 0 and i == 0), stop=(kt == TT - 1 and i == 1))
                mm.then_inc(pv_ready, 1)

            def piece(b, rnd, tp, bank_free):
                bank_free()
                pe.wait_ge(lat_lo, NP_ * b + QUART * (rnd + 1))
                for t in range(2):
                    for q in range(QUART * rnd, QUART * (rnd + 1)):
                        rows = slice((2 * tp + t) * P, (2 * tp + t + 1) * P)
                        mm = product3(pe, acc_ps[:, t, :], [a[:, q, rows] for a in lat_s],
                                      [w[:, q, :] for w in wvo_s], t == 0 and q % QUART == 0,
                                      t == 1 and q % QUART == QUART - 1, skip_group_check=True)
                mm.then_inc(acc_ready, 1)

            def step(bt, g):
                p, par = divmod(g, 2)
                todo = bt.piece(g)
                if todo:
                    piece(*todo, lambda: pe.wait_ge(qt_lo, NH * bt.now + 2 * p + 2))
                if g < NH:
                    scores(bt.now, g, 0)
                if par == 0 and bt.next_pair(p):
                    queries(*bt.next_pair(p), 4 * todo[0] + 2 * todo[1] + todo[2] + 1 if todo else None)
                if par == 1 and bt.next_pair(p):
                    queries_turn(*bt.next_pair(p))
                if g < NH:
                    scores(bt.now, g, 1)
                    scores(bt.now, g, 2)
                if bt.back(g, 2):
                    values(*bt.back(g, 2))
                if bt.back(g, 1):
                    turn(*bt.back(g, 1))
                if g < NH:
                    scores(bt.now, g, 3)

            queries(0, 0)
            queries_turn(0, 0)
            pipeline(step)(pe)
            for tp in range(2):
                piece(B - 1, 1, tp, lambda: pe.wait_ge(res_added, 4 * (B - 1) + 2 + tp))

        @block.scalar
        def _(act):
            def queries_latent(b, p):
                act.wait_ge(q_ready, NP_ * b + p + 1)
                act.activation(qp[:, :, :, 0:KVR], q_ps[:, :, :, 0:KVR], ACT.Copy).then_inc(q_abs, 1)

            def queries_hi(b, p, i):
                act.wait_ge(qt_ready, NH * b + 2 * p + i + 1)
                act.activation(qt_s[p % 2][i][0][:], qt_ps[i], ACT.Copy).then_inc(qt_hi, 1)

            def exps(b, g, qt):
                w = (qt + 1) * P
                i = g % 2
                act.wait_ge(max_ready, unit(b, g, qt) + 1)
                act.activation(prob[:, i, qt, 0:w], s_ps[qt % 2][:, 0:w], ACT.Exp, bias=negmax[:, i, qt:qt + 1],
                               accum_out=rowsum[:, i, qt:qt + 1]).then_inc(exp_done, 1)

            def turned_hi(b, g):
                act.wait_ge(pt_ready, NH * b + g + 1)
                for lo, hi in ((0, 512), (512, PT_W)):
                    act.activation(pt_s[0][:, lo:hi], pt_ps[:, lo:hi], ACT.Copy).then_inc(pt_hi, 1)

            def values_low(b, g):
                act.wait_ge(pv_ready, NH * b + g + 1)
                act.activation(o_low[:], o_ps[KVR:P, :], ACT.Copy).then_inc(o_copied, 1)

            def latent_hi(b, q):
                act.wait_ge(lat_added, NH * b + 2 * q + 2)
                act.activation(lat_s[0][:, q, :], lat[:, q % 2, :], ACT.Copy).then_inc(lat_hi, 1)

            def step(bt, g):
                p, par = divmod(g, 2)
                nxt = bt.next_pair(p)
                if g < NH:
                    exps(bt.now, g, 0)
                if nxt:
                    if par == 0:
                        queries_latent(*nxt)
                    else:
                        queries_hi(*nxt, 0)
                if g < NH:
                    exps(bt.now, g, 1)
                if nxt and par == 1:
                    queries_hi(*nxt, 1)
                if g < NH:
                    exps(bt.now, g, 2)
                if bt.back(g, 2):
                    values_low(*bt.back(g, 2))
                if par == 0 and bt.back(g, 4):
                    b, h = bt.back(g, 4)
                    latent_hi(b, h // 2)
                if bt.back(g, 1):
                    turned_hi(*bt.back(g, 1))
                if g < NH:
                    exps(bt.now, g, 3)

            queries_latent(0, 0)
            queries_hi(0, 0, 0)
            queries_hi(0, 0, 1)
            pipeline(step)(act)

        @block.vector
        def _(dve):
            def queries_rope(b, p):
                dve.wait_ge(q_abs, NP_ * b + p + 1)
                cos = rope_sb[:, 0, :, 0, :].unsqueeze(2).to_broadcast([P, TT, 2, ROPE])
                sin = rope_sb[:, 0, :, 1, :].unsqueeze(2).to_broadcast([P, TT, 2, ROPE])
                dve.tensor_tensor(qa[:], q_ps[:, :, :, KVR:P], cos, ALU.mult)
                dve.tensor_tensor(qb[:, :, :, 0:HALF], q_ps[:, :, :, KVR + HALF:P], sin[:, :, :, 0:HALF], ALU.mult)
                dve.tensor_tensor(qb[:, :, :, HALF:ROPE], q_ps[:, :, :, KVR:KVR + HALF], sin[:, :, :, HALF:ROPE],
                                  ALU.mult).then_inc(q_rope, 1)

            def queries_lo(b, p, i):
                dve.wait_ge(qt_hi, NH * b + 2 * p + i + 1)
                hi, lo = qt_s[p % 2][i]
                dve.tensor_tensor(lo[:], qt_ps[i], hi[:].bitcast(F32), ALU.subtract).then_inc(qt_lo, 1)

            def maxima(b, g, qt):
                i = g % 2
                dve.wait_ge(s_ready, unit(b, g, qt) + 1)
                dve.tensor_reduce(negmax[:, i, qt:qt + 1], s_ps[qt % 2][:, 0:(qt + 1) * P], AX.X, ALU.max,
                                  negate=True).then_inc(max_ready, 1)

            def turned_lo(b, g, i):
                lo, hi = ((0, 512), (512, PT_W))[i]
                dve.wait_ge(pt_hi, 2 * (NH * b + g) + i + 1)
                dve.tensor_tensor(pt_s[1][:, lo:hi], pt_ps[:, lo:hi], pt_s[0][:, lo:hi].bitcast(F32),
                                  ALU.subtract).then_inc(pt_lo, 1)

            def latent_add(b, g):
                q, par = divmod(g, 2)
                if par == 0 and not (isinstance(b, int) and NP_ * b + q < 2):
                    dve.wait_ge(lat_lo, NP_ * b + q - 1)
                dve.wait_ge(o_copied, NH * b + g + 1)
                dve.tensor_tensor(lat[par * KVR:(par + 1) * KVR, q % 2, :], o_ps[0:KVR, :], o_low[:], ALU.add)\
                   .then_inc(lat_added, 1)

            def residual(b, rnd, tp):
                if rnd == 0 and tp == 0:
                    dve.wait_ge(xres_loaded, 16 * b + 16)
                    dve.wait_ge(res_stored, 16 * b + 16)
                if rnd == 1:
                    dve.wait_ge(res_added, 4 * b + tp + 1)
                dve.wait_ge(acc_ready, 4 * b + 2 * rnd + tp + 1)
                tiles = res[:, 2 * tp:2 * tp + 2, :]
                base = x_res[:, 2 * tp:2 * tp + 2, :] if rnd == 0 else tiles
                dve.tensor_tensor(tiles, acc_ps, base, ALU.add).then_inc(res_added, 1)

            def step(bt, g):
                p, par = divmod(g, 2)
                nxt = bt.next_pair(p)
                now = g < NH
                if bt.piece(g):
                    residual(*bt.piece(g))
                if now:
                    maxima(bt.now, g, 0)
                if bt.back(g, 2):
                    turned_lo(*bt.back(g, 2), 1)
                if now:
                    maxima(bt.now, g, 1)
                    maxima(bt.now, g, 2)
                if nxt:
                    if par == 0:
                        queries_rope(*nxt)
                    else:
                        queries_lo(*nxt, 0)
                        queries_lo(*nxt, 1)
                if bt.back(g, 2):
                    latent_add(*bt.back(g, 2))
                if now:
                    maxima(bt.now, g, 3)
                if bt.back(g, 1):
                    turned_lo(*bt.back(g, 1), 0)

            dve.memset(primer[:], 0.0).then_inc(res_stored, 16)
            queries_rope(0, 0)
            queries_lo(0, 0, 0)
            queries_lo(0, 0, 1)
            pipeline(step)(dve)
            for tp in range(2):
                residual(B - 1, 1, tp)


def experts(nc, ctx, sem, wg, wu, wd, xnt_dram, res_dram, comb, ident, ps, out):
    def sb(name, shape, dt=F32):
        return ctx.enter_context(nc.sbuf_tensor(name, shape, dt))

    wg_s = [sb("wg_hi", [P, KC, FALL], F32R), sb("wg_lo", [P, KC, FALL], F32R)]
    wu_s = [sb("wu_hi", [P, KC, FALL], F32R), sb("wu_lo", [P, KC, FALL], F32R)]
    wd_s = [sb("wd_hi", [P, NG * FC + 2, H], F32R), sb("wd_lo", [P, NG * FC + 2, H], F32R)]
    raw_g = sb("raw_g", [P, KC, FG])
    raw_u = sb("raw_u", [P, KC, FG])
    raw_d = sb("raw_d", [P, FC, H])
    xt = [sb("xt_hi_e", [P, KC, S], F32R), sb("xt_lo_e", [P, KC, S], F32R)]
    hidden = sb("hidden", [P, 2, FG])
    weighted = sb("weighted", [P, 2, FG])
    at_s = [[sb(f"at_hi{i}", [P, FC, P], F32R), sb(f"at_lo{i}", [P, FC, P], F32R)] for i in range(2)]
    res = sb("res_e", [P, TT, H])

    g_ps = [ps[:, 0, :], ps[:, 1, :]]
    u_ps = [ps[:, 2, :], ps[:, 3, :]]
    at_ps = [ps[:, 4 + i, 0:FG].rearrange("p (c t) -> p c t", c=FC) for i in range(2)]
    acc_ps = ps[:, 6:8, :].rearrange("p b (t n) -> p (b t) n", t=2)

    raw_loaded = [sem(f"raw_loaded{j}") for j in range(3)]
    w_hi, w_lo = sem("w_hi"), sem("w_lo")
    xt_loaded = [sem(f"xt_loaded{t}") for t in range(TT)]
    res_loaded, out_stored = sem("res_loaded"), sem("out_stored")
    gu_ready, silu_done, act_done = sem("gu_ready"), sem("silu_done"), sem("act_done")
    at_ready, at_hi, at_lo = sem("at_ready"), sem("at_hi"), sem("at_lo")
    out_ready, out_added = sem("out_ready"), sem("out_added")
    U = (NG + 1) * TT
    out_t = out.rearrange("b (t p) h -> b p t h", p=P)

    MAIN = (FG, EG, [P] * FC)
    SHARED = (FSH, FSH // FE, [P, FSH - P])

    def batch(eng, b, group, weights=None):
        if weights is not None:
            weights(0, MAIN)
        for e in range(2):
            if weights is not None:
                weights(e + 1, MAIN)
            group(b, e, MAIN)
        with eng.Fori(2, NG - 1) as e:
            if weights is not None:
                weights(e + 1, MAIN)
            group(b, e, MAIN)
        if weights is not None:
            weights(NG, SHARED)
        group(b, NG - 1, MAIN)
        group(b, NG, SHARED)

    def before(b, e, kind, t, lag):
        if t >= lag:
            return b, e, kind, t - lag
        t += TT - lag
        if isinstance(e, int) and e == 0:
            if isinstance(b, int) and b == 0:
                return None
            return b - 1, NG, SHARED, t
        return b, e - 1, MAIN, t

    def unit(b, e, t):
        return U * b + TT * e + t

    def all_batches(eng, group, weights=None):
        batch(eng, 0, group, weights)
        with eng.Fori(1, B) as b:
            batch(eng, b, group)

    def blocks(kind):
        return [(slice(0, FC), P)] if kind is MAIN else [(slice(0, 1), P), (slice(1, 2), FSH - P)]

    def w_parts(e, kind):
        f, _, rows = kind
        for raw, w, dram in ((raw_g, wg_s, wg), (raw_u, wu_s, wu)):
            yield raw[:, :, 0:f], [a[:, :, bass.ds(e * FG, f)] for a in w], dram[:, :, bass.ds(e * FG, f)]
        n = len(rows)
        yield raw_d[:, 0:n, :], [a[:, bass.ds(e * FC, n), :] for a in wd_s], wd[:, bass.ds(e * FC, n), :]

    with nc.Block() as block:
        @block.sync
        def _(sp):
            def load_tile(b, t):
                for i in range(2):
                    sp.dma_start(xt[i][:, :, t * P:(t + 1) * P].bitcast(F32),
                                 xnt_dram[b][:, i, :, t * P:(t + 1) * P]).then_inc(xt_loaded[t], 16)

            def load_weights(e, kind):
                for j, (raw, _, dram) in enumerate(w_parts(e, kind)):
                    if not (isinstance(e, int) and e == 0):
                        sp.wait_ge(w_lo, 3 * e + j - 2)
                    sp.dma_start(raw, dram).then_inc(raw_loaded[j], 16)

            for t in range(TT):
                load_tile(0, t)
            sp.dma_start(res[:], res_dram[0]).then_inc(res_loaded, 16)
            load_weights(0, MAIN)
            with sp.Fori(1, NG) as e:
                load_weights(e, MAIN)
            load_weights(NG, SHARED)

            def finish(b):
                sp.wait_ge(out_added, 2 * b + 2)
                sp.dma_start(out_t[b], res[:]).then_inc(out_stored, 16)

            with sp.Fori(1, B) as b:
                for t in range(TT):
                    sp.wait_ge(gu_ready, U * b - TT + t + 1)
                    load_tile(b, t)
                finish(b - 1)
                sp.wait_ge(out_stored, 16 * b)
                sp.dma_start(res[:], res_dram[b]).then_inc(res_loaded, 16)
            finish(B - 1)
            sp.wait_ge(out_stored, 16 * B)

        @block.tensor
        def _(pe):
            def turn(b, e, kind, t):
                f, _, rows = kind
                u = unit(b, e, t)
                pe.wait_ge(act_done, u + 1)
                if not (isinstance(b, int) and isinstance(e, int) and u < 2):
                    pe.wait_ge(at_lo, u - 1)
                for c, k in enumerate(rows):
                    mm = pe.transpose(at_ps[t % 2][0:k, c, :], weighted[:, t % 2, c * P:c * P + k], ident[:])
                mm.then_inc(at_ready, 1)

            def down(b, e, kind, t):
                _, _, rows = kind
                pe.wait_ge(at_lo, unit(b, e, t) + 1)
                first = isinstance(e, int) and e == 0
                last = kind is SHARED
                if first and t % 2 == 0 and not (isinstance(b, int) and b == 0):
                    pe.wait_ge(out_added, 2 * b - 1 + t // 2)
                for c, k in enumerate(rows):
                    mm = product3(pe, acc_ps[:, t, :], [a[0:k, c, :] for a in at_s[t % 2]],
                                  [w[0:k, e * FC + c, :] for w in wd_s], first and c == 0 and t % 2 == 0,
                                  last and c == len(rows) - 1, skip_group_check=True)
                if last and t % 2 == 1:
                    mm.then_inc(out_ready, 1)

            def group(b, e, kind):
                f = kind[0]
                for t in range(TT):
                    u = unit(b, e, t)
                    if isinstance(b, int) and t == 0:
                        pe.wait_ge(w_lo, 3 * e + 3)
                    if isinstance(e, int) and e == 0:
                        pe.wait_ge(xt_loaded[t], 32 * b + 32)
                    if not (isinstance(b, int) and isinstance(e, int) and u < 2):
                        pe.wait_ge(act_done, u - 1)
                    for dst, w in ((g_ps, wg_s), (u_ps, wu_s)):
                        for kc in range(KC):
                            mm = product3(pe, dst[t % 2][:, 0:f], [a[:, kc, t * P:(t + 1) * P] for a in xt],
                                          [a[:, kc, bass.ds(e * FG, f)] for a in w], kc == 0, kc == KC - 1)
                    mm.then_inc(gu_ready, 1)
                    if before(b, e, kind, t, 1):
                        turn(*before(b, e, kind, t, 1))
                    if before(b, e, kind, t, 2):
                        down(*before(b, e, kind, t, 2))

            all_batches(pe, group)
            turn(B - 1, NG, SHARED, TT - 1)
            down(B - 1, NG, SHARED, TT - 2)
            down(B - 1, NG, SHARED, TT - 1)

        @block.scalar
        def _(act):
            def weights(e, kind):
                for j, (raw, (hi, _), _) in enumerate(w_parts(e, kind)):
                    act.wait_ge(raw_loaded[j], 16 * e + 16)
                    act.activation(hi, raw, ACT.Copy).then_inc(w_hi, 1)

            def turned_hi(b, e, kind, t):
                act.wait_ge(at_ready, unit(b, e, t) + 1)
                for c, k in blocks(kind):
                    ins = act.activation(at_s[t % 2][0][0:k, c, :], at_ps[t % 2][0:k, c, :], ACT.Copy)
                ins.then_inc(at_hi, 1)

            def group(b, e, kind):
                f = kind[0]
                for t in range(TT):
                    act.wait_ge(gu_ready, unit(b, e, t) + 1)
                    act.activation(hidden[:, t % 2, 0:f], g_ps[t % 2][:, 0:f], ACT.Silu).then_inc(silu_done, 1)
                    if before(b, e, kind, t, 1):
                        turned_hi(*before(b, e, kind, t, 1))

            all_batches(act, group, weights)
            turned_hi(B - 1, NG, SHARED, TT - 1)

        @block.vector
        def _(dve):
            def weights(e, kind):
                for j, (raw, (hi, lo), _) in enumerate(w_parts(e, kind)):
                    dve.wait_ge(w_hi, 3 * e + j + 1)
                    dve.tensor_tensor(lo, raw, hi.bitcast(F32), ALU.subtract).then_inc(w_lo, 1)

            def turned_lo(b, e, kind, t):
                dve.wait_ge(at_hi, unit(b, e, t) + 1)
                for c, k in blocks(kind):
                    ins = dve.tensor_tensor(at_s[t % 2][1][0:k, c, :], at_ps[t % 2][0:k, c, :],
                                            at_s[t % 2][0][0:k, c, :].bitcast(F32), ALU.subtract)
                ins.then_inc(at_lo, 1)

            def add(b, i):
                dve.wait_ge(out_ready, 2 * b + i + 1)
                if i == 0:
                    dve.wait_ge(res_loaded, 16 * b + 16)
                half = res[:, 2 * i:2 * i + 2, :]
                dve.tensor_tensor(half, acc_ps[:, 2 * i:2 * i + 2, :], half, ALU.add).then_inc(out_added, 1)

            def group(b, e, kind):
                _, ne, _ = kind
                for t in range(TT):
                    if isinstance(e, int) and e == 0 and t % 2 == 0 and not (isinstance(b, int) and b == 0):
                        add(b - 1, t // 2)
                    dve.wait_ge(silu_done, unit(b, e, t) + 1)
                    for j in range(ne):
                        cols = slice(j * FE, (j + 1) * FE)
                        ins = dve.scalar_tensor_tensor(weighted[:, t % 2, cols], hidden[:, t % 2, cols],
                                                       comb[:, b, t, bass.ds(e * EG + j, 1)], u_ps[t % 2][:, cols],
                                                       ALU.mult, ALU.mult)
                    ins.then_inc(act_done, 1)
                    if before(b, e, kind, t, 1):
                        turned_lo(*before(b, e, kind, t, 1))

            all_batches(dve, group, weights)
            turned_lo(B - 1, NG, SHARED, TT - 1)
            for i in range(2):
                add(B - 1, i)


def kernel(**inputs):
    import numpy as np
    import concourse.bacc as bacc
    from concourse.bass_utils import run_bass_kernel_spmd

    def arr(name):
        return np.asarray(inputs["L0_" + name])

    def rows(a, n=P):
        return a.reshape(-1, n, a.shape[-1]).transpose(1, 0, 2)

    halves = np.concatenate([np.arange(0, ROPE, 2), np.arange(1, ROPE, 2)])
    wqr = arr("attn_W_dq_rope").reshape(QR, NH, ROPE)[:, :, halves]
    krope = arr("attn_W_krope")[:, halves]
    hid = arr("ffn_wg"), arr("ffn_wu")
    shared = arr("ffn_sg"), arr("ffn_su")
    up = [np.concatenate([w.transpose(1, 0, 2).reshape(H, NE * FE), s], axis=1) for w, s in zip(hid, shared)]
    down = np.concatenate([arr("ffn_wd").reshape(NE * FE, H), arr("ffn_sd"), np.zeros((P - FSH % P, H), np.float32)])

    inv_freq = (np.float32(1.0) / np.float32(10000.0) ** (np.arange(HALF, dtype=np.float32) * np.float32(2.0 / ROPE)))
    ang = np.arange(S, dtype=np.float32)[:, None] * inv_freq.astype(np.float32)[None, :]
    cos, sin = np.cos(ang), np.sin(ang)
    table = np.stack([np.concatenate([cos, cos], 1), np.concatenate([-sin, sin], 1)], 1).astype(np.float32)
    table = np.stack([table, table / np.float32(NH)]).reshape(2, TT, P, 2, ROPE).transpose(2, 0, 1, 3, 4)

    arrays = {
        "x": arr("attn_x"),
        "wc": rows(np.concatenate([arr("attn_W_cq"), arr("attn_W_ckv"), krope, arr("ffn_gate_w")], axis=1)),
        "wqr": wqr,
        "nopeT": arr("attn_W_dq_nope").reshape(QR, NH, NOPE).transpose(2, 1, 0),
        "dkT": arr("attn_W_dk_nope").reshape(KVR, NH, NOPE).transpose(2, 1, 0),
        "dvT": arr("attn_W_dv").reshape(KVR, NH, VD).transpose(2, 1, 0),
        "wo": arr("attn_W_o").reshape(NH, VD, H).transpose(1, 0, 2),
        "qscale": arr("attn_q_scale"),
        "kvscale": arr("attn_kv_scale"),
        "rope": table,
        "wg": rows(up[0]),
        "wu": rows(up[1]),
        "wd": rows(down),
    }
    nc = bacc.Bacc("TRN2", target_bir_lowering=False, num_devices=1)
    args, given = [], {}
    for name, a in arrays.items():
        a = np.ascontiguousarray(a)
        given[f"in_{name}"] = a
        args.append(nc.dram_tensor(f"in_{name}", a.shape, mybir.dt.from_np(a.dtype), kind="ExternalInput").ap())
    args.append(nc.dram_tensor("out", (B, S, H), F32, kind="ExternalOutput").ap())
    build(nc, *args)
    r = run_bass_kernel_spmd(nc, [given], core_ids=[0])
    return r.results[0]["out"]
```

```python
from contextlib import ExitStack

import concourse.bass as bass
from concourse import mybir

F32 = mybir.dt.float32
F32R = mybir.dt.float32r
BF16 = mybir.dt.bfloat16
I32 = mybir.dt.int32
U8 = mybir.dt.uint8
ALU = mybir.AluOpType
ACT = mybir.ActivationFunctionType
AX = mybir.AxisListType

P = 128
B, S, H = 8, 512, 256
TT = S // P
KC = H // P
NH, NOPE, ROPE, VD = 16, 128, 64, 128
HALF = ROPE // 2
QR, KVR = 128, 64
NP_ = NH // 2
NE, FE, FSH, TOPK = 32, 96, 192, 6
HALFK = TOPK // 2
SC = -(-FSH // P)
NT = B * TT
GT = NT // 2
GSORT = GT * TOPK + NE
NTILE = 2 * GSORT
NSTEP = GT
ZCOLS = 2048
CW = QR + KVR + ROPE + NE
CKV, CKR, CG = QR, QR + KVR, QR + KVR + ROPE
SCALE = float((NOPE + ROPE) ** -0.5)
LN_EPS, RMS_EPS = 1e-5, 1e-6
MASKED = -1e30
PT_AT = [0, 512, 1024, 896]
PT_W = 1280


def split(dve, act, hi, lo, src, hi_sem, hi_value, lo_sem, hi_inc=1):
    if act is not None:
        act.activation(hi, src, ACT.Copy).then_inc(hi_sem, hi_inc)
    if dve is not None:
        dve.wait_ge(hi_sem, hi_value)
        dve.tensor_tensor(lo, src, hi.bitcast(F32), ALU.subtract).then_inc(lo_sem, 1)


def product3(pe, out, lhs, rhs, first, last, **kw):
    (lh, ll), (rh, rl) = lhs, rhs
    pe.matmul(out, lh, rh, start=first, stop=False, **kw)
    pe.matmul(out, lh, rl, start=False, stop=False, **kw)
    return pe.matmul(out, ll, rh, start=False, stop=last, **kw)


def build(nc, x, wc, wqr, nopeT, dkT, dvT, wo, qscale, kvscale, rope, route_row, tile_no, wgu, wd, sgu, sd, out):
    with ExitStack() as top:
        def sem(name):
            return top.enter_context(nc.semaphore(name))

        def dram(name, shape, dt=F32):
            return nc.dram_tensor(name, shape, dt, kind="Internal").ap()

        xn_dram = dram("xn_dram", (NT, P, H))
        xnt_dram = dram("xnt_dram", (NT, P, 2, KC, P))
        res_dram = dram("res_dram", (NT, P, H))
        base_dram = dram("base_dram", (NT, P, H))
        nqt_dram = dram("nqt_dram", (B, P, 2, S))
        nkv_dram = dram("nkv_dram", (B, P, TT, 2 * KVR))
        sorted_x = dram("sorted_x", (NTILE * P, H))
        sorted_y = dram("sorted_y", (NTILE * P, H))
        tile_expert = dram("tile_expert", (2, GSORT), U8)

        def sb(name, shape, dt=F32):
            return top.enter_context(nc.sbuf_tensor(name, shape, dt))

        comb = sb("comb", [P, NT, NE])
        slot_of = sb("slot_of", [P, NT, NE])
        slot_top = sb("slot_top", [P, NT, 8])
        slot_no = sb("slot_no", [P, NT, TOPK], I32)
        ident = sb("ident", [P, P])
        ps = top.enter_context(nc.psum_tensor("ps", [P, 8, 512], F32))
        with ExitStack() as ctx:
            attention(nc, ctx, sem, x, wc, wqr, nopeT, dkT, dvT, wo, qscale, kvscale, rope, route_row, tile_no,
                      xn_dram, xnt_dram, res_dram, nqt_dram, nkv_dram, sorted_x, tile_expert,
                      comb, slot_of, slot_top, slot_no, ident, ps)
        experts(nc, sem, wgu, wd, sgu, sd, sorted_x, sorted_y, tile_expert, xnt_dram, res_dram, base_dram,
                comb, slot_of, slot_top, slot_no, ident, ps, out)


def attention(nc, ctx, sem, x, wc, wqr, nopeT, dkT, dvT, wo, qscale, kvscale, rope, route_row, tile_no,
              xn_dram, xnt_dram, res_dram, nqt_dram, nkv_dram, sorted_x, tile_expert,
              comb, slot_of, slot_top, slot_no, ident, ps):
    def sb(name, shape, dt=F32):
        return ctx.enter_context(nc.sbuf_tensor(name, shape, dt))

    wq_s = [sb("wq_hi", [P, NH, P], F32R), sb("wq_lo", [P, NH, P], F32R)]
    wvo_s = [sb("wvo_hi", [P, NP_, H], F32R), sb("wvo_lo", [P, NP_, H], F32R)]
    kt_s = [sb("kt_hi", [P, B, S], F32R), sb("kt_lo", [P, B, S], F32R)]
    rope_sb = sb("rope_sb", [P, 2, TT, 2, ROPE])
    minus_half = sb("minus_half", [P, 2 * TT])
    zeros = sb("zeros", [P, ZCOLS])
    ident_bf = sb("ident_bf", [P, P], BF16)
    mask_bf = sb("mask_bf", [P, P], BF16)

    lctx = ExitStack()
    latents = lctx.enter_context
    wc_s = [latents(nc.sbuf_tensor(name, [P, KC, CW], F32R)) for name in ("wc_hi", "wc_lo")]
    kvs_bc = latents(nc.sbuf_tensor("kvs_bc", [P, KVR], F32))
    route_c = latents(nc.sbuf_tensor("route_c", [P, NSTEP + NE * NE], F32))
    tile_c = latents(nc.sbuf_tensor("tile_c", [P, 1], F32))
    earlier = latents(nc.sbuf_tensor("earlier", [P, P], BF16))
    every = latents(nc.sbuf_tensor("every", [P, P], BF16))

    consts_ready = sem("consts_ready")
    loaded = sem("weights_loaded")
    absorbed = sem("absorbed")
    prep_dve = sem("prep_dve")
    prep_hi = sem("prep_hi")
    prep_lo = sem("prep_lo")

    with ExitStack() as pctx:
        def tb(name, shape, dt=F32):
            return pctx.enter_context(nc.sbuf_tensor(name, shape, dt))

        wc_raw = tb("wc_raw", [P, KC, CW])
        wqr_raw = tb("wqr_raw", [P, NH, ROPE])
        nope_raw = tb("nope_raw", [P, NH, QR])
        dk_raw = tb("dk_raw", [P, NH, KVR])
        dv_raw = tb("dv_raw", [P, NH, KVR])
        wo_raw = tb("wo_raw", [P, NH, H])
        qs = tb("qs", [P, 1])
        wq_f = tb("wq_f", [P, NH, P])
        absorbed_ps = ps[:, 0:2, :].rearrange("p b (h r) -> p (b h) r", r=KVR)
        wvo_ps = ps[:, 2:6, :].rearrange("p b (h n) -> p (b h) n", n=H)

        with nc.Block() as block:
            @block.sync
            def _(sp):
                for dst, src in ((nope_raw, nopeT), (dk_raw, dkT), (wqr_raw, wqr), (dv_raw, dvT),
                                 (wo_raw, wo), (wc_raw, wc), (rope_sb, rope)):
                    sp.dma_start(dst[:], src).then_inc(loaded, 16)
                sp.dma_start(qs[:], qscale.rearrange("(p a) -> p a", a=1)).then_inc(loaded, 16)
                sp.dma_start(kvs_bc[:], kvscale.rearrange("(a r) -> a r", a=1).to_broadcast([P, KVR]))\
                  .then_inc(loaded, 16)
                sp.dma_start(route_c[:], route_row.to_broadcast([P, NSTEP + NE * NE])).then_inc(loaded, 16)
                sp.dma_start(tile_c[:], tile_no).then_inc(loaded, 16)
                sp.wait_ge(loaded, 11 * 16)

            @block.gpsimd
            def _(pool):
                pool.memset(ident[:], 0.0).then_inc(consts_ready, 1)
                pool.memset(ident_bf[:], 0.0).then_inc(consts_ready, 1)
                pool.memset(mask_bf[:], 0.0).then_inc(consts_ready, 1)
                pool.memset(minus_half[:], -0.5).then_inc(consts_ready, 1)
                pool.memset(earlier[:], 1.0).then_inc(consts_ready, 1)
                pool.memset(every[:], 1.0).then_inc(consts_ready, 1)
                pool.memset(zeros[:], 0.0)
                pool.wait_ge(consts_ready, 6)
                pool.affine_select(out=earlier[:], in_=earlier[:], compare_op=ALU.is_gt, fill=0.0, base=0,
                                   pattern=[[1, P]], channel_multiplier=-1).then_inc(consts_ready, 1)
                for m in (ident, ident_bf):
                    pool.affine_select(out=m[:], in_=m[:], compare_op=ALU.not_equal, fill=1.0, base=0,
                                       pattern=[[-1, P]], channel_multiplier=1).then_inc(consts_ready, 1)
                pool.affine_select(out=mask_bf[:], in_=mask_bf[:], compare_op=ALU.is_ge, fill=MASKED, base=0,
                                   pattern=[[-1, P]], channel_multiplier=1).then_inc(consts_ready, 1)

            @block.tensor
            def _(pe):
                pe.wait_ge(loaded, 11 * 16)
                for h in range(NH):
                    mm = pe.matmul(absorbed_ps[:, h, :], nope_raw[:, h, :], dk_raw[:, h, :], start=True, stop=True)
                mm.then_inc(absorbed, 1)
                for h in range(NH):
                    at = (h % 2) * KVR
                    mm = pe.matmul(wvo_ps[at:at + KVR, h // 2, :], dv_raw[:, h, :], wo_raw[:, h, :],
                                   start=True, stop=True)
                mm.then_inc(absorbed, 1)

            @block.scalar
            def _(act):
                act.wait_ge(loaded, 11 * 16)
                split(None, act, wc_s[0][:], None, wc_raw[:], prep_hi, 0, None)
                act.wait_ge(prep_dve, 2)
                split(None, act, wq_s[0][:], None, wq_f[:], prep_hi, 0, None)
                act.wait_ge(absorbed, 2)
                split(None, act, wvo_s[0][:], None, wvo_ps, prep_hi, 0, None)

            @block.vector
            def _(dve):
                dve.wait_ge(loaded, 11 * 16)
                dve.tensor_scalar(wq_f[:, :, KVR:P], wqr_raw[:], qs[:, 0:1], SCALE, ALU.mult, ALU.mult)\
                   .then_inc(prep_dve, 1)
                dve.wait_ge(absorbed, 1)
                dve.tensor_scalar(wq_f[:, :, 0:KVR], absorbed_ps, qs[:, 0:1], SCALE, ALU.mult, ALU.mult)\
                   .then_inc(prep_dve, 1)
                dve.wait_ge(prep_dve, 2)
                split(dve, None, wc_s[0][:], wc_s[1][:], wc_raw[:], prep_hi, 1, prep_lo)
                split(dve, None, wq_s[0][:], wq_s[1][:], wq_f[:], prep_hi, 2, prep_lo)
                dve.wait_ge(absorbed, 2)
                split(dve, None, wvo_s[0][:], wvo_s[1][:], wvo_ps, prep_hi, 3, prep_lo)

    with lctx:
        project(nc, lctx, sem, x, wc_s, kvs_bc, kt_s, rope_sb, minus_half, ident, comb, ps,
                xn_dram, xnt_dram, nqt_dram, nkv_dram, sorted_x, tile_expert, zeros,
                route_c, tile_c, earlier, every, slot_of, slot_top, slot_no)
    heads(nc, ctx, sem, x, wq_s, wvo_s, kt_s, rope_sb, ident, ident_bf, mask_bf, ps,
          nqt_dram, nkv_dram, res_dram, xn_dram, sorted_x, slot_no, zeros)


def project(nc, ctx, sem, x, wc_s, kvs_bc, kt_s, rope_sb, minus_half, ident, comb, ps,
            xn_dram, xnt_dram, nqt_dram, nkv_dram, sorted_x, tile_expert, zeros,
            route_c, tile_c, earlier, every, slot_of, slot_top, slot_no):
    def sb(name, shape, dt=F32):
        return ctx.enter_context(nc.sbuf_tensor(name, shape, dt))

    x_in = sb("x_in", [P, TT, H])
    spare = sb("spare", [P, 8])
    stats = sb("stats", [P, TT, 6])
    mv = sb("mv", [P, TT, 2])
    var = sb("var", [P, TT])
    rstd = sb("rstd", [P, TT])
    xn = sb("xn", [P, TT, H])
    xnt = [sb("xnt_hi", [P, KC, S], F32R), sb("xnt_lo", [P, KC, S], F32R)]
    junk = sb("junk", [P, TT, QR + KVR])
    sumsq = sb("sumsq", [P, 2, TT])
    meansq = sb("meansq", [P, 2, TT])
    rms = sb("rms", [P, 2, TT])
    nq = sb("nq", [P, TT, QR])
    tkv = sb("tkv", [P, TT, KVR])
    kp = sb("kp", [P, TT, P])
    ka = sb("ka", [P, TT, ROPE])
    kb = sb("kb", [P, TT, ROPE])
    nkv = sb("nkv_out", [P, TT, 2 * KVR], F32R)
    nqt = sb("nqt_out", [P, 2, S], F32R)
    expg = sb("expg", [P, TT, NE])
    gate = sb("gate", [P, TT, NE])
    score = sb("score", [P, TT, NE + 2])
    top8 = sb("top8", [P, TT, 8])
    picked = sb("picked", [P, TT, NE + 2])
    chosen = sb("chosen", [P, TT, NE])
    wsum = sb("wsum", [P, TT])
    winv = sb("winv", [P, TT])
    mask = sb("mask", [P, NT, NE], BF16)
    filled = sb("filled", [P, 2 * NE, NSTEP])
    tiles_of = sb("tiles_of", [P, 2, NE])
    upto = sb("upto", [P, 2, NE, NE])
    ends = sb("ends", [P, 2, NE])
    starts = sb("starts", [P, 2, NE])
    first_row = sb("first_row", [P, 2, NE])
    sum_row = sb("sum_row", [P, NT, NE])
    passed = sb("passed", [P, 2, NE])
    owner_f = sb("owner_f", [P, 2])
    owner = sb("owner", [P, 2], U8)

    xt_ps = ps[:, 0:2, :]
    c_ps = ps[:, 2:6, 0:CW]
    nqt_ps, kt_ps = ps[:, 6, :], ps[:, 7, :]

    x_loaded = sem("x_loaded")
    var_ready, rstd_ready, xn_ready = sem("var_ready"), sem("rstd_ready"), sem("xn_ready")
    norm_chain, gate_chain = sem("norm_chain"), sem("gate_chain")
    xt_ready, xt_hi, xt_lo, xt_stored = sem("xt_ready"), sem("xt_hi"), sem("xt_lo"), sem("xt_stored")
    c_ready, squared, logits_exp = sem("c_ready"), sem("squared"), sem("logits_exp")
    meansq_ready, rms_ready = sem("meansq_ready"), sem("rms_ready")
    nq_ready, kp_parts, kp_ready, nkv_ready = sem("nq_ready"), sem("kp_parts"), sem("kp_ready"), sem("nkv_ready")
    nk_ready, nk_hi, nk_lo = sem("nk_ready"), sem("nk_hi"), sem("nk_lo")
    nq_stored, nkv_stored, expg_read = sem("nq_stored"), sem("nkv_stored"), sem("expg_read")
    xn_stored = sem("xn_stored")
    zeros_stored = sem("zeros_stored")
    masked, counted, ranked = sem("masked"), sem("counted"), sem("ranked")
    route_chain, owner_stored = sem("route_chain"), sem("owner_stored")
    rank_ps = ps[:, 0:2, :].rearrange("p g (t e) -> p g t e", e=NE)
    count_ps = ps[:, 2, 0:2 * NE].rearrange("p (g e) -> p g e", e=NE)
    zero_part = sorted_x[0:GSORT * P].rearrange("(i p n) h -> i p (n h)", i=B, p=P)\
                        .rearrange("i p (a f) -> i p a f", f=ZCOLS)

    x_t = x.rearrange("b (t p) h -> b p t h", p=P)
    OWNER_STEP = 7
    GATE_CHAIN = 8

    def all_batches(eng, first, body):
        first()
        with eng.Fori(0, B - 1) as i:
            body(i, i + 1)
        body(B - 1, None)

    with nc.Block() as block:
        @block.sync
        def _(sp):
            def load(i):
                sp.dma_start(x_in[:], x_t[i]).then_inc(x_loaded, 16)

            def store_tokens(i):
                sp.dma_start(xn_dram[bass.ds(TT * i, TT)].rearrange("t p h -> p t h"), xn[:]).then_inc(xn_stored, 16)

            def body(i, j, following):
                for k, done in enumerate((xt_hi, xt_lo)):
                    sp.wait_ge(done, KC * i + KC)
                    for kc in range(KC):
                        sp.dma_start(xnt_dram[bass.ds(TT * i, TT)][:, :, k, kc, :].rearrange("t p c -> p t c"),
                                     xnt[k][:, kc, :].rearrange("p (t c) -> p t c", t=TT).bitcast(F32))\
                            .then_inc(xt_stored, 16)
                if j is not None:
                    sp.wait_ge(xn_ready, TT * j + TT)
                    if following is not None:
                        load(following)
                    store_tokens(j)
                sp.dma_start(zero_part[i], zeros[:].unsqueeze(1).to_broadcast([P, zero_part.shape[2], ZCOLS]))\
                    .then_inc(zeros_stored, 16)
                sp.wait_ge(nkv_ready, i + 1)
                sp.dma_start(nkv_dram[i], nkv[:].bitcast(F32)).then_inc(nkv_stored, 16)
                sp.wait_ge(nk_lo, 2 * i + 2)
                sp.dma_start(nqt_dram[i], nqt[:].bitcast(F32)).then_inc(nq_stored, 16)

            load(0)
            sp.wait_ge(xn_ready, TT)
            load(1)
            store_tokens(0)
            with sp.Fori(0, B - 2) as i:
                body(i, i + 1, i + 2)
            body(B - 2, B - 1, None)
            body(B - 1, None, None)
            sp.wait_ge(route_chain, OWNER_STEP)
            for g in range(2):
                sp.dma_start(tile_expert[g].rearrange("(p a) -> p a", a=1), owner[:, g:g + 1])\
                    .then_inc(owner_stored, 16)
            sp.wait_ge(owner_stored, 32)
            sp.wait_ge(xn_stored, 16 * B)
            sp.wait_ge(zeros_stored, 16 * B)
            sp.wait_ge(xt_stored, 64 * B)
            sp.wait_ge(nkv_stored, 16 * B + 16)
            sp.wait_ge(nq_stored, 16 * B + 16)

        @block.gpsimd
        def _(pool):
            def token_rstd(i):
                pool.wait_ge(var_ready, i + 1)
                pool.tensor_tensor(rstd[:], var[:], minus_half[:, 0:TT], ALU.pow).then_inc(rstd_ready, 1)

            def body(i, j):
                if j is not None:
                    token_rstd(j)
                pool.wait_ge(meansq_ready, 2 * i + 2)
                pool.tensor_tensor(rms[:].rearrange("p k t -> p (k t)"), meansq[:].rearrange("p k t -> p (k t)"),
                                   minus_half[:], ALU.pow).then_inc(rms_ready, 1)

            all_batches(pool, lambda: token_rstd(0), body)

        @block.tensor
        def _(pe):
            def tokens_turn(i):
                pe.wait_ge(xn_ready, TT * i + TT)
                for kc in range(KC):
                    for t in range(TT):
                        mm = pe.transpose(xt_ps[:, kc, t * P:(t + 1) * P], xn[:, t, kc * P:(kc + 1) * P], ident[:])
                    mm.then_inc(xt_ready, 1)

            def body(i, j):
                pe.wait_ge(xt_lo, KC * i + KC)
                for t in range(TT):
                    for kc in range(KC):
                        mm = product3(pe, c_ps[:, t, :], [a[:, kc, t * P:(t + 1) * P] for a in xnt],
                                      [w[:, kc, :] for w in wc_s], kc == 0, kc == KC - 1)
                    mm.then_inc(c_ready, 1)
                if j is not None:
                    tokens_turn(j)
                pe.wait_ge(nq_ready, i + 1)
                for t in range(TT):
                    mm = pe.transpose(nqt_ps[:, t * P:(t + 1) * P], nq[:, t, :], ident[:])
                mm.then_inc(nk_ready, 1)
                pe.wait_ge(kp_ready, i + 1)
                for t in range(TT):
                    mm = pe.transpose(kt_ps[:, t * P:(t + 1) * P], kp[:, t, :], ident[:])
                mm.then_inc(nk_ready, 1)

            all_batches(pe, lambda: tokens_turn(0), body)

            pe.wait_ge(masked, B)
            for g in range(2):
                for t in range(GT):
                    mm = pe.matmul(count_ps[:, g, :], every[:], mask[:, g * GT + t, :], start=g == 0 and t == 0,
                                   stop=g == 1 and t == GT - 1, skip_group_check=True)
            mm.then_inc(counted, 1)
            for g in range(2):
                own = mask[:, g * GT:(g + 1) * GT, :]
                pe.matmul(rank_ps[:, g], earlier[:], own, start=True, stop=False, skip_group_check=True)
                for t in range(GT - 1):
                    mm = pe.matmul(rank_ps[:, g, t + 1:GT, :], every[:],
                                   own[:, t:t + 1, :].to_broadcast([P, GT - 1 - t, NE]),
                                   start=False, stop=t == GT - 2, skip_group_check=True)
            mm.then_inc(ranked, 1)

        @block.scalar
        def _(act):
            def tokens_hi(i, stored):
                for kc in range(KC):
                    act.wait_ge(xt_ready, KC * i + kc + 1)
                    if stored is not None and kc == 0:
                        act.wait_ge(xt_stored, stored)
                    act.activation(xnt[0][:, kc, :], xt_ps[:, kc, :], ACT.Copy).then_inc(xt_hi, 1)

            def body(i, j):
                for t in range(TT):
                    act.wait_ge(c_ready, TT * i + t + 1)
                    for k, (at, w) in enumerate(((0, QR), (CKV, KVR))):
                        act.activation(junk[:, t, at:at + w], c_ps[:, t, at:at + w], ACT.Square,
                                       accum_out=sumsq[:, k, t:t + 1]).then_inc(squared, 1)
                act.wait_ge(expg_read, i + 1)
                act.activation(expg[:], c_ps[:, :, CG:CW], ACT.Exp, scale=-1.0).then_inc(logits_exp, 1)
                if j is not None:
                    tokens_hi(j, 64 * i + 64)
                act.wait_ge(nk_ready, 2 * i + 1)
                act.wait_ge(nq_stored, 16 * i + 16)
                act.activation(nqt[:, 0, :], nqt_ps, ACT.Copy).then_inc(nk_hi, 1)
                act.wait_ge(nk_ready, 2 * i + 2)
                act.activation(kt_s[0][:, i, :], kt_ps, ACT.Copy).then_inc(nk_hi, 1)

            all_batches(act, lambda: tokens_hi(0, None), body)

        @block.vector
        def _(dve):
            def carry_wait(i):
                dve.memset(spare[:, i:i + 1], 0.0)

            def layer_norm_variance(i):
                dve.wait_ge(x_loaded, 16 * i + 16)
                for t in range(TT):
                    ins = dve.bn_stats(stats[:, t, :], x_in[:, t, :])
                ins.then_inc(norm_chain, 1)
                dve.wait_ge(norm_chain, 2 * i + 1)
                carry_wait(0)
                for t in range(TT):
                    ins = dve.bn_aggr(mv[:, t, :], stats[:, t, :])
                ins.then_inc(norm_chain, 1)
                dve.wait_ge(norm_chain, 2 * i + 2)
                dve.tensor_scalar(var[:], mv[:, :, 1], LN_EPS, None, ALU.add).then_inc(var_ready, 1)

            def layer_norm_apply(i):
                dve.wait_ge(rstd_ready, i + 1)
                if not (isinstance(i, int) and i == 0):
                    dve.wait_ge(xn_stored, 16 * i)
                for t in range(TT):
                    dve.tensor_scalar(xn[:, t, :], x_in[:, t, :], mv[:, t, 0:1], rstd[:, t:t + 1],
                                      ALU.subtract, ALU.mult).then_inc(xn_ready, 1)

            def tokens_lo(i):
                for kc in range(KC):
                    dve.wait_ge(xt_hi, KC * i + kc + 1)
                    dve.tensor_tensor(xnt[1][:, kc, :], xt_ps[:, kc, :], xnt[0][:, kc, :].bitcast(F32), ALU.subtract)\
                       .then_inc(xt_lo, 1)

            def latents_rms(i):
                dve.wait_ge(squared, 2 * TT * i + 2 * TT)
                for k, n in enumerate((QR, KVR)):
                    dve.tensor_scalar(meansq[:, k, :], sumsq[:, k, :], 1.0 / n, RMS_EPS, ALU.mult, ALU.add)\
                       .then_inc(meansq_ready, 1)

            def latents(i):
                dve.wait_ge(rms_ready, i + 1)
                dve.wait_ge(logits_exp, i + 1)
                dve.tensor_tensor(nq[:], c_ps[:, :, 0:QR], rms[:, 0, :].unsqueeze(2).to_broadcast([P, TT, QR]),
                                  ALU.mult).then_inc(nq_ready, 1)
                dve.tensor_tensor(tkv[:], c_ps[:, :, CKV:CKR], rms[:, 1, :].unsqueeze(2).to_broadcast([P, TT, KVR]),
                                  ALU.mult)
                dve.tensor_tensor(ka[:], c_ps[:, :, CKR:CG], rope_sb[:, 1, :, 0, :], ALU.mult)
                dve.tensor_tensor(kb[:, :, 0:HALF], c_ps[:, :, CKR + HALF:CG], rope_sb[:, 1, :, 1, 0:HALF], ALU.mult)
                dve.tensor_tensor(kb[:, :, HALF:ROPE], c_ps[:, :, CKR:CKR + HALF], rope_sb[:, 1, :, 1, HALF:ROPE],
                                  ALU.mult).then_inc(kp_parts, 1)
                dve.wait_ge(kp_parts, 2 * i + 1)
                dve.tensor_tensor(kp[:, :, KVR:P], ka[:], kb[:], ALU.add)
                dve.tensor_tensor(kp[:, :, 0:KVR], tkv[:], kvs_bc[:].unsqueeze(1).to_broadcast([P, TT, KVR]),
                                  ALU.mult).then_inc(kp_ready, 1)
                dve.wait_ge(kp_ready, i + 1)
                dve.wait_ge(nkv_stored, 16 * i + 16)
                dve.tensor_copy(nkv[:, :, 0:KVR], kp[:, :, 0:KVR]).then_inc(kp_parts, 1)
                dve.wait_ge(kp_parts, 2 * i + 2)
                dve.tensor_tensor(nkv[:, :, KVR:2 * KVR], kp[:, :, 0:KVR], nkv[:, :, 0:KVR].bitcast(F32),
                                  ALU.subtract).then_inc(nkv_ready, 1)

            def latents_lo(i):
                for k, (hi, lo, src) in enumerate(((nqt[:, 0, :], nqt[:, 1, :], nqt_ps),
                                                   (kt_s[0][:, i, :], kt_s[1][:, i, :], kt_ps))):
                    dve.wait_ge(nk_hi, 2 * i + k + 1)
                    dve.tensor_tensor(lo, src, hi.bitcast(F32), ALU.subtract).then_inc(nk_lo, 1)

            def gate_chained(i, step, ins):
                ins.then_inc(gate_chain, 1)
                dve.wait_ge(gate_chain, 1 + GATE_CHAIN * i + step)

            def gates_pick(i):
                dve.tensor_scalar(gate[:], expg[:], 1.0, None, ALU.add).then_inc(expg_read, 1)
                dve.wait_ge(expg_read, i + 2)
                gate_chained(i, 1, dve.reciprocal(score[:, :, 0:NE], gate[:]))
                carry_wait(1)
                for t in range(TT):
                    ins = dve.max(top8[:, t, :], score[:, t, :])
                gate_chained(i, 2, ins)
                gate_chained(i, 3, dve.memset(top8[:, :, TOPK:8], -1.0))
                carry_wait(2)
                for t in range(TT):
                    ins = dve.match_replace(picked[:, t, :], top8[:, t, :], score[:, t, :], -2.0)
                ins.then_inc(gate_chain, 1)

            def gates_share(i):
                dve.wait_ge(gate_chain, 1 + GATE_CHAIN * i + 4)
                dve.tensor_scalar(mask[:, bass.ds(TT * i, TT), :], picked[:, :, 0:NE], -2.0, None, ALU.is_equal)\
                   .then_inc(masked, 1)
                for t in range(TT):
                    ins = dve.scalar_tensor_tensor(chosen[:, t, :], picked[:, t, 0:NE], -2.0, score[:, t, 0:NE],
                                                   ALU.is_equal, ALU.mult, accum_out=wsum[:, t:t + 1])
                gate_chained(i, 5, ins)
                gate_chained(i, 6, dve.tensor_scalar(winv[:], wsum[:], 1e-20, None, ALU.add))
                gate_chained(i, 7, dve.reciprocal(wsum[:], winv[:]))
                gate_chained(i, GATE_CHAIN, dve.tensor_tensor(comb[:, bass.ds(TT * i, TT), :], chosen[:],
                                                              wsum[:].unsqueeze(2).to_broadcast([P, TT, NE]),
                                                              ALU.mult))

            def start():
                dve.memset(score[:, :, NE:NE + 2], -1.0).then_inc(gate_chain, 1)
                dve.memset(spare[:, 3:4], 0.0).then_inc(nq_stored, 16)
                dve.memset(spare[:, 4:5], 0.0).then_inc(nkv_stored, 16)
                dve.memset(spare[:, 5:6], 0.0).then_inc(expg_read, 1)
                dve.wait_ge(gate_chain, 1)
                layer_norm_variance(0)
                layer_norm_apply(0)
                tokens_lo(0)

            def body(i, j, last):
                if j is not None:
                    layer_norm_variance(j)
                if last is not None:
                    gates_pick(last)
                if j is not None:
                    layer_norm_apply(j)
                latents_rms(i)
                if last is not None:
                    gates_share(last)
                latents(i)
                if j is not None:
                    tokens_lo(j)
                latents_lo(i)

            def routes():
                steps = [0]

                def chain(ins):
                    steps[0] += 1
                    ins.then_inc(route_chain, 1)
                    dve.wait_ge(route_chain, steps[0])

                dve.wait_ge(counted, 1)
                chain(dve.tensor_tensor(filled[:], count_ps.rearrange("p g e -> p (g e)").unsqueeze(2)
                                        .to_broadcast([P, 2 * NE, NSTEP]),
                                        route_c[:, 0:NSTEP].unsqueeze(1).to_broadcast([P, 2 * NE, NSTEP]), ALU.is_gt))
                chain(dve.tensor_reduce(tiles_of[:].rearrange("p g e -> p (g e)"), filled[:], AX.X, ALU.add))
                no_later = route_c[:, NSTEP:].rearrange("p (e f) -> p e f", f=NE)
                for g in range(2):
                    ins = dve.tensor_tensor(upto[:, g], tiles_of[:, g, :].unsqueeze(1).to_broadcast([P, NE, NE]),
                                            no_later, ALU.mult)
                chain(ins)
                chain(dve.tensor_reduce(ends[:], upto[:], AX.X, ALU.add))
                chain(dve.tensor_scalar(passed[:], ends[:], tile_c[:, 0:1], None, ALU.is_le))
                chain(dve.tensor_reduce(owner_f[:], passed[:], AX.X, ALU.add))
                chain(dve.tensor_scalar(owner[:], owner_f[:], float(NE - 1), None, ALU.min))
                assert steps[0] == OWNER_STEP, steps[0]
                chain(dve.tensor_tensor(starts[:], ends[:], tiles_of[:], ALU.subtract))
                for g in range(2):
                    ins = dve.tensor_scalar(first_row[:, g, :], starts[:, g, :], float(P), float(g * GSORT * P + 1),
                                            ALU.mult, ALU.add)
                chain(ins)
                dve.wait_ge(ranked, 1)
                for g in range(2):
                    ins = dve.tensor_tensor(sum_row[:, g * GT:(g + 1) * GT, :], rank_ps[:, g],
                                            first_row[:, g, :].unsqueeze(1).to_broadcast([P, GT, NE]), ALU.add)
                chain(ins)
                chain(dve.tensor_tensor(slot_of[:], sum_row[:], mask[:], ALU.mult))
                for t in range(NT):
                    ins = dve.max(slot_top[:, t, :], slot_of[:, t, :])
                chain(ins)
                dve.tensor_scalar(slot_no[:], slot_top[:, :, 0:TOPK], -1.0, None, ALU.add)

            start()
            body(0, 1, None)
            with dve.Fori(1, B - 1) as i:
                body(i, i + 1, i - 1)
            body(B - 1, None, B - 2)
            gates_pick(B - 1)
            gates_share(B - 1)
            routes()


def heads(nc, ctx, sem, x, wq_s, wvo_s, kt_s, rope_sb, ident, ident_bf, mask_bf, ps,
          nqt_dram, nkv_dram, res_dram, xn_dram, sorted_x, slot_no, zeros):
    def sb(name, shape, dt=F32):
        return ctx.enter_context(nc.sbuf_tensor(name, shape, dt))

    QUART = NP_ // 2
    x_res = sb("x_res", [P, TT, H])
    res = sb("res", [P, TT, H])
    primer = sb("primer", [P, 1])
    xn_row = [sb(f"xn_row{i}", [P, H]) for i in range(2)]
    row_no = [sb(f"row_no{i}", [P, TOPK], I32) for i in range(2)]
    carrier = sb("carrier", [P, 2])
    nqt = [sb(f"nqt{i}", [P, 2, S], F32R) for i in range(2)]
    nkv = [sb(f"nkv{i}", [P, TT, 2 * KVR], F32R) for i in range(2)]
    qp = sb("qp", [P, TT, 2, P])
    qa = sb("qa", [P, TT, 2, ROPE])
    qb = sb("qb", [P, TT, 2, ROPE])
    qt_s = [[[sb(f"qt{i}{j}_{k}", [P, S], F32R) for k in ("hi", "lo")] for j in range(2)] for i in range(2)]
    negmax = sb("negmax", [P, 2, TT])
    rowsum = sb("rowsum", [P, 2, TT])
    rinv = sb("rinv", [P, 2, TT])
    minus_one = sb("minus_one", [P, 1])
    prob = sb("prob", [P, 2, TT, S])
    pt_s = [sb("pt_hi", [P, PT_W], F32R), sb("pt_lo", [P, PT_W], F32R)]
    o_low = sb("o_low", [KVR, S])
    lat = sb("lat", [P, 2, S])
    lat_s = [sb("lat_hi", [P, NP_, S], F32R), sb("lat_lo", [P, NP_, S], F32R)]

    q_ps = ps[:, 0:2, :].rearrange("p b (t h c) -> p (b t) h c", t=2, h=2)
    qt_ps = [ps[:, 0, :], ps[:, 1, :]]
    s_ps = [ps[:, 2, :], ps[:, 3, :]]
    pt_ps = ps[:, 4:7, :].rearrange("p b n -> p (b n)")
    o_ps = ps[:, 7, :]
    acc_ps = ps[:, 1, :].rearrange("p (t n) -> p t n", t=2)

    nqt_loaded = [sem(f"nqt_loaded{i}") for i in range(2)]
    nkv_loaded = [sem(f"nkv_loaded{i}") for i in range(2)]
    xres_loaded = sem("xres_loaded")
    q_ready, q_abs, q_rope, q_done = sem("q_ready"), sem("q_abs"), sem("q_rope"), sem("q_done")
    qt_ready, qt_hi, qt_lo = sem("qt_ready"), sem("qt_hi"), sem("qt_lo")
    s_ready, max_ready, exp_done = sem("s_ready"), sem("max_ready"), sem("exp_done")
    minus_one_ready, rinv_pool, rinv_dve = sem("minus_one_ready"), sem("rinv_pool"), sem("rinv_dve")
    normed_dve, normed_pool = sem("normed_dve"), sem("normed_pool")
    pt_ready, pt_hi, pt_lo = sem("pt_ready"), sem("pt_hi"), sem("pt_lo")
    pv_ready, o_copied, lat_added = sem("pv_ready"), sem("o_copied"), sem("lat_added")
    lat_hi, lat_lo = sem("lat_hi"), sem("lat_lo")
    acc_ready, res_added = sem("acc_ready"), sem("res_added")
    res_stored = sem("res_stored")
    scattered = [sem(f"scattered{i}") for i in range(2)]
    row_loaded = [sem(f"row_loaded{i}") for i in range(2)]
    row_no_ready = sem("row_no_ready")

    x_t = x.rearrange("b (t p) h -> b p t h", p=P)
    zero_part = sorted_x[GSORT * P:].rearrange("(i p n) h -> i p (n h)", i=B, p=P)\
                        .rearrange("i p (a f) -> i p a f", f=ZCOLS)
    zeros_stored = sem("zeros2_stored")
    TAIL = 4

    class Batches:
        def __init__(self, now, last, following):
            self.now, self.last, self.following = now, last, following

        def back(self, g, lag):
            if 0 <= g - lag < NH:
                return self.now, g - lag
            return None if g >= NH + lag or self.last is None else (self.last, g - lag + NH)

        def next_pair(self, p):
            if p + 1 < NP_:
                return self.now, p + 1
            return None if self.following is None or p >= NP_ else (self.following, 0)

        def piece(self, g):
            p, par = divmod(g, 2)
            if par == 0 and p in (QUART - 2, QUART - 1) and self.last is not None:
                return self.last, 1, p - QUART + 2
            if par == 0 and p in (NP_ - 2, NP_ - 1):
                return self.now, 0, p - NP_ + 2
            return None

    def pipeline(step, between_groups=None):
        def run(eng):
            def batches(first, last):
                with eng.Fori(first, last) as b:
                    for g in range(NH // 2, NH):
                        step(Batches(b, None, b + 1), g)
                    for g in range(NH // 2):
                        step(Batches(b + 1, b, None), g)

            for g in range(NH // 2):
                step(Batches(0, None, 1), g)
            if between_groups is None:
                batches(0, B - 1)
            else:
                batches(0, B // 2 - 1)
                between_groups()
                batches(B // 2 - 1, B - 1)
            for g in range(NH // 2, NH + TAIL):
                step(Batches(B - 1, None, None), g)
        return run

    def unit(b, g, qt=0):
        return TT * (NH * b + g) + qt

    with nc.Block() as block:
        @block.sync
        def _(sp):
            for i in range(2):
                sp.dma_start(nqt[i][:].bitcast(F32), nqt_dram[0]).then_inc(nqt_loaded[i], 16)
            for i in range(2):
                sp.dma_start(nkv[i][:].bitcast(F32), nkv_dram[0]).then_inc(nkv_loaded[i], 16)
            sp.dma_start(x_res[:], x_t[0]).then_inc(xres_loaded, 16)

            def fill(i):
                sp.dma_start(zero_part[i], zeros[:].unsqueeze(1).to_broadcast([P, zero_part.shape[2], ZCOLS]))\
                    .then_inc(zeros_stored, 16)

            def during(b):
                sp.wait_ge(q_ready, NP_ * b + QUART)
                sp.dma_start(nqt[0][:].bitcast(F32), nqt_dram[b + 1]).then_inc(nqt_loaded[0], 16)
                sp.wait_ge(pv_ready, NH * b + NH // 2)
                sp.dma_start(nkv[0][:].bitcast(F32), nkv_dram[b + 1]).then_inc(nkv_loaded[0], 16)
                sp.wait_ge(q_ready, NP_ * b + NP_)
                sp.dma_start(nqt[1][:].bitcast(F32), nqt_dram[b + 1]).then_inc(nqt_loaded[1], 16)
                sp.wait_ge(res_added, 4 * b + 2)
                sp.dma_start(x_res[:], x_t[b + 1]).then_inc(xres_loaded, 16)
                sp.wait_ge(pv_ready, NH * b + NH)
                sp.dma_start(nkv[1][:].bitcast(F32), nkv_dram[b + 1]).then_inc(nkv_loaded[1], 16)
                sp.wait_ge(res_added, 4 * b + 4)
                sp.dma_start(res_dram[bass.ds(TT * b, TT)].rearrange("t p h -> p t h"), res[:]).then_inc(res_stored, 16)
            fill(0)
            fill(1)
            with sp.Fori(0, B // 2 - 1) as b:
                for half in range(2):
                    fill(2 * b + (2 + half))
                during(b)
            with sp.Fori(B // 2 - 1, B - 1) as b:
                during(b)
            sp.wait_ge(zeros_stored, 16 * B)
            sp.wait_ge(res_added, 4 * B)
            sp.dma_start(res_dram[TT * (B - 1):TT * B].rearrange("t p h -> p t h"), res[:]).then_inc(res_stored, 16)
            sp.wait_ge(res_stored, 16 * B + 16)

        @block.gpsimd
        def _(pool):
            def rope_add(b, p):
                pool.wait_ge(q_rope, NP_ * b + p + 1)
                pool.tensor_tensor(qp[:, :, :, KVR:P], qa[:], qb[:], ALU.add).then_inc(q_done, 1)

            def norm(b, g, qt):
                w = (qt + 1) * P
                i = g % 2
                pool.wait_ge(exp_done, unit(b, g, qt) + 1)
                pool.tensor_tensor(rinv[:, i, qt:qt + 1], rowsum[:, i, qt:qt + 1], minus_one[:], ALU.pow)\
                    .then_inc(rinv_pool, 1)
                pool.wait_ge(rinv_pool, 2 * (NH * b + g) + qt - 1)
                pool.tensor_tensor(prob[:, i, qt, 0:w], prob[:, i, qt, 0:w],
                                   rinv[:, i, qt:qt + 1].to_broadcast([P, w]), ALU.mult).then_inc(normed_pool, 1)

            def scatter(b, q, half):
                par, before = q % 2, TT // 2 * b + q // 2
                if half == 0:
                    pool.wait_ge(row_loaded[par], 16 * before + 16)
                    pool.wait_ge(row_no_ready, TT * b + q + 1)
                    pool.tensor_tensor(carrier[:, par:par + 1], minus_one[:], minus_one[:], ALU.mult)
                for k in range(HALFK * half, HALFK * (half + 1)):
                    pool.indirect_dma_start(sorted_x, bass.IndirectOffsetOnAxis(ap=row_no[par][:, k:k + 1], axis=0),
                                            xn_row[par][:], None).then_inc(scattered[par], 16)

            def latent_lo(b, q):
                pool.wait_ge(lat_hi, NP_ * b + q + 1)
                pool.tensor_tensor(lat_s[1][:, q, :], lat[:, q % 2, :], lat_s[0][:, q, :].bitcast(F32),
                                   ALU.subtract).then_inc(lat_lo, 1)

            def step(bt, g):
                p, par = divmod(g, 2)
                if bt.back(g, 1):
                    norm(*bt.back(g, 1), TT - 1)
                if par == 1 and bt.back(g, 4):
                    b, h = bt.back(g, 4)
                    latent_lo(b, h // 2)
                if g < NH and par == 1:
                    scatter(bt.now, g // 4, g // 2 % 2)
                if par == 0 and bt.next_pair(p):
                    rope_add(*bt.next_pair(p))
                if g < NH:
                    norm(bt.now, g, 2)

            pool.memset(minus_one[:], -1.0).then_inc(minus_one_ready, 1)
            pool.wait_ge(minus_one_ready, 1)
            rope_add(0, 0)
            pipeline(step, lambda: pool.wait_ge(zeros_stored, 16 * B))(pool)
            for par in range(2):
                pool.wait_ge(scattered[par], 16 * TOPK * (NT // 2))

        @block.tensor
        def _(pe):
            def queries(b, p, after_piece=None):
                if not (isinstance(b, int) and b == 0 and p == 0):
                    pe.wait_ge(qt_lo, NH * b + 2 * p)
                if p % QUART == 0:
                    pe.wait_ge(nqt_loaded[p // QUART], 16 * b + 16)
                for t in range(TT):
                    if t == 2 and after_piece is not None:
                        pe.wait_ge(res_added, after_piece)
                    mm = product3(pe, q_ps[:, t], [nqt[p // QUART][:, i, t * P:(t + 1) * P] for i in range(2)],
                                  [w[:, 2 * p:2 * p + 2, :] for w in wq_s], t % 2 == 0, t % 2 == 1,
                                  skip_group_check=True)
                mm.then_inc(q_ready, 1)

            def queries_turn(b, p):
                pe.wait_ge(q_abs, NP_ * b + p + 1)
                pe.wait_ge(q_done, NP_ * b + p + 1)
                for i in range(2):
                    for t in range(TT):
                        mm = pe.transpose(qt_ps[i][:, t * P:(t + 1) * P], qp[:, t, i, :], ident[:])
                    mm.then_inc(qt_ready, 1)

            def scores(b, g, qt):
                if qt == 0:
                    pe.wait_ge(qt_lo, NH * b + g + 1)
                if not (isinstance(b, int) and unit(b, g, qt) < 2):
                    pe.wait_ge(exp_done, unit(b, g, qt) - 1)
                w = (qt + 1) * P
                s = s_ps[qt % 2]
                product3(pe, s[:, 0:w], [a[:, qt * P:w] for a in qt_s[g // 2 % 2][g % 2]],
                         [a[:, b, 0:w] for a in kt_s], True, False)
                pe.matmul(s[:, qt * P:w], ident_bf[:], mask_bf[:], start=False, stop=True).then_inc(s_ready, 1)

            def turn(b, g):
                if not (isinstance(b, int) and b == 0 and g == 0):
                    pe.wait_ge(pt_lo, 2 * (NH * b + g))
                for qt in range(TT):
                    pe.wait_ge((normed_dve, normed_pool)[qt // 2], 2 * (NH * b + g) + qt % 2 + 1)
                    for kt in range(qt + 1):
                        at = PT_AT[kt] + (qt - kt) * P
                        mm = pe.transpose(pt_ps[:, at:at + P], prob[:, g % 2, qt, kt * P:(kt + 1) * P], ident[:])
                mm.then_inc(pt_ready, 1)

            def values(b, g):
                half = 2 * g // NH
                if g % (NH // 2) == 0:
                    pe.wait_ge(nkv_loaded[half], 16 * b + 16)
                pe.wait_ge(pt_lo, 2 * (NH * b + g) + 2)
                if not (isinstance(b, int) and b == 0 and g == 0):
                    pe.wait_ge(lat_added, NH * b + g)
                for kt in range(TT):
                    w = S - kt * P
                    for i in range(2):
                        mm = pe.matmul(o_ps[:, kt * P:S], nkv[half][:, kt, :], pt_s[i][:, PT_AT[kt]:PT_AT[kt] + w],
                                       start=(kt == 0 and i == 0), stop=(kt == TT - 1 and i == 1))
                mm.then_inc(pv_ready, 1)

            def piece(b, rnd, tp, bank_free):
                bank_free()
                pe.wait_ge(lat_lo, NP_ * b + QUART * (rnd + 1))
                for t in range(2):
                    for q in range(QUART * rnd, QUART * (rnd + 1)):
                        rows = slice((2 * tp + t) * P, (2 * tp + t + 1) * P)
                        mm = product3(pe, acc_ps[:, t, :], [a[:, q, rows] for a in lat_s],
                                      [w[:, q, :] for w in wvo_s], t == 0 and q % QUART == 0,
                                      t == 1 and q % QUART == QUART - 1, skip_group_check=True)
                mm.then_inc(acc_ready, 1)

            def step(bt, g):
                p, par = divmod(g, 2)
                todo = bt.piece(g)
                if todo:
                    piece(*todo, lambda: pe.wait_ge(qt_lo, NH * bt.now + 2 * p + 2))
                if g < NH:
                    scores(bt.now, g, 0)
                if par == 0 and bt.next_pair(p):
                    queries(*bt.next_pair(p), 4 * todo[0] + 2 * todo[1] + todo[2] + 1 if todo else None)
                if par == 1 and bt.next_pair(p):
                    queries_turn(*bt.next_pair(p))
                if g < NH:
                    scores(bt.now, g, 1)
                    scores(bt.now, g, 2)
                if bt.back(g, 2):
                    values(*bt.back(g, 2))
                if bt.back(g, 1):
                    turn(*bt.back(g, 1))
                if g < NH:
                    scores(bt.now, g, 3)

            queries(0, 0)
            queries_turn(0, 0)
            pipeline(step)(pe)
            for tp in range(2):
                piece(B - 1, 1, tp, lambda: pe.wait_ge(res_added, 4 * (B - 1) + 2 + tp))

        @block.scalar
        def _(act):
            def queries_latent(b, p):
                act.wait_ge(q_ready, NP_ * b + p + 1)
                act.activation(qp[:, :, :, 0:KVR], q_ps[:, :, :, 0:KVR], ACT.Copy).then_inc(q_abs, 1)

            def queries_hi(b, p, i):
                act.wait_ge(qt_ready, NH * b + 2 * p + i + 1)
                act.activation(qt_s[p % 2][i][0][:], qt_ps[i], ACT.Copy).then_inc(qt_hi, 1)

            def exps(b, g, qt):
                w = (qt + 1) * P
                i = g % 2
                act.wait_ge(max_ready, unit(b, g, qt) + 1)
                act.activation(prob[:, i, qt, 0:w], s_ps[qt % 2][:, 0:w], ACT.Exp, bias=negmax[:, i, qt:qt + 1],
                               accum_out=rowsum[:, i, qt:qt + 1]).then_inc(exp_done, 1)

            def turned_hi(b, g):
                act.wait_ge(pt_ready, NH * b + g + 1)
                for lo, hi in ((0, 512), (512, PT_W)):
                    act.activation(pt_s[0][:, lo:hi], pt_ps[:, lo:hi], ACT.Copy).then_inc(pt_hi, 1)

            def values_low(b, g):
                act.wait_ge(pv_ready, NH * b + g + 1)
                act.activation(o_low[:], o_ps[KVR:P, :], ACT.Copy).then_inc(o_copied, 1)

            def latent_hi(b, q):
                act.wait_ge(lat_added, NH * b + 2 * q + 2)
                act.activation(lat_s[0][:, q, :], lat[:, q % 2, :], ACT.Copy).then_inc(lat_hi, 1)

            def step(bt, g):
                p, par = divmod(g, 2)
                nxt = bt.next_pair(p)
                if g < NH and g % 4 == 0:
                    q = g // 4
                    if not (isinstance(bt.now, int) and bt.now == 0 and q < 2):
                        act.wait_ge(scattered[q % 2], 16 * TOPK * (TT // 2 * bt.now + q // 2))
                    act.dma_start(xn_row[q % 2][:], xn_dram[TT * bt.now + q]).then_inc(row_loaded[q % 2], 16)
                if g < NH:
                    exps(bt.now, g, 0)
                if nxt:
                    if par == 0:
                        queries_latent(*nxt)
                    else:
                        queries_hi(*nxt, 0)
                if g < NH:
                    exps(bt.now, g, 1)
                if nxt and par == 1:
                    queries_hi(*nxt, 1)
                if g < NH:
                    exps(bt.now, g, 2)
                if bt.back(g, 2):
                    values_low(*bt.back(g, 2))
                if par == 0 and bt.back(g, 4):
                    b, h = bt.back(g, 4)
                    latent_hi(b, h // 2)
                if bt.back(g, 1):
                    turned_hi(*bt.back(g, 1))
                if g < NH:
                    exps(bt.now, g, 3)

            queries_latent(0, 0)
            queries_hi(0, 0, 0)
            queries_hi(0, 0, 1)
            pipeline(step)(act)

        @block.vector
        def _(dve):
            def queries_rope(b, p):
                dve.wait_ge(q_abs, NP_ * b + p + 1)
                cos = rope_sb[:, 0, :, 0, :].unsqueeze(2).to_broadcast([P, TT, 2, ROPE])
                sin = rope_sb[:, 0, :, 1, :].unsqueeze(2).to_broadcast([P, TT, 2, ROPE])
                dve.tensor_tensor(qa[:], q_ps[:, :, :, KVR:P], cos, ALU.mult)
                dve.tensor_tensor(qb[:, :, :, 0:HALF], q_ps[:, :, :, KVR + HALF:P], sin[:, :, :, 0:HALF], ALU.mult)
                dve.tensor_tensor(qb[:, :, :, HALF:ROPE], q_ps[:, :, :, KVR:KVR + HALF], sin[:, :, :, HALF:ROPE],
                                  ALU.mult).then_inc(q_rope, 1)

            def queries_lo(b, p, i):
                dve.wait_ge(qt_hi, NH * b + 2 * p + i + 1)
                hi, lo = qt_s[p % 2][i]
                dve.tensor_tensor(lo[:], qt_ps[i], hi[:].bitcast(F32), ALU.subtract).then_inc(qt_lo, 1)

            def maxima(b, g, qt):
                i = g % 2
                dve.wait_ge(s_ready, unit(b, g, qt) + 1)
                dve.tensor_reduce(negmax[:, i, qt:qt + 1], s_ps[qt % 2][:, 0:(qt + 1) * P], AX.X, ALU.max,
                                  negate=True).then_inc(max_ready, 1)

            def norm(b, g, qt):
                w = (qt + 1) * P
                i = g % 2
                dve.wait_ge(exp_done, unit(b, g, qt) + 1)
                dve.reciprocal(rinv[:, i, qt:qt + 1], rowsum[:, i, qt:qt + 1]).then_inc(rinv_dve, 1)
                dve.wait_ge(rinv_dve, 2 * (NH * b + g) + qt + 1)
                dve.tensor_scalar(prob[:, i, qt, 0:w], prob[:, i, qt, 0:w], rinv[:, i, qt:qt + 1], None, ALU.mult)\
                   .then_inc(normed_dve, 1)

            def turned_lo(b, g, i):
                lo, hi = ((0, 512), (512, PT_W))[i]
                dve.wait_ge(pt_hi, 2 * (NH * b + g) + i + 1)
                dve.tensor_tensor(pt_s[1][:, lo:hi], pt_ps[:, lo:hi], pt_s[0][:, lo:hi].bitcast(F32),
                                  ALU.subtract).then_inc(pt_lo, 1)

            def latent_add(b, g):
                q, par = divmod(g, 2)
                if par == 0 and not (isinstance(b, int) and NP_ * b + q < 2):
                    dve.wait_ge(lat_lo, NP_ * b + q - 1)
                dve.wait_ge(o_copied, NH * b + g + 1)
                dve.tensor_tensor(lat[par * KVR:(par + 1) * KVR, q % 2, :], o_ps[0:KVR, :], o_low[:], ALU.add)\
                   .then_inc(lat_added, 1)

            def residual(b, rnd, tp):
                if rnd == 0 and tp == 0:
                    dve.wait_ge(xres_loaded, 16 * b + 16)
                    dve.wait_ge(res_stored, 16 * b + 16)
                if rnd == 1:
                    dve.wait_ge(res_added, 4 * b + tp + 1)
                dve.wait_ge(acc_ready, 4 * b + 2 * rnd + tp + 1)
                tiles = res[:, 2 * tp:2 * tp + 2, :]
                base = x_res[:, 2 * tp:2 * tp + 2, :] if rnd == 0 else tiles
                dve.tensor_tensor(tiles, acc_ps, base, ALU.add).then_inc(res_added, 1)

            def step(bt, g):
                p, par = divmod(g, 2)
                nxt = bt.next_pair(p)
                now = g < NH
                if bt.piece(g):
                    residual(*bt.piece(g))
                if now and g % 4 == 0:
                    q = g // 4
                    if not (isinstance(bt.now, int) and bt.now == 0 and q < 2):
                        dve.wait_ge(scattered[q % 2], 16 * TOPK * (TT // 2 * bt.now + q // 2))
                    dve.tensor_copy(row_no[q % 2][:], slot_no[:, TT * bt.now + q, :]).then_inc(row_no_ready, 1)
                if now:
                    maxima(bt.now, g, 0)
                if bt.back(g, 2):
                    turned_lo(*bt.back(g, 2), 1)
                if now:
                    maxima(bt.now, g, 1)
                    maxima(bt.now, g, 2)
                if nxt:
                    if par == 0:
                        queries_rope(*nxt)
                    else:
                        queries_lo(*nxt, 0)
                        queries_lo(*nxt, 1)
                if now:
                    norm(bt.now, g, 0)
                    norm(bt.now, g, 1)
                if bt.back(g, 2):
                    latent_add(*bt.back(g, 2))
                if now:
                    maxima(bt.now, g, 3)
                if bt.back(g, 1):
                    turned_lo(*bt.back(g, 1), 0)

            dve.memset(primer[:], 0.0).then_inc(res_stored, 16)
            queries_rope(0, 0)
            queries_lo(0, 0, 0)
            queries_lo(0, 0, 1)
            pipeline(step)(dve)
            for tp in range(2):
                residual(B - 1, 1, tp)


def experts(nc, sem, wgu, wd, sgu, sd, sorted_x, sorted_y, tile_expert, xnt_dram, res_dram, base_dram,
            comb, slot_of, slot_top, slot_no, ident, ps, out):
    shared_sems = {name: sem(name) for name in (
        "sh_w_loaded", "sh_w_hi", "sh_w_lo", "sh_gu_ready", "sh_silu", "sh_act", "sh_at_ready", "sh_at_hi",
        "sh_at_lo", "sh_out_ready", "sh_added")}
    for name in ("sh_x_loaded", "sh_res_loaded", "base_stored"):
        shared_sems[name] = [sem(f"{name}{i}") for i in range(2)]
    comb_sems = {name: sem(name) for name in ("summed", "weights_found", "idx_copied", "one_ready")}
    base_sems = [sem(f"base_loaded{i}") for i in range(3)]
    out_sems = [sem(f"out_stored{i}") for i in range(3)]
    gather_sems = [[sem(f"gathered{i}{u}") for u in range(2)] for i in range(3)]

    with ExitStack() as ctx:
        wgu_s = [ctx.enter_context(nc.sbuf_tensor(f"wgu_{k}", [P, KC, NE, 2 * FE], F32R)) for k in ("hi", "lo")]
        wd_s = [ctx.enter_context(nc.sbuf_tensor(f"wd_{k}", [FE, NE, H], F32R)) for k in ("hi", "lo")]
        with ExitStack() as part:
            shared = Shared(nc, part, "a", 0, shared_sems, sgu, sd, xnt_dram, res_dram, base_dram, ident, ps)
            weights_and_shared(nc, part, sem, shared, wgu_s, wd_s, wgu, wd)
        with ExitStack() as part:
            combine = Combine(nc, part, "b", 0, comb_sems, base_sems[0:1], out_sems[0:1], gather_sems[0:1], base_dram,
                              sorted_y[0:GSORT * P], comb, slot_of, slot_top, slot_no, out)
            sorted_tiles(nc, part, sem, combine, wgu_s, wd_s, sorted_x, sorted_y, tile_expert, ident, ps)
    with ExitStack() as part:
        shared = Shared(nc, part, "c", 1, shared_sems, sgu, sd, xnt_dram, res_dram, base_dram, ident, ps)
        combine = Combine(nc, part, "c", 2, comb_sems, base_sems[1:], out_sems[1:], gather_sems[1:], base_dram, sorted_y,
                          comb, slot_of, slot_top, slot_no, out)
        shared_and_rest(nc, part, shared, combine)


class Shared:
    def __init__(self, nc, ctx, tag, times, sems, sgu, sd, xnt_dram, res_dram, base_dram, ident, ps):
        def two(name, shape, dt=F32):
            return [ctx.enter_context(nc.sbuf_tensor(f"{name}{i}_{tag}", shape, dt)) for i in range(2)]

        def weight(name, shape):
            return [ctx.enter_context(nc.sbuf_tensor(f"{name}_{k}_{tag}", shape, F32R)) for k in ("hi", "lo")]

        self.s, self.ident, self.drams, self.times = sems, ident, (sgu, sd), times
        self.sgu, self.sd = weight("sgu", [P, KC, 2 * FSH]), weight("sd", [P, SC, H])
        self.xnt_dram, self.res_dram, self.base_dram = xnt_dram, res_dram, base_dram
        self.xt = two("sh_xt", [P, 2, KC, P], F32R)
        self.res = two("sh_res", [P, H])
        self.base = two("sh_base", [P, H])
        self.hidden = two("sh_hidden", [P, FSH])
        self.act = two("sh_act", [P, FSH])
        self.at = [two(f"sh_at_{k}", [P, SC, P], F32R) for k in ("hi", "lo")]
        self.gu_ps = [ps[:, 2 + i, 0:2 * FSH] for i in range(2)]
        self.at_ps = [ps[:, 4 + i, 0:SC * P].rearrange("p (c t) -> p c t", c=SC) for i in range(2)]
        self.out_ps = [ps[:, 6 + i, 0:H] for i in range(2)]
        self.chunks = [P, FSH - P]

    def load_weights(self, sp, raws):
        for raw, dram in zip(raws, self.drams):
            sp.dma_start(raw, dram).then_inc(self.s["sh_w_loaded"], 16)

    def weights_hi(self, act, raws):
        act.wait_ge(self.s["sh_w_loaded"], 32 * self.times + 32)
        for (hi, _), raw in zip((self.sgu, self.sd), raws):
            act.activation(hi[:], raw, ACT.Copy).then_inc(self.s["sh_w_hi"], 1)

    def weights_lo(self, dve, raws):
        for j, ((hi, lo), raw) in enumerate(zip((self.sgu, self.sd), raws)):
            dve.wait_ge(self.s["sh_w_hi"], 2 * self.times + j + 1)
            dve.tensor_tensor(lo[:], raw, hi[:].bitcast(F32), ALU.subtract).then_inc(self.s["sh_w_lo"], 1)

    def load_x(self, sp, n, par, first):
        if not (isinstance(n, int) and n < first + 2):
            sp.wait_ge(self.s["sh_gu_ready"], n - 1)
        sp.dma_start(self.xt[par][:].bitcast(F32), self.xnt_dram[n]).then_inc(self.s["sh_x_loaded"][par], 16)

    def load_res(self, sp, n, par, first):
        if not (isinstance(n, int) and n < first + 2):
            sp.wait_ge(self.s["sh_added"], n - 1)
        sp.dma_start(self.res[par][:], self.res_dram[n]).then_inc(self.s["sh_res_loaded"][par], 16)

    def store(self, sp, n, par):
        sp.wait_ge(self.s["sh_added"], n + 1)
        sp.dma_start(self.base_dram[n], self.base[par][:]).then_inc(self.s["base_stored"][par], 16)

    def gate_up(self, pe, n, par, half):
        pe.wait_ge(self.s["sh_x_loaded"][par], 16 * half + 16)
        for kc in range(KC):
            mm = product3(pe, self.gu_ps[par], [self.xt[par][:, i, kc, :] for i in range(2)],
                          [w[:, kc, :] for w in self.sgu], kc == 0, kc == KC - 1)
        mm.then_inc(self.s["sh_gu_ready"], 1)

    def turn(self, pe, n, par):
        pe.wait_ge(self.s["sh_act"], n + 1)
        for c, k in enumerate(self.chunks):
            mm = pe.transpose(self.at_ps[par][0:k, c, :], self.act[par][:, c * P:c * P + k], self.ident[:])
        mm.then_inc(self.s["sh_at_ready"], 1)

    def down(self, pe, n, par, first):
        pe.wait_ge(self.s["sh_at_lo"], n + 1)
        if not (isinstance(n, int) and n < first + 2):
            pe.wait_ge(self.s["sh_added"], n - 1)
        for c, k in enumerate(self.chunks):
            mm = product3(pe, self.out_ps[par], [a[par][0:k, c, :] for a in self.at], [w[0:k, c, :] for w in self.sd],
                          c == 0, c == SC - 1)
        mm.then_inc(self.s["sh_out_ready"], 1)

    def silu(self, act, n, par):
        act.wait_ge(self.s["sh_gu_ready"], n + 1)
        act.activation(self.hidden[par][:], self.gu_ps[par][:, 0:FSH], ACT.Silu).then_inc(self.s["sh_silu"], 1)

    def turned_hi(self, act, n, par):
        act.wait_ge(self.s["sh_at_ready"], n + 1)
        for c, k in enumerate(self.chunks):
            ins = act.activation(self.at[0][par][0:k, c, :], self.at_ps[par][0:k, c, :], ACT.Copy)
        ins.then_inc(self.s["sh_at_hi"], 1)

    def times_up(self, dve, n, par):
        dve.wait_ge(self.s["sh_silu"], n + 1)
        dve.tensor_tensor(self.act[par][:], self.hidden[par][:], self.gu_ps[par][:, FSH:2 * FSH], ALU.mult)\
           .then_inc(self.s["sh_act"], 1)

    def turned_lo(self, dve, n, par):
        dve.wait_ge(self.s["sh_at_hi"], n + 1)
        for c, k in enumerate(self.chunks):
            ins = dve.tensor_tensor(self.at[1][par][0:k, c, :], self.at_ps[par][0:k, c, :],
                                    self.at[0][par][0:k, c, :].bitcast(F32), ALU.subtract)
        ins.then_inc(self.s["sh_at_lo"], 1)

    def add(self, dve, n, par, half):
        dve.wait_ge(self.s["sh_out_ready"], n + 1)
        dve.wait_ge(self.s["sh_res_loaded"][par], 16 * half + 16)
        dve.wait_ge(self.s["base_stored"][par], 16 * half + 16)
        dve.tensor_tensor(self.base[par][:], self.out_ps[par], self.res[par][:], ALU.add)\
           .then_inc(self.s["sh_added"], 1)


class Combine:
    def __init__(self, nc, ctx, tag, copies_before, sems, base_sems, out_sems, gather_sems, base_dram, sorted_y,
                 comb, slot_of, slot_top, slot_no, out):
        def sb(name, shape, dt=F32):
            return ctx.enter_context(nc.sbuf_tensor(f"{name}_{tag}", shape, dt))

        self.s, self.base_dram, self.sorted_y, self.comb = sems, base_dram, sorted_y, comb
        self.slot_of, self.slot_top, self.slot_no = slot_of, slot_top, slot_no
        self.out = out.rearrange("b (t p) h -> (b t) p h", p=P)
        self.nbuf = len(out_sems)
        self.base = [sb(f"base{i}", [P, H]) for i in range(self.nbuf)]
        self.sum = [sb(f"sum{i}", [P, H]) for i in range(self.nbuf)]
        self.base_loaded, self.out_stored, self.gathered = base_sems, out_sems, gather_sems
        self.rows = [[sb(f"rows{i}{u}", [P, HALFK, H]) for u in range(2)] for i in range(self.nbuf)]
        self.idx = [[sb(f"idx{i}{u}", [P, HALFK], I32) for u in range(2)] for i in range(self.nbuf)]
        self.one = sb("one", [P, 1])
        self.carrier = sb("carrier", [P, 2, NT])
        self.copies_before = copies_before
        self.share = sb("share", [P, TOPK])
        self.found = sb("found", [P, TOPK, NE])

    def load_base(self, sp, m, par=0):
        sp.wait_ge(self.s["summed"], TOPK * m + (TOPK + 1 - TOPK * self.nbuf))
        sp.dma_start(self.base[par][:], self.base_dram[m]).then_inc(self.base_loaded[par], 16)

    def store(self, sp, m, par=0):
        sp.wait_ge(self.s["summed"], TOPK * m + 2 * TOPK)
        sp.dma_start(self.out[m], self.sum[par][:]).then_inc(self.out_stored[par], 16)

    def gather(self, pool, m, u, par=0):
        pool.wait_ge(self.s["summed"], TOPK * m + (TOPK + HALFK * (u + 1) - TOPK * self.nbuf))
        pool.wait_ge(self.s["idx_copied"], 2 * m + u + 1 + self.copies_before)
        pool.tensor_tensor(self.carrier[:, u, bass.ds(m, 1)], self.one[:], self.one[:], ALU.mult)
        for k in range(HALFK):
            pool.indirect_dma_start(self.rows[par][u][:, k, :], None, self.sorted_y,
                                    bass.IndirectOffsetOnAxis(ap=self.idx[par][u][:, k:k + 1], axis=0))\
                .then_inc(self.gathered[par][u], 16)

    def start(self, dve, m):
        for i in range(self.nbuf):
            for u in range(2):
                self.copy_indices(dve, m + i, u, (m + i) % self.nbuf)

    def copy_indices(self, dve, m, u, par):
        dve.tensor_copy(self.idx[par][u][:], self.slot_no[:, m, HALFK * u:HALFK * (u + 1)])\
           .then_inc(self.s["idx_copied"], 1)

    def find_shares(self, dve, m, ks=range(TOPK)):
        if ks[0] == 0:
            dve.wait_ge(self.s["summed"], TOPK * m + TOPK)
        for k in ks:
            ins = dve.scalar_tensor_tensor(self.found[:, k, :], self.slot_of[:, m, :], self.slot_top[:, m, k:k + 1],
                                           self.comb[:, m, :], ALU.is_equal, ALU.mult,
                                           accum_out=self.share[:, k:k + 1])
        if ks[-1] == TOPK - 1:
            ins.then_inc(self.s["weights_found"], 1)

    def add(self, dve, m, k, before=None, par=0):
        before = m if before is None else before
        u, place = divmod(k, HALFK)
        if place == 0:
            dve.wait_ge(self.gathered[par][u], 16 * HALFK * before + 16 * HALFK)
        if k == 0:
            dve.wait_ge(self.s["weights_found"], m + 1)
            dve.wait_ge(self.base_loaded[par], 16 * before + 16)
            dve.wait_ge(self.out_stored[par], 16 * before + 16)
        last = (self.base if k == 0 else self.sum)[par]
        dve.wait_ge(self.s["summed"], TOPK * m + TOPK + k)
        dve.scalar_tensor_tensor(self.sum[par][:], self.rows[par][u][:, place, :], self.share[:, k:k + 1],
                                 last[:], ALU.mult, ALU.add).then_inc(self.s["summed"], 1)
        if place == 0 and not (isinstance(m, int) and m + self.nbuf >= NT):
            self.copy_indices(dve, m + self.nbuf, u, par)


def weights_and_shared(nc, ctx, sem, shared, wgu_s, wd_s, wgu, wd):
    def sb(name, shape, dt=F32):
        return ctx.enter_context(nc.sbuf_tensor(name, shape, dt))

    EC = NE // GT
    raw_gu = [sb(f"raw_gu{i}", [P, KC, EC, 2 * FE]) for i in range(2)]
    raw_d = [sb(f"raw_d{i}", [P, EC, H]) for i in range(2)]
    shared_raws = raw_gu[1][:].rearrange("p k e f -> p k (e f)"), raw_d[1][:]
    raw_loaded = [sem(f"raw_loaded{i}") for i in range(2)]
    w_hi, w_lo = sem("w_hi"), sem("w_lo")
    primer = sb("primer_a", [P, 2])

    def steps(eng, step):
        for n in range(4):
            step(n, n % 2, n // 2)
        with eng.Fori(2, GT // 2) as i:
            for par in range(2):
                step(2 * i + par, par, i)
        for n in range(GT, GT + 2):
            step(n, n % 2, n // 2)

    def tile(n, lag):
        return not isinstance(n, int) or 0 <= n - lag < GT

    def parts(n, par, half):
        chunk = bass.ds(EC * n, EC)
        yield raw_gu[par][:], [w[:, :, chunk, :] for w in wgu_s], wgu[:, :, chunk, :]
        yield raw_d[par][0:FE], [w[:, chunk, :] for w in wd_s], wd[:, chunk, :]

    with nc.Block() as block:
        @block.sync
        def _(sp):
            shared.load_weights(sp, shared_raws)
            shared.load_x(sp, 0, 0, 0)

            def load_raw(n, par):
                if not (isinstance(n, int) and n < 2):
                    sp.wait_ge(w_lo, 2 * n - 2)
                elif n == 1:
                    sp.wait_ge(shared.s["sh_w_lo"], 2)
                for raw, _, dram in parts(n, par, None):
                    sp.dma_start(raw, dram).then_inc(raw_loaded[par], 16)

            def step(n, par, half):
                if not isinstance(n, int) or n + 1 < GT:
                    shared.load_x(sp, n + 1, 1 - par, 0)
                    load_raw(n + 1, 1 - par)
                if tile(n, 1):
                    shared.load_res(sp, n - 1, 1 - par, 0)
                if tile(n, 3):
                    shared.store(sp, n - 3, 1 - par)

            load_raw(0, 0)
            for n in range(4):
                step(n, n % 2, n // 2)
            with sp.Fori(2, GT // 2 - 1) as i:
                for par in range(2):
                    step(2 * i + par, par, i)
            for n in range(GT - 2, GT + 3):
                step(n, n % 2, n // 2)
            for par in range(2):
                sp.wait_ge(shared.s["base_stored"][par], 16 + 16 * (GT // 2))

        @block.tensor
        def _(pe):
            pe.wait_ge(shared.s["sh_w_lo"], 2)

            def step(n, par, half):
                if tile(n, 0):
                    shared.gate_up(pe, n, par, half)
                if tile(n, 1):
                    shared.turn(pe, n - 1, 1 - par)
                if tile(n, 2):
                    shared.down(pe, n - 2, par, 0)

            steps(pe, step)

        @block.scalar
        def _(act):
            shared.weights_hi(act, shared_raws)

            def step(n, par, half):
                if tile(n, 0):
                    act.wait_ge(raw_loaded[par], 32 * half + 32)
                    for raw, (hi, _), _ in parts(n, par, half):
                        act.activation(hi, raw, ACT.Copy).then_inc(w_hi, 1)
                    shared.silu(act, n, par)
                if tile(n, 1):
                    shared.turned_hi(act, n - 1, 1 - par)

            steps(act, step)

        @block.vector
        def _(dve):
            for par in range(2):
                dve.memset(primer[:, par:par + 1], 0.0).then_inc(shared.s["base_stored"][par], 16)
            shared.weights_lo(dve, shared_raws)

            def step(n, par, half):
                if tile(n, 0):
                    for j, (raw, (hi, lo), _) in enumerate(parts(n, par, half)):
                        dve.wait_ge(w_hi, 2 * n + j + 1)
                        dve.tensor_tensor(lo, raw, hi.bitcast(F32), ALU.subtract).then_inc(w_lo, 1)
                    shared.times_up(dve, n, par)
                if tile(n, 1):
                    shared.turned_lo(dve, n - 1, 1 - par)
                if tile(n, 2):
                    shared.add(dve, n - 2, par, half - 1)

            steps(dve, step)


def sorted_tiles(nc, ctx, sem, combine, wgu_s, wd_s, sorted_x, sorted_y, tile_expert, ident, ps):
    def sb(name, shape, dt=F32):
        return ctx.enter_context(nc.sbuf_tensor(name, shape, dt))

    ITER = 32
    PAIRS = ITER // 2
    NIT = NTILE // ITER
    PER = NTILE // NT
    NC = ITER // PER
    HALFWAY = NIT // 2
    DONE = NC * (NIT - HALFWAY) - 1
    AHEAD = 4
    rows_in = [sb(f"rows_in{i}", [P, 2, H]) for i in range(AHEAD)]
    rows_out = [sb(f"rows_out{i}", [P, 2, H]) for i in range(2)]
    xt = [[sb(f"xt_e{i}{k}", [P, KC, P], F32R) for k in ("hi", "lo")] for i in range(2)]
    hidden = [sb(f"hidden{i}", [P, FE]) for i in range(2)]
    act_f = [sb(f"act_f{i}", [P, FE]) for i in range(2)]
    at = [[sb(f"at{i}{k}", [FE, P], F32R) for k in ("hi", "lo")] for i in range(2)]
    expert_row = sb("expert_row", [1, NTILE], U8)
    ALL_LAST = sum((NE - 1) << 8 * k for k in range(4))
    primer = sb("primer_b", [P, 4])

    xt_ps = [ps[:, i, 0:H] for i in range(2)]
    gu_ps = [ps[:, 2 + i, 0:2 * FE] for i in range(2)]
    at_ps = [ps[0:FE, 4 + i, 0:P] for i in range(2)]
    y_ps = [ps[:, 6 + i, 0:H] for i in range(2)]

    in_loaded = [sem(f"in_loaded{i}") for i in range(AHEAD)]
    out_stored = [sem(f"rows_stored{i}") for i in range(2)]
    expert_loaded = sem("expert_loaded")
    xt_ready, xt_hi, xt_lo = sem("ext_ready"), sem("ext_hi"), sem("ext_lo")
    gu_ready, silu_done, act_done = sem("gu_ready"), sem("silu_done"), sem("act_done")
    at_ready, at_hi, at_lo = sem("at_ready"), sem("at_hi"), sem("at_lo")
    y_ready, y_copied = sem("y_ready"), sem("y_copied")
    in_pairs = sorted_x.rearrange("(r s p) h -> r p s h", s=2, p=P)
    out_pairs = sorted_y.rearrange("(r s p) h -> r p s h", s=2, p=P)

    def iterations(eng, body):
        none = [None] * NC
        body(0, none)
        with eng.Fori(1, HALFWAY) as i:
            body(i, none)
        body(HALFWAY, [None] + list(range(NC - 1)))
        with eng.Fori(HALFWAY + 1, NIT - 1) as i:
            body(i, [NC * i + (s - NC * HALFWAY - 1) for s in range(NC)])
        body(NIT - 1, range(DONE - NC, DONE))

    def tile(i, j, lag):
        c = ITER * i + j - lag
        return None if isinstance(c, int) and not 0 <= c < NTILE else c

    with nc.Block() as block:
        @block.sync
        def _(sp):
            def load(r, at):
                if not (isinstance(r, int) and r < AHEAD):
                    sp.wait_ge(xt_ready, 2 * r + (2 - 2 * AHEAD))
                sp.dma_start(rows_in[at][:], in_pairs[r]).then_inc(in_loaded[at], 16)

            def store(r, par):
                sp.wait_ge(y_copied, 2 * r + 2)
                sp.dma_start(out_pairs[r], rows_out[par][:]).then_inc(out_stored[par], 16)

            def body(i, ms):
                for d in range(PAIRS):
                    m = ms[2 * d // PER]
                    if m is not None and 2 * d % PER == 0:
                        combine.load_base(sp, m)
                    r = PAIRS * i + d
                    if not (isinstance(i, int) and r + AHEAD - 1 >= NTILE // 2):
                        load(r + AHEAD - 1, (d + AHEAD - 1) % AHEAD)
                    if not (isinstance(i, int) and r < 2):
                        store(r - 2, d % 2)
                    if m is not None and 2 * d % PER == PER - 2:
                        combine.store(sp, m)

            sp.dma_start(expert_row[:], tile_expert.rearrange("(a g) p -> a (g p)", a=1)).then_inc(expert_loaded, 16)
            for r in range(AHEAD - 1):
                load(r, r)
            iterations(sp, body)
            for r in range(NTILE // 2 - 2, NTILE // 2):
                store(r, r % 2)
            for par in range(2):
                sp.wait_ge(out_stored[par], 16 + 16 * (NTILE // 4))
            sp.wait_ge(combine.out_stored[0], 16 + 16 * DONE)

        @block.gpsimd
        def _(pool):
            pool.memset(combine.one[:], 1.0).then_inc(combine.s["one_ready"], 1)
            pool.wait_ge(combine.s["one_ready"], 1)
            for par in range(2):
                pool.wait_ge(out_stored[par], 16 + 16 * (NTILE // 8))
            with pool.Fori(0, DONE) as m:
                for u in range(2):
                    combine.gather(pool, m, u)

        @block.tensor
        def _(pe):
            pe.wait_ge(expert_loaded, 16)

            words = expert_row[:].bitcast(I32)

            def steps(i, js):
                read = {}

                def read_experts(j):
                    first = ITER // 4 * i + j // 4
                    read[j // 4] = pe.value_load(words[0:1, bass.ds(first, 1)], min_val=0, max_val=ALL_LAST)

                def expert_of(j):
                    if j // 4 not in read:
                        read_experts(j)
                    return (read[j // 4] >> 8 * (j % 4)) & (NE - 1)

                for j in js:
                    par = j % 2
                    c = tile(i, j, 0)
                    if c is not None:
                        if par == 0:
                            pe.wait_ge(in_loaded[j // 2 % AHEAD], 16 * (PAIRS // AHEAD * i + j // (2 * AHEAD)) + 16)
                        for kc in range(KC):
                            mm = pe.transpose(xt_ps[par][:, kc * P:(kc + 1) * P],
                                              rows_in[j // 2 % AHEAD][:, par, kc * P:(kc + 1) * P], ident[:])
                        mm.then_inc(xt_ready, 1)
                    c = tile(i, j, 1)
                    if c is not None:
                        owner = expert_of(j - 1)
                        pe.wait_ge(xt_lo, c + 1)
                        for kc in range(KC):
                            mm = product3(pe, gu_ps[1 - par], [a[:, kc, :] for a in xt[1 - par]],
                                          [w[:, kc, bass.ds(owner, 1), :].rearrange("p a f -> p (a f)") for w in wgu_s],
                                          kc == 0, kc == KC - 1)
                        mm.then_inc(gu_ready, 1)
                    if j % 4 == 0 and tile(i, j, 0) is not None:
                        read_experts(j)
                    c = tile(i, j, 2)
                    if c is not None:
                        pe.wait_ge(act_done, c + 1)
                        pe.transpose(at_ps[par], act_f[par][:], ident[:]).then_inc(at_ready, 1)
                    c = tile(i, j, 3)
                    if c is not None:
                        owner = expert_of(j - 3)
                        pe.wait_ge(at_lo, c + 1)
                        if not (isinstance(c, int) and c < 2):
                            pe.wait_ge(y_copied, c - 1)
                        product3(pe, y_ps[1 - par], [a[:] for a in at[1 - par]],
                                 [w[:, bass.ds(owner, 1), :].rearrange("p a h -> p (a h)") for w in wd_s],
                                 True, True).then_inc(y_ready, 1)

            iterations(pe, lambda i, ms: steps(i, range(ITER)))
            steps(NIT, range(3))

        @block.scalar
        def _(act):
            def steps(i, js):
                for j in js:
                    par = j % 2
                    c = tile(i, j, 0)
                    if c is not None:
                        act.wait_ge(xt_ready, c + 1)
                        act.activation(xt[par][0][:].rearrange("p k t -> p (k t)"), xt_ps[par], ACT.Copy)\
                           .then_inc(xt_hi, 1)
                    c = tile(i, j, 1)
                    if c is not None:
                        act.wait_ge(gu_ready, c + 1)
                        act.activation(hidden[1 - par][:], gu_ps[1 - par][:, 0:FE], ACT.Silu).then_inc(silu_done, 1)
                    c = tile(i, j, 2)
                    if c is not None:
                        act.wait_ge(at_ready, c + 1)
                        act.activation(at[par][0][:], at_ps[par], ACT.Copy).then_inc(at_hi, 1)
                    c = tile(i, j, 3)
                    if c is not None:
                        d = (j - 3) // 2
                        act.wait_ge(y_ready, c + 1)
                        if par == 1:
                            act.wait_ge(out_stored[d % 2], 16 * (PAIRS // 2 * i + d // 2) + 16)
                        act.activation(rows_out[d % 2][:, (j - 3) % 2, :], y_ps[1 - par], ACT.Copy)\
                           .then_inc(y_copied, 1)

            iterations(act, lambda i, ms: steps(i, range(ITER)))
            steps(NIT, range(3))

        @block.vector
        def _(dve):
            for par in range(2):
                dve.memset(primer[:, par:par + 1], 0.0).then_inc(out_stored[par], 16)
            combine.start(dve, 0)
            dve.memset(primer[:, 2:3], 0.0).then_inc(combine.s["summed"], TOPK)
            dve.memset(primer[:, 3:4], 0.0).then_inc(combine.out_stored[0], 16)

            def steps(i, js, ms=[None]):
                for j in js:
                    par = j % 2
                    m = ms[j // PER]
                    c = tile(i, j, 0)
                    if c is not None:
                        dve.wait_ge(xt_hi, c + 1)
                        dve.tensor_tensor(xt[par][1][:].rearrange("p k t -> p (k t)"), xt_ps[par],
                                          xt[par][0][:].rearrange("p k t -> p (k t)").bitcast(F32), ALU.subtract)\
                           .then_inc(xt_lo, 1)
                    c = tile(i, j, 1)
                    if c is not None:
                        dve.wait_ge(silu_done, c + 1)
                        dve.tensor_tensor(act_f[1 - par][:], hidden[1 - par][:], gu_ps[1 - par][:, FE:2 * FE],
                                          ALU.mult).then_inc(act_done, 1)
                    c = tile(i, j, 2)
                    if c is not None:
                        dve.wait_ge(at_hi, c + 1)
                        dve.tensor_tensor(at[par][1][:], at_ps[par], at[par][0][:].bitcast(F32), ALU.subtract)\
                           .then_inc(at_lo, 1)
                    if m is not None:
                        if j % PER < 2:
                            combine.find_shares(dve, m, range(HALFK * (j % PER), HALFK * (j % PER + 1)))
                        else:
                            combine.add(dve, m, j % PER - 2)

            iterations(dve, lambda i, ms: steps(i, range(ITER), ms))
            steps(NIT, range(3))


def shared_and_rest(nc, ctx, shared, combine):
    DONE = GT - 1
    LAG = GT - DONE + 3
    NT2 = 2 * GT
    raws = [ctx.enter_context(nc.sbuf_tensor(name, shape, F32))[:]
            for name, shape in (("raw_sgu", [P, KC, 2 * FSH]), ("raw_sd", [P, SC, H]))]

    def steps(eng, step):
        for n in range(GT, GT + 4):
            step(n, n % 2, n // 2)
        with eng.Fori(GT // 2 + 2, GT - 1) as i:
            for par in range(2):
                step(2 * i + par, par, i)
        for n in range(NT2 - 2, NT2 + LAG):
            step(n, n % 2, n // 2)

    def tile(n, lag):
        return not isinstance(n, int) or GT <= n - lag < NT2

    def in_buffer(m, par, half=None):
        m_half = m // 2 if half is None else half - LAG // 2
        return m_half - (DONE + 1 - par) // 2

    def token_tile(n):
        return not isinstance(n, int) or n - LAG >= DONE

    with nc.Block() as block:
        @block.sync
        def _(sp):
            shared.load_weights(sp, raws)
            shared.load_x(sp, GT, 0, GT)

            def step(n, par, half):
                if token_tile(n):
                    sp.wait_ge(shared.s["base_stored"][(par - LAG) % 2], 16 * ((par - LAG) // 2 + half) + 32)
                    combine.load_base(sp, n - LAG, (par - LAG) % 2)
                    if not isinstance(n, int) or n - LAG > DONE:
                        combine.store(sp, n - (LAG + 1), (par - LAG - 1) % 2)
                if tile(n, 0):
                    if not isinstance(n, int) or n + 1 < NT2:
                        shared.load_x(sp, n + 1, 1 - par, GT)
                    shared.load_res(sp, n, par, GT)
                if tile(n, 2):
                    shared.store(sp, n - 2, par)

            steps(sp, step)
            combine.store(sp, NT2 - 1, (NT2 - 1) % 2)
            for par in range(2):
                sp.wait_ge(combine.out_stored[par], 16 + 16 * in_buffer(NT2 + par, par))
            for par in range(2):
                sp.wait_ge(shared.s["base_stored"][par], 16 + 16 * (NT2 // 2))

        @block.gpsimd
        def _(pool):
            pool.memset(combine.one[:], 1.0).then_inc(combine.s["one_ready"], 1)
            pool.wait_ge(combine.s["one_ready"], 2)
            for u in range(2):
                combine.gather(pool, DONE, u, DONE % 2)
            with pool.Fori((DONE + 1) // 2, NT2 // 2) as i:
                for par in range(2):
                    for u in range(2):
                        combine.gather(pool, 2 * i + par, u, par)

        @block.tensor
        def _(pe):
            pe.wait_ge(shared.s["sh_w_lo"], 4)

            def step(n, par, half):
                if tile(n, 0):
                    shared.gate_up(pe, n, par, half)
                if tile(n, 1):
                    shared.turn(pe, n - 1, 1 - par)
                if tile(n, 2):
                    shared.down(pe, n - 2, par, GT)

            steps(pe, step)

        @block.scalar
        def _(act):
            shared.weights_hi(act, raws)

            def step(n, par, half):
                if tile(n, 0):
                    shared.silu(act, n, par)
                if tile(n, 1):
                    shared.turned_hi(act, n - 1, 1 - par)

            steps(act, step)

        @block.vector
        def _(dve):
            combine.start(dve, DONE)
            for par in range(2):
                dve.memset(combine.found[:, par, :], 0.0).then_inc(combine.out_stored[par], 16)
            shared.weights_lo(dve, raws)

            def step(n, par, half):
                if tile(n, 0):
                    shared.times_up(dve, n, par)
                if tile(n, 1):
                    shared.turned_lo(dve, n - 1, 1 - par)
                if tile(n, 2):
                    shared.add(dve, n - 2, par, half - 1)
                if token_tile(n):
                    combine.find_shares(dve, n - LAG)
                    for k in range(TOPK):
                        combine.add(dve, n - LAG, k, in_buffer(n - LAG, (par - LAG) % 2, half), (par - LAG) % 2)

            steps(dve, step)


def kernel(**inputs):
    import numpy as np
    import concourse.bacc as bacc
    from concourse.bass_utils import run_bass_kernel_spmd

    def arr(name):
        return np.asarray(inputs["L0_" + name])

    def rows(a, n=P):
        return a.reshape(-1, n, a.shape[-1]).transpose(1, 0, 2)

    halves = np.concatenate([np.arange(0, ROPE, 2), np.arange(1, ROPE, 2)])
    wqr = arr("attn_W_dq_rope").reshape(QR, NH, ROPE)[:, :, halves]
    krope = arr("attn_W_krope")[:, halves]
    up = np.concatenate([arr("ffn_wg"), arr("ffn_wu")], axis=2).reshape(NE, KC, P, 2 * FE)
    no_later = np.tril(np.ones((NE, NE), np.float32)).reshape(1, -1)
    multiples = (np.arange(NSTEP, dtype=np.float32) * P).reshape(1, -1)

    inv_freq = (np.float32(1.0) / np.float32(10000.0) ** (np.arange(HALF, dtype=np.float32) * np.float32(2.0 / ROPE)))
    ang = np.arange(S, dtype=np.float32)[:, None] * inv_freq.astype(np.float32)[None, :]
    cos, sin = np.cos(ang), np.sin(ang)
    table = np.stack([np.concatenate([cos, cos], 1), np.concatenate([-sin, sin], 1)], 1).astype(np.float32)
    table = np.stack([table, table / np.float32(NH)]).reshape(2, TT, P, 2, ROPE).transpose(2, 0, 1, 3, 4)

    arrays = {
        "x": arr("attn_x"),
        "wc": rows(np.concatenate([arr("attn_W_cq"), arr("attn_W_ckv"), krope, arr("ffn_gate_w")], axis=1)),
        "wqr": wqr,
        "nopeT": arr("attn_W_dq_nope").reshape(QR, NH, NOPE).transpose(2, 1, 0),
        "dkT": arr("attn_W_dk_nope").reshape(KVR, NH, NOPE).transpose(2, 1, 0),
        "dvT": arr("attn_W_dv").reshape(KVR, NH, VD).transpose(2, 1, 0),
        "wo": arr("attn_W_o").reshape(NH, VD, H).transpose(1, 0, 2),
        "qscale": arr("attn_q_scale"),
        "kvscale": arr("attn_kv_scale"),
        "rope": table,
        "route_row": np.concatenate([multiples, no_later], axis=1),
        "tile_no": np.arange(P, dtype=np.float32).reshape(P, 1),
        "wgu": up.transpose(2, 1, 0, 3),
        "wd": arr("ffn_wd").transpose(1, 0, 2),
        "sgu": rows(np.concatenate([arr("ffn_sg"), arr("ffn_su")], axis=1)),
        "sd": rows(np.concatenate([arr("ffn_sd"), np.zeros((SC * P - FSH, H), np.float32)])),
    }
    nc = bacc.Bacc("TRN2", target_bir_lowering=False, num_devices=1)
    args, given = [], {}
    for name, a in arrays.items():
        a = np.ascontiguousarray(a)
        given[f"in_{name}"] = a
        args.append(nc.dram_tensor(f"in_{name}", a.shape, mybir.dt.from_np(a.dtype), kind="ExternalInput").ap())
    args.append(nc.dram_tensor("out", (B, S, H), F32, kind="ExternalOutput").ap())
    build(nc, *args)
    r = run_bass_kernel_spmd(nc, [given], core_ids=[0])
    return r.results[0]["out"]
```
